# Optimizing a Trainium2 kernel written in Bass

```python
import numpy as np
import jax
import jax.numpy as jnp

def _softmax(x, axis=-1):
    return jax.nn.softmax(x, axis=axis)

def _gelu(x):
    return jax.nn.gelu(x, approximate=True)

def _silu(x):
    return jax.nn.silu(x)

def _sigmoid(x):
    return jax.nn.sigmoid(x)

def _layernorm(x, axis=-1, eps=1e-05):
    m = jnp.mean(x, axis=axis, keepdims=True)
    v = jnp.var(x, axis=axis, keepdims=True)
    return (x - m) / jnp.sqrt(v + eps)

def _scatter_add(tgt, idx, src, axis=0):
    return tgt.at[idx].add(src)

def _segment_sum(src, seg, n):
    return jax.ops.segment_sum(src, seg, n)
kernel_name = 'mk_gps_d4_gnn_r16_3df359'

def setup_inputs(seed: int=0):
    np.random.seed(seed)
    _w = jnp.asarray

    def _rec_inputs():
        import jax
        import jax.numpy as jnp
        _gk = jax.random.key(seed)
        x = -0.0001538 + 1 * jax.random.normal(jax.random.fold_in(_gk, 1), (512, 768), jnp.float32)
        src = jax.random.randint(jax.random.fold_in(_gk, 2), (16384,), 0, 512, jnp.int32)
        dst = jax.random.randint(jax.random.fold_in(_gk, 3), (16384,), 0, 512, jnp.int32)
        _o = jnp.argsort(dst, stable=True)
        src = src[_o]
        dst = dst[_o]
        return (x, src, dst)
    x, src, dst = _rec_inputs()

    def _L0_gnn_setup():
        import jax, jax.numpy as jnp
        import numpy as np
        NEG_SLOPE = 0.2
        EPS = 1e-16
        N_NODES = 512
        N_EDGES = 4096
        D_IN = 768
        D_HID = 768
        H1 = 8
        H2 = 1

        def gat_layer(x, W, a_s, a_d, b, edge_index, concat):
            n = x.shape[0]
            H, C = a_s.shape
            h = (x @ W).reshape(n, H, C)
            src, dst = (edge_index[0], edge_index[1])
            alpha_s = jnp.einsum('nhc,hc->nh', h, a_s)
            alpha_d = jnp.einsum('nhc,hc->nh', h, a_d)
            e = jax.nn.leaky_relu(alpha_s[src] + alpha_d[dst], NEG_SLOPE)
            m = jax.ops.segment_max(e, dst, num_segments=n)
            e = jnp.exp(e - m[dst])
            denom = jax.ops.segment_sum(e, dst, num_segments=n)
            alpha = e / (denom[dst] + EPS)
            msg = h[src] * alpha[:, :, None]
            out = jax.ops.segment_sum(msg, dst, num_segments=n)
            out = out.reshape(n, H * C) if concat else out.mean(axis=1)
            return out + b
        key = jax.random.key(seed)
        ks = jax.random.split(key, 10)
        x = jax.random.normal(ks[0], (N_NODES, D_IN), dtype=jnp.float32)
        edge_list = jax.random.randint(ks[1], (2, N_EDGES), 0, N_NODES, dtype=jnp.int32)
        s = 0.05
        W1 = jax.random.normal(ks[2], (D_IN, H1 * D_HID), dtype=jnp.float32) * s
        a_src1 = jax.random.normal(ks[3], (H1, D_HID), dtype=jnp.float32) * s
        a_dst1 = jax.random.normal(ks[4], (H1, D_HID), dtype=jnp.float32) * s
        b1 = jnp.zeros((H1 * D_HID,), dtype=jnp.float32)
        W2 = jax.random.normal(ks[5], (H1 * D_HID, H2 * D_HID), dtype=jnp.float32) * s
        a_src2 = jax.random.normal(ks[6], (H2, D_HID), dtype=jnp.float32) * s
        a_dst2 = jax.random.normal(ks[7], (H2, D_HID), dtype=jnp.float32) * s
        b2 = jnp.zeros((H2 * D_HID,), dtype=jnp.float32)
        return {'x': x, 'W1': W1, 'a_src1': a_src1, 'a_dst1': a_dst1, 'b1': b1, 'W2': W2, 'a_src2': a_src2, 'a_dst2': a_dst2, 'b2': b2, 'edge_list': edge_list}
    _L0_gnn_all = _L0_gnn_setup()
    _L0_gnn_in = {k: v for k, v in _L0_gnn_all.items() if k in ('W1', 'a_src1', 'a_dst1', 'b1', 'W2', 'a_src2', 'a_dst2', 'b2')}
    del _L0_gnn_all

    def _L0_mix_setup():
        import jax, jax.numpy as jnp
        import numpy as np
        DIM = 768
        HEADS = 12
        HEAD_DIM = DIM // HEADS
        M = int(DIM * 0.5)
        HIDDEN = int(DIM * 4.0)
        SCALE = HEAD_DIM ** (-0.25)
        EPSILON = 1e-08
        LN_EPS = 1e-05

        def _orf(key):

            def one(k):
                a = jax.random.normal(k, (M, HEAD_DIM))
                q, _ = jnp.linalg.qr(a)
                return q.T
            ks = jax.random.split(key, HEADS)
            return jax.vmap(one)(ks) * np.sqrt(M)

        def _layernorm(x, g, b):
            mu = jnp.mean(x, axis=-1, keepdims=True)
            var = jnp.mean(jnp.square(x - mu), axis=-1, keepdims=True)
            return (x - mu) * jax.lax.rsqrt(var + LN_EPS) * g + b

        def _feature_map(x, w):
            xs = x * SCALE
            proj = jnp.einsum('bhnc,hcm->bhnm', xs, w)
            sq = 0.5 * jnp.sum(xs * xs, axis=-1, keepdims=True)
            return jnp.exp(proj - sq) / np.sqrt(M)

        def _performer_attn(x, qkv_w, qkv_b, w_orf, proj_w, proj_b):
            B, N, _ = x.shape
            qkv = x @ qkv_w + qkv_b
            qkv = qkv.reshape(B, N, 3, HEADS, HEAD_DIM)
            qkv = jnp.transpose(qkv, (2, 0, 3, 1, 4))
            q = _feature_map(qkv[0], w_orf)
            k = _feature_map(qkv[1], w_orf)
            v = qkv[2]
            k_sum = jnp.sum(k, axis=2)
            D = jnp.einsum('bhnm,bhm->bhn', q, k_sum)[..., None] + EPSILON
            ktv = jnp.einsum('bhnm,bhnc->bhmc', k, v)
            out = jnp.einsum('bhnm,bhmc->bhnc', q, ktv) / D
            out = jnp.transpose(out, (0, 2, 1, 3)).reshape(B, N, DIM)
            return out @ proj_w + proj_b
        key = jax.random.key(seed)
        ks = jax.random.split(key, 8)
        s = 0.02
        return {'x': jax.random.normal(ks[0], (32, 1024, DIM), jnp.float32), 'ln1_g': jnp.ones((DIM,), jnp.float32), 'ln1_b': jnp.zeros((DIM,), jnp.float32), 'qkv_w': jax.random.normal(ks[1], (DIM, 3 * DIM), jnp.float32) * s, 'qkv_b': jnp.zeros((3 * DIM,), jnp.float32), 'w_orf': _orf(ks[2]).astype(jnp.float32), 'proj_w': jax.random.normal(ks[3], (DIM, DIM), jnp.float32) * s, 'proj_b': jnp.zeros((DIM,), jnp.float32), 'ln2_g': jnp.ones((DIM,), jnp.float32), 'ln2_b': jnp.zeros((DIM,), jnp.float32), 'fc1_w': jax.random.normal(ks[4], (DIM, HIDDEN), jnp.float32) * s, 'fc1_b': jnp.zeros((HIDDEN,), jnp.float32), 'fc2_w': jax.random.normal(ks[5], (HIDDEN, DIM), jnp.float32) * s, 'fc2_b': jnp.zeros((DIM,), jnp.float32)}
    _L0_mix_all = _L0_mix_setup()
    _L0_mix_in = {k: v for k, v in _L0_mix_all.items() if k in ('ln1_g', 'ln1_b', 'qkv_w', 'qkv_b', 'w_orf', 'proj_w', 'proj_b', 'ln2_g', 'ln2_b', 'fc1_w', 'fc1_b', 'fc2_w', 'fc2_b')}
    del _L0_mix_all

    def _L0_ffn_setup():
        import jax, jax.numpy as jnp
        import numpy as np
        D = 768
        I = 192
        E = 8
        K = 2
        LIMIT = 10.0
        VOCAB = 2048

        def _expert(xf, W1, W2, W3):
            gate = jnp.minimum(xf @ W1, LIMIT)
            up = jnp.clip(xf @ W3, -LIMIT, LIMIT)
            return jax.nn.silu(gate) * up @ W2
        key = jax.random.key(seed)
        ks = jax.random.split(key, 10)
        s = 0.02
        return {'x': jax.random.normal(ks[0], (1, 128, D), dtype=jnp.float32), 'input_ids': jax.random.randint(ks[1], (1, 128), 0, VOCAB, dtype=jnp.int64), 'gate_w': jax.random.normal(ks[2], (D, E), dtype=jnp.float32) * s, 'gate_bias': jnp.zeros((E,), dtype=jnp.float32), 'w1': jax.random.normal(ks[3], (E, D, I), dtype=jnp.float32) * s, 'w2': jax.random.normal(ks[4], (E, I, D), dtype=jnp.float32) * s, 'w3': jax.random.normal(ks[5], (E, D, I), dtype=jnp.float32) * s, 'w1s': jax.random.normal(ks[6], (D, I), dtype=jnp.float32) * s, 'w2s': jax.random.normal(ks[7], (I, D), dtype=jnp.float32) * s, 'w3s': jax.random.normal(ks[8], (D, I), dtype=jnp.float32) * s}
    _L0_ffn_all = _L0_ffn_setup()
    _L0_ffn_in = {k: v for k, v in _L0_ffn_all.items() if k in ('input_ids', 'gate_w', 'gate_bias', 'w1', 'w2', 'w3', 'w1s', 'w2s', 'w3s')}
    del _L0_ffn_all

    def _L1_gnn_setup():
        import jax, jax.numpy as jnp
        import numpy as np
        N = 1250
        E_RAND = 20000
        NEG_SLOPE = 0.2

        def gat_layer(x, W, a_src, a_dst, bias, src, dst, heads, out_c, concat):
            n = x.shape[0]
            h = (x @ W).reshape(n, heads, out_c)
            al_s = jnp.einsum('nhc,hc->nh', h, a_src)
            al_d = jnp.einsum('nhc,hc->nh', h, a_dst)
            e = jax.nn.leaky_relu(al_s[src] + al_d[dst], NEG_SLOPE)
            m = jax.ops.segment_max(e, dst, num_segments=n)
            ex = jnp.exp(e - m[dst])
            z = jax.ops.segment_sum(ex, dst, num_segments=n)
            alpha = ex / (z[dst] + 1e-16)
            msg = h[src] * alpha[:, :, None]
            out = jax.ops.segment_sum(msg, dst, num_segments=n)
            out = out.reshape(n, heads * out_c) if concat else out.mean(axis=1)
            return out + bias
        key = jax.random.key(seed)
        ks = jax.random.split(key, 10)
        x = jax.random.normal(ks[0], (N, 768), dtype=jnp.float32)
        src = jax.random.randint(ks[1], (E_RAND,), 0, N)
        dst = jax.random.randint(ks[2], (E_RAND,), 0, N)
        loop = jnp.arange(N)
        edge_index = jnp.stack([jnp.concatenate([src, loop]), jnp.concatenate([dst, loop])])
        s = 1.0 / np.sqrt(768.0)
        W1 = jax.random.normal(ks[3], (768, 768), dtype=jnp.float32) * s
        a_src1 = jax.random.normal(ks[4], (8, 96), dtype=jnp.float32) * 0.1
        a_dst1 = jax.random.normal(ks[5], (8, 96), dtype=jnp.float32) * 0.1
        b1 = jnp.zeros((768,), dtype=jnp.float32)
        W2 = jax.random.normal(ks[6], (768, 768), dtype=jnp.float32) * s
        a_src2 = jax.random.normal(ks[7], (1, 768), dtype=jnp.float32) * 0.1
        a_dst2 = jax.random.normal(ks[8], (1, 768), dtype=jnp.float32) * 0.1
        b2 = jnp.zeros((768,), dtype=jnp.float32)
        return {'x': x, 'edge_index': edge_index, 'W1': W1, 'a_src1': a_src1, 'a_dst1': a_dst1, 'b1': b1, 'W2': W2, 'a_src2': a_src2, 'a_dst2': a_dst2, 'b2': b2}
    _L1_gnn_all = _L1_gnn_setup()
    _L1_gnn_in = {k: v for k, v in _L1_gnn_all.items() if k in ('W1', 'a_src1', 'a_dst1', 'b1', 'W2', 'a_src2', 'a_dst2', 'b2')}
    del _L1_gnn_all

    def _L1_mix_setup():
        import jax, jax.numpy as jnp
        import numpy as np
        DIM = 768
        HEADS = 12
        HEAD_DIM = DIM // HEADS
        EPS = 1e-06
        LN_EPS = 1e-05

        def _elu1(t):
            return jax.nn.elu(t) + 1.0
        key = jax.random.key(seed)
        k1, k2, k3, k4 = jax.random.split(key, 4)
        x = jax.random.normal(k1, (8, 256, DIM), dtype=jnp.float32)
        ln_gamma = jnp.ones((DIM,), dtype=jnp.float32)
        ln_beta = jnp.zeros((DIM,), dtype=jnp.float32)
        w_qkv = jax.random.normal(k2, (3 * DIM, DIM), dtype=jnp.float32) * (1.0 / np.sqrt(DIM))
        w_proj = jax.random.normal(k3, (DIM, DIM), dtype=jnp.float32) * (1.0 / np.sqrt(DIM))
        b_proj = jax.random.normal(k4, (DIM,), dtype=jnp.float32) * 0.01
        return {'x': x, 'ln_gamma': ln_gamma, 'ln_beta': ln_beta, 'w_qkv': w_qkv, 'w_proj': w_proj, 'b_proj': b_proj}
    _L1_mix_all = _L1_mix_setup()
    _L1_mix_in = {k: v for k, v in _L1_mix_all.items() if k in ('ln_gamma', 'ln_beta', 'w_qkv', 'w_proj', 'b_proj')}
    del _L1_mix_all

    def _L1_ffn_setup():
        import jax, jax.numpy as jnp
        import numpy as np
        ATOM = {'vm': 0, 'im': 1, 'cm': 2, 'sc': 3, 'cc': 4}
        TASK_PAIRS = [('vm', 'sc'), ('vm', 'cc'), ('im', 'sc'), ('im', 'cc'), ('cm', 'sc'), ('cm', 'cc')]
        SRC_IDX = np.array([[ATOM[l], ATOM[r]] for l, r in TASK_PAIRS], dtype=np.int32)
        DST_IDX = np.array([[ATOM[r], ATOM[l]] for l, r in TASK_PAIRS], dtype=np.int32)
        NCLS = 6
        NATOMS = 5

        def _l2norm(x, eps=1e-12):
            return x / jnp.clip(jnp.linalg.norm(x, axis=-1, keepdims=True), eps)
        key = jax.random.key(seed)
        ks = jax.random.split(key, 12)
        B, NPATCH, D, H = (64, 197, 768, 192)
        std = 0.02
        x = jax.random.normal(ks[0], (B, NCLS + NPATCH, D), dtype=jnp.float32)
        fc1_w = jax.random.normal(ks[1], (H, D), dtype=jnp.float32) * std
        fc1_b = jnp.zeros((H,), jnp.float32)
        fc2_w = jax.random.normal(ks[2], (D, H), dtype=jnp.float32) * std
        fc2_b = jnp.zeros((D,), jnp.float32)
        gate_pair = jax.random.normal(ks[3], (NCLS, 2, D), dtype=jnp.float32) * std
        atom_in_w = jax.random.normal(ks[4], (NATOMS, H, D), dtype=jnp.float32) * std
        atom_in_b = jax.random.normal(ks[5], (NATOMS, H), dtype=jnp.float32) * std
        atom_out_w = jax.random.normal(ks[6], (NATOMS, D, H), dtype=jnp.float32) * std
        atom_out_b = jax.random.normal(ks[7], (NATOMS, D), dtype=jnp.float32) * std
        balance_bias = jnp.zeros((NCLS, 2), jnp.float32)
        return {'x': x, 'fc1_w': fc1_w, 'fc1_b': fc1_b, 'fc2_w': fc2_w, 'fc2_b': fc2_b, 'gate_pair': gate_pair, 'atom_in_w': atom_in_w, 'atom_in_b': atom_in_b, 'atom_out_w': atom_out_w, 'atom_out_b': atom_out_b, 'balance_bias': balance_bias}
    _L1_ffn_all = _L1_ffn_setup()
    _L1_ffn_in = {k: v for k, v in _L1_ffn_all.items() if k in ('fc1_w', 'fc1_b', 'fc2_w', 'fc2_b', 'gate_pair', 'atom_in_w', 'atom_in_b', 'atom_out_w', 'atom_out_b', 'balance_bias')}
    del _L1_ffn_all

    def _L2_gnn_setup():
        import jax, jax.numpy as jnp
        import numpy as np
        N_NODES = 625
        N_EDGES = 6250
        DIM = 768
        key = jax.random.key(seed)
        k1, k2, k3, k4 = jax.random.split(key, 4)
        x = jax.random.normal(k1, (N_NODES, DIM), dtype=jnp.float32)
        edge_index = jax.random.randint(k2, (2, N_EDGES), 0, N_NODES, dtype=jnp.int32)
        W = jax.random.normal(k3, (DIM, DIM), dtype=jnp.float32) / np.sqrt(DIM)
        b = jnp.zeros((DIM,), dtype=jnp.float32)
        return {'x': x, 'edge_index': edge_index, 'W': W, 'b': b}
    _L2_gnn_all = _L2_gnn_setup()
    _L2_gnn_in = {k: v for k, v in _L2_gnn_all.items() if k in ('W', 'b')}
    del _L2_gnn_all

    def _L2_mix_setup():
        import jax, jax.numpy as jnp
        import numpy as np
        FEATS = 768
        HEAD = 12

        def _phi(t):
            return jax.nn.elu(t) + 1.0
        key = jax.random.key(seed)
        ks = jax.random.split(key, 9)
        f = FEATS
        s = 1.0 / np.sqrt(f)
        x = jax.random.normal(ks[0], (4, 256, f), dtype=jnp.float32)
        Wq = jax.random.normal(ks[1], (f, f), dtype=jnp.float32) * s
        bq = jax.random.normal(ks[2], (f,), dtype=jnp.float32) * 0.01
        Wk = jax.random.normal(ks[3], (f, f), dtype=jnp.float32) * s
        bk = jax.random.normal(ks[4], (f,), dtype=jnp.float32) * 0.01
        Wv = jax.random.normal(ks[5], (f, f), dtype=jnp.float32) * s
        bv = jax.random.normal(ks[6], (f,), dtype=jnp.float32) * 0.01
        Wo = jax.random.normal(ks[7], (f, f), dtype=jnp.float32) * s
        bo = jax.random.normal(ks[8], (f,), dtype=jnp.float32) * 0.01
        return {'x': x, 'Wq': Wq, 'bq': bq, 'Wk': Wk, 'bk': bk, 'Wv': Wv, 'bv': bv, 'Wo': Wo, 'bo': bo}
    _L2_mix_all = _L2_mix_setup()
    _L2_mix_in = {k: v for k, v in _L2_mix_all.items() if k in ('Wq', 'bq', 'Wk', 'bk', 'Wv', 'bv', 'Wo', 'bo')}
    del _L2_mix_all

    def _L2_ffn_setup():
        import jax, jax.numpy as jnp
        import numpy as np
        B, S, H, I = (4, 128, 768, 1536)
        E, K = (3, 2)
        INIT = 0.02

        def _expert(x, gw, uw, dw):
            return jax.nn.silu(x @ gw) * (x @ uw) @ dw
        key = jax.random.key(seed)
        ks = jax.random.split(key, 8)
        f32 = jnp.float32
        return {'x': jax.random.normal(ks[0], (B, S, H), f32), 'shared_gate': jax.random.normal(ks[1], (H, I), f32) * INIT, 'shared_up': jax.random.normal(ks[2], (H, I), f32) * INIT, 'shared_down': jax.random.normal(ks[3], (I, H), f32) * INIT, 'routed_gate': jax.random.normal(ks[4], (E, H, I), f32) * INIT, 'routed_up': jax.random.normal(ks[5], (E, H, I), f32) * INIT, 'routed_down': jax.random.normal(ks[6], (E, I, H), f32) * INIT, 'router_w': jax.random.normal(ks[7], (H, E), f32) * INIT, 'routing_bias': jnp.zeros((E,), f32)}
    _L2_ffn_all = _L2_ffn_setup()
    _L2_ffn_in = {k: v for k, v in _L2_ffn_all.items() if k in ('shared_gate', 'shared_up', 'shared_down', 'routed_gate', 'routed_up', 'routed_down', 'router_w', 'routing_bias')}
    del _L2_ffn_all

    def _L3_gnn_setup():
        import jax, jax.numpy as jnp
        import numpy as np
        N_NODES = 625
        key = jax.random.key(seed)
        k1, k2, k3 = jax.random.split(key, 3)
        x = jax.random.normal(k1, (N_NODES, 768), dtype=jnp.float32)
        edge_index = jax.random.randint(k2, (2, 6250), 0, N_NODES, dtype=jnp.int32)
        W = jax.random.normal(k3, (768, 768), dtype=jnp.float32) * (1.0 / np.sqrt(768))
        b = jnp.zeros((768,), dtype=jnp.float32)
        return {'x': x, 'edge_index': edge_index, 'W': W, 'b': b}
    _L3_gnn_all = _L3_gnn_setup()
    _L3_gnn_in = {k: v for k, v in _L3_gnn_all.items() if k in ('W', 'b')}
    del _L3_gnn_all

    def _L3_mix_setup():
        import jax, jax.numpy as jnp
        import numpy as np
        DIM = 768
        NUM_HEADS = 12
        HEAD_DIM = DIM // NUM_HEADS
        HIDDEN = int(DIM * 4.0)
        EPS = 1e-08

        def layer_norm(x, w, b):
            mu = jnp.mean(x, axis=-1, keepdims=True)
            var = jnp.mean(jnp.square(x - mu), axis=-1, keepdims=True)
            return (x - mu) * jax.lax.rsqrt(var + EPS) * w + b

        def linear_attention(x, qkv_w, qkv_b, proj_w, proj_b):
            B, N, C = x.shape
            qkv = (x @ qkv_w + qkv_b).reshape(B, N, 3, NUM_HEADS, HEAD_DIM)
            qkv = qkv.transpose(2, 0, 3, 1, 4)
            q, k, v = (qkv[0], qkv[1], qkv[2])
            q = jax.nn.elu(q) + 1.0
            k = jax.nn.elu(k) + 1.0
            kv = jnp.einsum('bhsd,bhse->bhde', k, v)
            z = 1.0 / jnp.einsum('bhsd,bhd->bhs', q, k.sum(axis=-2))
            out = jnp.einsum('bhde,bhsd,bhs->bhse', kv, q, z)
            out = out.transpose(0, 2, 1, 3).reshape(B, N, C)
            return out @ proj_w + proj_b
        key = jax.random.key(seed)
        ks = jax.random.split(key, 10)
        s = 0.02
        return {'x': jax.random.normal(ks[0], (16, 256, DIM), dtype=jnp.float32), 'qkv_w': jax.random.normal(ks[1], (DIM, 3 * DIM), dtype=jnp.float32) * s, 'qkv_b': jnp.zeros((3 * DIM,), dtype=jnp.float32), 'proj_w': jax.random.normal(ks[2], (DIM, DIM), dtype=jnp.float32) * s, 'proj_b': jnp.zeros((DIM,), dtype=jnp.float32), 'fc1_w': jax.random.normal(ks[3], (DIM, HIDDEN), dtype=jnp.float32) * s, 'fc1_b': jnp.zeros((HIDDEN,), dtype=jnp.float32), 'fc2_w': jax.random.normal(ks[4], (HIDDEN, DIM), dtype=jnp.float32) * s, 'fc2_b': jnp.zeros((DIM,), dtype=jnp.float32), 'ln1_w': jnp.ones((DIM,), dtype=jnp.float32), 'ln1_b': jnp.zeros((DIM,), dtype=jnp.float32), 'ln2_w': jnp.ones((DIM,), dtype=jnp.float32), 'ln2_b': jnp.zeros((DIM,), dtype=jnp.float32)}
    _L3_mix_all = _L3_mix_setup()
    _L3_mix_in = {k: v for k, v in _L3_mix_all.items() if k in ('qkv_w', 'qkv_b', 'proj_w', 'proj_b', 'fc1_w', 'fc1_b', 'fc2_w', 'fc2_b', 'ln1_w', 'ln1_b', 'ln2_w', 'ln2_b')}
    del _L3_mix_all

    def _L3_ffn_setup():
        import jax, jax.numpy as jnp
        import numpy as np
        import math
        SQRT_2_OVER_PI = math.sqrt(2.0 / math.pi)

        def gelu(x):
            return x * 0.5 * (1.0 + jnp.tanh(SQRT_2_OVER_PI * (x + 0.044715 * x * x * x)))
        key = jax.random.key(seed)
        ks = jax.random.split(key, 6)
        B, S, D, M, E = (8, 512, 768, 192, 8)
        return {'x': jax.random.normal(ks[0], (B, S, D), dtype=jnp.float32), 'router_w': jax.random.normal(ks[1], (D, E), dtype=jnp.float32) * (1.0 / np.sqrt(D)), 'w1': jax.random.normal(ks[2], (E, D, M), dtype=jnp.float32) * (1.0 / np.sqrt(D)), 'b1': jax.random.normal(ks[3], (E, M), dtype=jnp.float32) * 1e-06, 'w2': jax.random.normal(ks[4], (E, M, D), dtype=jnp.float32) * (1.0 / np.sqrt(M)), 'b2': jax.random.normal(ks[5], (E, D), dtype=jnp.float32) * 1e-06}
    _L3_ffn_all = _L3_ffn_setup()
    _L3_ffn_in = {k: v for k, v in _L3_ffn_all.items() if k in ('router_w', 'w1', 'b1', 'w2', 'b2')}
    del _L3_ffn_all
    return {'x': x, 'src': src, 'dst': dst, 'L0_gnn_W1': _L0_gnn_in['W1'], 'L0_gnn_a_src1': _L0_gnn_in['a_src1'], 'L0_gnn_a_dst1': _L0_gnn_in['a_dst1'], 'L0_gnn_b1': _L0_gnn_in['b1'], 'L0_gnn_W2': _L0_gnn_in['W2'], 'L0_gnn_a_src2': _L0_gnn_in['a_src2'], 'L0_gnn_a_dst2': _L0_gnn_in['a_dst2'], 'L0_gnn_b2': _L0_gnn_in['b2'], 'L0_mix_ln1_g': _L0_mix_in['ln1_g'], 'L0_mix_ln1_b': _L0_mix_in['ln1_b'], 'L0_mix_qkv_w': _L0_mix_in['qkv_w'], 'L0_mix_qkv_b': _L0_mix_in['qkv_b'], 'L0_mix_w_orf': _L0_mix_in['w_orf'], 'L0_mix_proj_w': _L0_mix_in['proj_w'], 'L0_mix_proj_b': _L0_mix_in['proj_b'], 'L0_mix_ln2_g': _L0_mix_in['ln2_g'], 'L0_mix_ln2_b': _L0_mix_in['ln2_b'], 'L0_mix_fc1_w': _L0_mix_in['fc1_w'], 'L0_mix_fc1_b': _L0_mix_in['fc1_b'], 'L0_mix_fc2_w': _L0_mix_in['fc2_w'], 'L0_mix_fc2_b': _L0_mix_in['fc2_b'], 'L0_ffn_input_ids': _L0_ffn_in['input_ids'], 'L0_ffn_gate_w': _L0_ffn_in['gate_w'], 'L0_ffn_gate_bias': _L0_ffn_in['gate_bias'], 'L0_ffn_w1': _L0_ffn_in['w1'], 'L0_ffn_w2': _L0_ffn_in['w2'], 'L0_ffn_w3': _L0_ffn_in['w3'], 'L0_ffn_w1s': _L0_ffn_in['w1s'], 'L0_ffn_w2s': _L0_ffn_in['w2s'], 'L0_ffn_w3s': _L0_ffn_in['w3s'], 'L1_gnn_W1': _L1_gnn_in['W1'], 'L1_gnn_a_src1': _L1_gnn_in['a_src1'], 'L1_gnn_a_dst1': _L1_gnn_in['a_dst1'], 'L1_gnn_b1': _L1_gnn_in['b1'], 'L1_gnn_W2': _L1_gnn_in['W2'], 'L1_gnn_a_src2': _L1_gnn_in['a_src2'], 'L1_gnn_a_dst2': _L1_gnn_in['a_dst2'], 'L1_gnn_b2': _L1_gnn_in['b2'], 'L1_mix_ln_gamma': _L1_mix_in['ln_gamma'], 'L1_mix_ln_beta': _L1_mix_in['ln_beta'], 'L1_mix_w_qkv': _L1_mix_in['w_qkv'], 'L1_mix_w_proj': _L1_mix_in['w_proj'], 'L1_mix_b_proj': _L1_mix_in['b_proj'], 'L1_ffn_fc1_w': _L1_ffn_in['fc1_w'], 'L1_ffn_fc1_b': _L1_ffn_in['fc1_b'], 'L1_ffn_fc2_w': _L1_ffn_in['fc2_w'], 'L1_ffn_fc2_b': _L1_ffn_in['fc2_b'], 'L1_ffn_gate_pair': _L1_ffn_in['gate_pair'], 'L1_ffn_atom_in_w': _L1_ffn_in['atom_in_w'], 'L1_ffn_atom_in_b': _L1_ffn_in['atom_in_b'], 'L1_ffn_atom_out_w': _L1_ffn_in['atom_out_w'], 'L1_ffn_atom_out_b': _L1_ffn_in['atom_out_b'], 'L1_ffn_balance_bias': _L1_ffn_in['balance_bias'], 'L2_gnn_W': _L2_gnn_in['W'], 'L2_gnn_b': _L2_gnn_in['b'], 'L2_mix_Wq': _L2_mix_in['Wq'], 'L2_mix_bq': _L2_mix_in['bq'], 'L2_mix_Wk': _L2_mix_in['Wk'], 'L2_mix_bk': _L2_mix_in['bk'], 'L2_mix_Wv': _L2_mix_in['Wv'], 'L2_mix_bv': _L2_mix_in['bv'], 'L2_mix_Wo': _L2_mix_in['Wo'], 'L2_mix_bo': _L2_mix_in['bo'], 'L2_ffn_shared_gate': _L2_ffn_in['shared_gate'], 'L2_ffn_shared_up': _L2_ffn_in['shared_up'], 'L2_ffn_shared_down': _L2_ffn_in['shared_down'], 'L2_ffn_routed_gate': _L2_ffn_in['routed_gate'], 'L2_ffn_routed_up': _L2_ffn_in['routed_up'], 'L2_ffn_routed_down': _L2_ffn_in['routed_down'], 'L2_ffn_router_w': _L2_ffn_in['router_w'], 'L2_ffn_routing_bias': _L2_ffn_in['routing_bias'], 'L3_gnn_W': _L3_gnn_in['W'], 'L3_gnn_b': _L3_gnn_in['b'], 'L3_mix_qkv_w': _L3_mix_in['qkv_w'], 'L3_mix_qkv_b': _L3_mix_in['qkv_b'], 'L3_mix_proj_w': _L3_mix_in['proj_w'], 'L3_mix_proj_b': _L3_mix_in['proj_b'], 'L3_mix_fc1_w': _L3_mix_in['fc1_w'], 'L3_mix_fc1_b': _L3_mix_in['fc1_b'], 'L3_mix_fc2_w': _L3_mix_in['fc2_w'], 'L3_mix_fc2_b': _L3_mix_in['fc2_b'], 'L3_mix_ln1_w': _L3_mix_in['ln1_w'], 'L3_mix_ln1_b': _L3_mix_in['ln1_b'], 'L3_mix_ln2_w': _L3_mix_in['ln2_w'], 'L3_mix_ln2_b': _L3_mix_in['ln2_b'], 'L3_ffn_router_w': _L3_ffn_in['router_w'], 'L3_ffn_w1': _L3_ffn_in['w1'], 'L3_ffn_b1': _L3_ffn_in['b1'], 'L3_ffn_w2': _L3_ffn_in['w2'], 'L3_ffn_b2': _L3_ffn_in['b2']}

def reference(x, src, dst, L0_gnn_W1, L0_gnn_a_src1, L0_gnn_a_dst1, L0_gnn_b1, L0_gnn_W2, L0_gnn_a_src2, L0_gnn_a_dst2, L0_gnn_b2, L0_mix_ln1_g, L0_mix_ln1_b, L0_mix_qkv_w, L0_mix_qkv_b, L0_mix_w_orf, L0_mix_proj_w, L0_mix_proj_b, L0_mix_ln2_g, L0_mix_ln2_b, L0_mix_fc1_w, L0_mix_fc1_b, L0_mix_fc2_w, L0_mix_fc2_b, L0_ffn_input_ids, L0_ffn_gate_w, L0_ffn_gate_bias, L0_ffn_w1, L0_ffn_w2, L0_ffn_w3, L0_ffn_w1s, L0_ffn_w2s, L0_ffn_w3s, L1_gnn_W1, L1_gnn_a_src1, L1_gnn_a_dst1, L1_gnn_b1, L1_gnn_W2, L1_gnn_a_src2, L1_gnn_a_dst2, L1_gnn_b2, L1_mix_ln_gamma, L1_mix_ln_beta, L1_mix_w_qkv, L1_mix_w_proj, L1_mix_b_proj, L1_ffn_fc1_w, L1_ffn_fc1_b, L1_ffn_fc2_w, L1_ffn_fc2_b, L1_ffn_gate_pair, L1_ffn_atom_in_w, L1_ffn_atom_in_b, L1_ffn_atom_out_w, L1_ffn_atom_out_b, L1_ffn_balance_bias, L2_gnn_W, L2_gnn_b, L2_mix_Wq, L2_mix_bq, L2_mix_Wk, L2_mix_bk, L2_mix_Wv, L2_mix_bv, L2_mix_Wo, L2_mix_bo, L2_ffn_shared_gate, L2_ffn_shared_up, L2_ffn_shared_down, L2_ffn_routed_gate, L2_ffn_routed_up, L2_ffn_routed_down, L2_ffn_router_w, L2_ffn_routing_bias, L3_gnn_W, L3_gnn_b, L3_mix_qkv_w, L3_mix_qkv_b, L3_mix_proj_w, L3_mix_proj_b, L3_mix_fc1_w, L3_mix_fc1_b, L3_mix_fc2_w, L3_mix_fc2_b, L3_mix_ln1_w, L3_mix_ln1_b, L3_mix_ln2_w, L3_mix_ln2_b, L3_ffn_router_w, L3_ffn_w1, L3_ffn_b1, L3_ffn_w2, L3_ffn_b2):
    import jax
    import jax.numpy as jnp

    def _L0_gnn_ref(x, W1, a_src1, a_dst1, b1, W2, a_src2, a_dst2, b2, edge_list):
        import jax, jax.numpy as jnp
        import numpy as np
        NEG_SLOPE = 0.2
        EPS = 1e-16
        N_NODES = 512
        N_EDGES = 4096
        D_IN = 768
        D_HID = 768
        H1 = 8
        H2 = 1

        def gat_layer(x, W, a_s, a_d, b, edge_index, concat):
            n = x.shape[0]
            H, C = a_s.shape
            h = (x @ W).reshape(n, H, C)
            src, dst = (edge_index[0], edge_index[1])
            alpha_s = jnp.einsum('nhc,hc->nh', h, a_s)
            alpha_d = jnp.einsum('nhc,hc->nh', h, a_d)
            e = jax.nn.leaky_relu(alpha_s[src] + alpha_d[dst], NEG_SLOPE)
            m = jax.ops.segment_max(e, dst, num_segments=n)
            e = jnp.exp(e - m[dst])
            denom = jax.ops.segment_sum(e, dst, num_segments=n)
            alpha = e / (denom[dst] + EPS)
            msg = h[src] * alpha[:, :, None]
            out = jax.ops.segment_sum(msg, dst, num_segments=n)
            out = out.reshape(n, H * C) if concat else out.mean(axis=1)
            return out + b
        h = gat_layer(x, W1, a_src1, a_dst1, b1, edge_list, concat=True)
        h = jax.nn.elu(h)
        out = gat_layer(h, W2, a_src2, a_dst2, b2, edge_list, concat=True)
        return out

    def _L0_mix_ref(x, ln1_g, ln1_b, qkv_w, qkv_b, w_orf, proj_w, proj_b, ln2_g, ln2_b, fc1_w, fc1_b, fc2_w, fc2_b):
        import jax, jax.numpy as jnp
        import numpy as np
        DIM = 768
        HEADS = 12
        HEAD_DIM = DIM // HEADS
        M = int(DIM * 0.5)
        HIDDEN = int(DIM * 4.0)
        SCALE = HEAD_DIM ** (-0.25)
        EPSILON = 1e-08
        LN_EPS = 1e-05

        def _orf(key):

            def one(k):
                a = jax.random.normal(k, (M, HEAD_DIM))
                q, _ = jnp.linalg.qr(a)
                return q.T
            ks = jax.random.split(key, HEADS)
            return jax.vmap(one)(ks) * np.sqrt(M)

        def _layernorm(x, g, b):
            mu = jnp.mean(x, axis=-1, keepdims=True)
            var = jnp.mean(jnp.square(x - mu), axis=-1, keepdims=True)
            return (x - mu) * jax.lax.rsqrt(var + LN_EPS) * g + b

        def _feature_map(x, w):
            xs = x * SCALE
            proj = jnp.einsum('bhnc,hcm->bhnm', xs, w)
            sq = 0.5 * jnp.sum(xs * xs, axis=-1, keepdims=True)
            return jnp.exp(proj - sq) / np.sqrt(M)

        def _performer_attn(x, qkv_w, qkv_b, w_orf, proj_w, proj_b):
            B, N, _ = x.shape
            qkv = x @ qkv_w + qkv_b
            qkv = qkv.reshape(B, N, 3, HEADS, HEAD_DIM)
            qkv = jnp.transpose(qkv, (2, 0, 3, 1, 4))
            q = _feature_map(qkv[0], w_orf)
            k = _feature_map(qkv[1], w_orf)
            v = qkv[2]
            k_sum = jnp.sum(k, axis=2)
            D = jnp.einsum('bhnm,bhm->bhn', q, k_sum)[..., None] + EPSILON
            ktv = jnp.einsum('bhnm,bhnc->bhmc', k, v)
            out = jnp.einsum('bhnm,bhmc->bhnc', q, ktv) / D
            out = jnp.transpose(out, (0, 2, 1, 3)).reshape(B, N, DIM)
            return out @ proj_w + proj_b
        h = x + _performer_attn(_layernorm(x, ln1_g, ln1_b), qkv_w, qkv_b, w_orf, proj_w, proj_b)
        y = _layernorm(h, ln2_g, ln2_b)
        y = jax.nn.gelu(y @ fc1_w + fc1_b) @ fc2_w + fc2_b
        return h + y

    def _L0_ffn_ref(x, input_ids, gate_w, gate_bias, w1, w2, w3, w1s, w2s, w3s):
        import jax, jax.numpy as jnp
        import numpy as np
        D = 768
        I = 192
        E = 8
        K = 2
        LIMIT = 10.0
        VOCAB = 2048

        def _expert(xf, W1, W2, W3):
            gate = jnp.minimum(xf @ W1, LIMIT)
            up = jnp.clip(xf @ W3, -LIMIT, LIMIT)
            return jax.nn.silu(gate) * up @ W2
        B, T, _ = x.shape
        flat = x.reshape(-1, D)
        N = flat.shape[0]
        scores = jnp.sqrt(jax.nn.softplus(flat @ gate_w))
        routed_scores = scores + gate_bias
        _, indices = jax.lax.top_k(routed_scores, K)
        weights = jnp.take_along_axis(scores, indices, axis=1)
        weights = weights / jnp.clip(weights.sum(axis=-1, keepdims=True), 1e-06)
        combine = jnp.zeros((N, E), dtype=weights.dtype)
        combine = combine.at[jnp.arange(N)[:, None], indices].add(weights)
        y = _expert(flat, w1s, w2s, w3s)
        gate_h = jnp.minimum(jnp.einsum('td,edi->eti', flat, w1), LIMIT)
        up_h = jnp.clip(jnp.einsum('td,edi->eti', flat, w3), -LIMIT, LIMIT)
        h = jax.nn.silu(gate_h) * up_h
        out_e = jnp.einsum('eti,eid->etd', h, w2)
        routed = jnp.einsum('etd,te->td', out_e, combine)
        return (y + routed).reshape(B, T, D)

    def _L1_gnn_ref(x, edge_index, W1, a_src1, a_dst1, b1, W2, a_src2, a_dst2, b2):
        import jax, jax.numpy as jnp
        import numpy as np
        N = 1250
        E_RAND = 20000
        NEG_SLOPE = 0.2

        def gat_layer(x, W, a_src, a_dst, bias, src, dst, heads, out_c, concat):
            n = x.shape[0]
            h = (x @ W).reshape(n, heads, out_c)
            al_s = jnp.einsum('nhc,hc->nh', h, a_src)
            al_d = jnp.einsum('nhc,hc->nh', h, a_dst)
            e = jax.nn.leaky_relu(al_s[src] + al_d[dst], NEG_SLOPE)
            m = jax.ops.segment_max(e, dst, num_segments=n)
            ex = jnp.exp(e - m[dst])
            z = jax.ops.segment_sum(ex, dst, num_segments=n)
            alpha = ex / (z[dst] + 1e-16)
            msg = h[src] * alpha[:, :, None]
            out = jax.ops.segment_sum(msg, dst, num_segments=n)
            out = out.reshape(n, heads * out_c) if concat else out.mean(axis=1)
            return out + bias
        src, dst = (edge_index[0], edge_index[1])
        h = gat_layer(x, W1, a_src1, a_dst1, b1, src, dst, heads=8, out_c=96, concat=True)
        h = jax.nn.elu(h)
        out = gat_layer(h, W2, a_src2, a_dst2, b2, src, dst, heads=1, out_c=768, concat=False)
        return out

    def _L1_mix_ref(x, ln_gamma, ln_beta, w_qkv, w_proj, b_proj):
        import jax, jax.numpy as jnp
        import numpy as np
        DIM = 768
        HEADS = 12
        HEAD_DIM = DIM // HEADS
        EPS = 1e-06
        LN_EPS = 1e-05

        def _elu1(t):
            return jax.nn.elu(t) + 1.0
        bsz, n, dim = x.shape
        mu = jnp.mean(x, axis=-1, keepdims=True)
        var = jnp.mean(jnp.square(x - mu), axis=-1, keepdims=True)
        y = (x - mu) * jax.lax.rsqrt(var + LN_EPS) * ln_gamma + ln_beta
        qkv = jnp.einsum('bnd,ed->bne', y, w_qkv)
        qkv = qkv.reshape(bsz, n, 3, HEADS, HEAD_DIM)
        qkv = jnp.transpose(qkv, (2, 0, 3, 1, 4))
        q, k, v = (_elu1(qkv[0]), _elu1(qkv[1]), qkv[2])
        kv = jnp.einsum('bhnd,bhne->bhde', k, v)
        k_sum = jnp.sum(k, axis=2)
        z = 1.0 / (jnp.einsum('bhnd,bhd->bhn', q, k_sum) + EPS)
        out = jnp.einsum('bhnd,bhde->bhne', q, kv) * z[..., None]
        out = jnp.transpose(out, (0, 2, 1, 3)).reshape(bsz, n, dim)
        return jnp.einsum('bnd,ed->bne', out, w_proj) + b_proj

    def _L1_ffn_ref(x, fc1_w, fc1_b, fc2_w, fc2_b, gate_pair, atom_in_w, atom_in_b, atom_out_w, atom_out_b, balance_bias):
        import jax, jax.numpy as jnp
        import numpy as np
        ATOM = {'vm': 0, 'im': 1, 'cm': 2, 'sc': 3, 'cc': 4}
        TASK_PAIRS = [('vm', 'sc'), ('vm', 'cc'), ('im', 'sc'), ('im', 'cc'), ('cm', 'sc'), ('cm', 'cc')]
        SRC_IDX = np.array([[ATOM[l], ATOM[r]] for l, r in TASK_PAIRS], dtype=np.int32)
        DST_IDX = np.array([[ATOM[r], ATOM[l]] for l, r in TASK_PAIRS], dtype=np.int32)
        NCLS = 6
        NATOMS = 5

        def _l2norm(x, eps=1e-12):
            return x / jnp.clip(jnp.linalg.norm(x, axis=-1, keepdims=True), eps)
        src = jnp.asarray(SRC_IDX)
        dst = jnp.asarray(DST_IDX)
        D = x.shape[-1]
        H = atom_in_w.shape[1]
        cls_tokens = x[:, :NCLS]
        patch_tokens = x[:, NCLS:]
        patch_out = jax.nn.gelu(patch_tokens @ fc1_w.T + fc1_b, approximate=False) @ fc2_w.T + fc2_b
        gate_in = _l2norm(cls_tokens.astype(jnp.float32))
        gate_w = _l2norm(gate_pair.astype(jnp.float32))
        gate_logits = jnp.einsum('bnd,nrd->bnr', gate_in, gate_w) + balance_bias[None]
        route_probs = jax.nn.softmax(gate_logits, axis=-1)
        chosen_route = jnp.argmax(route_probs, axis=-1)
        hid_all = jax.nn.gelu(jnp.einsum('bnd,ahd->bnah', cls_tokens, atom_in_w) + atom_in_b[None, None], approximate=False)
        sh_pair = hid_all[:, jnp.arange(NCLS)[:, None], src, :]
        route_out_w = atom_out_w[dst.reshape(-1)].reshape(NCLS, 2, D, H)
        route_candidates = jnp.einsum('bnrh,nrdh->bnrd', sh_pair, route_out_w) + atom_out_b[dst][None]
        chosen_w = jnp.take_along_axis(route_probs, chosen_route[..., None], axis=-1)
        chosen_cand = jnp.take_along_axis(route_candidates, chosen_route[:, :, None, None], axis=2)[:, :, 0]
        cls_out = chosen_cand * chosen_w.astype(chosen_cand.dtype)
        return jnp.concatenate([cls_out, patch_out], axis=1)

    def _L2_gnn_ref(x, edge_index, W, b):
        import jax, jax.numpy as jnp
        import numpy as np
        N_NODES = 625
        N_EDGES = 6250
        DIM = 768
        n = x.shape[0]
        loop = jnp.arange(n, dtype=edge_index.dtype)
        src = jnp.concatenate([edge_index[0], loop])
        dst = jnp.concatenate([edge_index[1], loop])
        deg = jax.ops.segment_sum(jnp.ones_like(dst, dtype=x.dtype), dst, num_segments=n)
        deg_inv_sqrt = jnp.where(deg > 0, jax.lax.rsqrt(deg), 0.0)
        norm = deg_inv_sqrt[src] * deg_inv_sqrt[dst]
        h = x @ W
        msg = h[src] * norm[:, None]
        out = jax.ops.segment_sum(msg, dst, num_segments=n)
        return out + b

    def _L2_mix_ref(x, Wq, bq, Wk, bk, Wv, bv, Wo, bo):
        import jax, jax.numpy as jnp
        import numpy as np
        FEATS = 768
        HEAD = 12

        def _phi(t):
            return jax.nn.elu(t) + 1.0
        b, n, f = x.shape
        h = HEAD
        d = f // h

        def heads(t):
            return t.reshape(b, n, h, d).transpose(0, 2, 1, 3)
        q = _phi(heads(x @ Wq + bq))
        k = _phi(heads(x @ Wk + bk))
        v = heads(x @ Wv + bv)
        kv = jnp.einsum('bhnd,bhne->bhde', k, v)
        ksum = k.sum(axis=2)
        z = 1.0 / jnp.einsum('bhld,bhd->bhl', q, ksum)
        num = jnp.einsum('bhld,bhde->bhle', q, kv)
        normed = num * z[..., None]
        out = normed.transpose(0, 2, 1, 3).reshape(b, n, f)
        return out @ Wo + bo

    def _L2_ffn_ref(x, shared_gate, shared_up, shared_down, routed_gate, routed_up, routed_down, router_w, routing_bias):
        import jax, jax.numpy as jnp
        import numpy as np
        B, S, H, I = (4, 128, 768, 1536)
        E, K = (3, 2)
        INIT = 0.02

        def _expert(x, gw, uw, dw):
            return jax.nn.silu(x @ gw) * (x @ uw) @ dw
        shared_out = _expert(x, shared_gate, shared_up, shared_down)
        routing_probs = jax.nn.sigmoid(x @ router_w + routing_bias)
        scores, indices = jax.lax.top_k(routing_probs, K)
        scores = scores / scores.sum(axis=-1, keepdims=True)
        combine_w = (jax.nn.one_hot(indices, E, dtype=x.dtype) * scores[..., None]).sum(axis=-2)
        g = jnp.einsum('bsh,ehi->ebsi', x, routed_gate)
        u = jnp.einsum('bsh,ehi->ebsi', x, routed_up)
        h = jax.nn.silu(g) * u
        out_e = jnp.einsum('ebsi,eih->ebsh', h, routed_down)
        combined = jnp.einsum('ebsh,bse->bsh', out_e, combine_w)
        return shared_out + combined

    def _L3_gnn_ref(x, edge_index, W, b):
        import jax, jax.numpy as jnp
        import numpy as np
        N_NODES = 625
        n = x.shape[0]
        loops = jnp.arange(n, dtype=edge_index.dtype)
        row = jnp.concatenate([edge_index[0], loops])
        col = jnp.concatenate([edge_index[1], loops])
        ones = jnp.ones(row.shape[0], dtype=x.dtype)
        deg = jax.ops.segment_sum(ones, col, num_segments=n)
        dinv = jnp.where(deg > 0, jax.lax.rsqrt(deg), 0.0)
        norm = dinv[row] * dinv[col]
        h = x @ W
        msg = h[row] * norm[:, None]
        out = jax.ops.segment_sum(msg, col, num_segments=n) + b
        return out

    def _L3_mix_ref(x, qkv_w, qkv_b, proj_w, proj_b, fc1_w, fc1_b, fc2_w, fc2_b, ln1_w, ln1_b, ln2_w, ln2_b):
        import jax, jax.numpy as jnp
        import numpy as np
        DIM = 768
        NUM_HEADS = 12
        HEAD_DIM = DIM // NUM_HEADS
        HIDDEN = int(DIM * 4.0)
        EPS = 1e-08

        def layer_norm(x, w, b):
            mu = jnp.mean(x, axis=-1, keepdims=True)
            var = jnp.mean(jnp.square(x - mu), axis=-1, keepdims=True)
            return (x - mu) * jax.lax.rsqrt(var + EPS) * w + b

        def linear_attention(x, qkv_w, qkv_b, proj_w, proj_b):
            B, N, C = x.shape
            qkv = (x @ qkv_w + qkv_b).reshape(B, N, 3, NUM_HEADS, HEAD_DIM)
            qkv = qkv.transpose(2, 0, 3, 1, 4)
            q, k, v = (qkv[0], qkv[1], qkv[2])
            q = jax.nn.elu(q) + 1.0
            k = jax.nn.elu(k) + 1.0
            kv = jnp.einsum('bhsd,bhse->bhde', k, v)
            z = 1.0 / jnp.einsum('bhsd,bhd->bhs', q, k.sum(axis=-2))
            out = jnp.einsum('bhde,bhsd,bhs->bhse', kv, q, z)
            out = out.transpose(0, 2, 1, 3).reshape(B, N, C)
            return out @ proj_w + proj_b
        y = linear_attention(layer_norm(x, ln1_w, ln1_b), qkv_w, qkv_b, proj_w, proj_b)
        x = x + y
        h = layer_norm(x, ln2_w, ln2_b)
        h = jax.nn.gelu(h @ fc1_w + fc1_b, approximate=False) @ fc2_w + fc2_b
        return x + h

    def _L3_ffn_ref(x, router_w, w1, b1, w2, b2):
        import jax, jax.numpy as jnp
        import numpy as np
        import math
        SQRT_2_OVER_PI = math.sqrt(2.0 / math.pi)

        def gelu(x):
            return x * 0.5 * (1.0 + jnp.tanh(SQRT_2_OVER_PI * (x + 0.044715 * x * x * x)))
        B, S, D = x.shape
        E = router_w.shape[1]
        T = B * S
        C = T // E
        xf = x.reshape(T, D)
        router_logits = xf @ router_w
        router_probs = jax.nn.softmax(router_logits, axis=-1)
        expert_gate = jnp.max(router_probs, axis=-1)
        expert_index = jnp.argmax(router_probs, axis=-1)
        expert_mask = jax.nn.one_hot(expert_index, E, dtype=xf.dtype)
        position_in_expert = (jnp.cumsum(expert_mask, axis=0) * expert_mask).astype(jnp.int32)
        expert_mask = expert_mask * (position_in_expert < C).astype(xf.dtype)
        expert_mask_flat = jnp.sum(expert_mask, axis=-1)
        expert_gate = expert_gate * expert_mask_flat
        combine = (expert_gate * expert_mask_flat)[:, None, None] * jax.nn.one_hot(expert_index, E, dtype=xf.dtype)[:, :, None] * jax.nn.one_hot(position_in_expert, C, dtype=xf.dtype)
        dispatch = (combine != 0).astype(xf.dtype)
        expert_inputs = jnp.einsum('td,tec->ecd', xf, dispatch)
        h = gelu(jnp.einsum('ecd,edm->ecm', expert_inputs, w1) + b1[:, None, :])
        expert_outputs = gelu(jnp.einsum('ecm,emd->ecd', h, w2) + b2[:, None, :])
        out = jnp.einsum('ecd,tec->td', expert_outputs, combine)
        return out.reshape(B, S, D)
    edge_index = jnp.stack([src, dst])
    xn = _layernorm(x, axis=-1)
    x = x + _L0_gnn_ref(xn, L0_gnn_W1, L0_gnn_a_src1, L0_gnn_a_dst1, L0_gnn_b1, L0_gnn_W2, L0_gnn_a_src2, L0_gnn_a_dst2, L0_gnn_b2, edge_index) + _L0_mix_ref(xn[None], L0_mix_ln1_g, L0_mix_ln1_b, L0_mix_qkv_w, L0_mix_qkv_b, L0_mix_w_orf, L0_mix_proj_w, L0_mix_proj_b, L0_mix_ln2_g, L0_mix_ln2_b, L0_mix_fc1_w, L0_mix_fc1_b, L0_mix_fc2_w, L0_mix_fc2_b)[0]
    x = x + _L0_ffn_ref(_layernorm(x, axis=-1)[None], L0_ffn_input_ids, L0_ffn_gate_w, L0_ffn_gate_bias, L0_ffn_w1, L0_ffn_w2, L0_ffn_w3, L0_ffn_w1s, L0_ffn_w2s, L0_ffn_w3s)[0]
    xn = _layernorm(x, axis=-1)
    x = x + _L1_gnn_ref(xn, edge_index, L1_gnn_W1, L1_gnn_a_src1, L1_gnn_a_dst1, L1_gnn_b1, L1_gnn_W2, L1_gnn_a_src2, L1_gnn_a_dst2, L1_gnn_b2) + _L1_mix_ref(xn[None], L1_mix_ln_gamma, L1_mix_ln_beta, L1_mix_w_qkv, L1_mix_w_proj, L1_mix_b_proj)[0]
    x = x + _L1_ffn_ref(_layernorm(x, axis=-1)[None], L1_ffn_fc1_w, L1_ffn_fc1_b, L1_ffn_fc2_w, L1_ffn_fc2_b, L1_ffn_gate_pair, L1_ffn_atom_in_w, L1_ffn_atom_in_b, L1_ffn_atom_out_w, L1_ffn_atom_out_b, L1_ffn_balance_bias)[0]
    xn = _layernorm(x, axis=-1)
    x = x + _L2_gnn_ref(xn, edge_index, L2_gnn_W, L2_gnn_b) + _L2_mix_ref(xn[None], L2_mix_Wq, L2_mix_bq, L2_mix_Wk, L2_mix_bk, L2_mix_Wv, L2_mix_bv, L2_mix_Wo, L2_mix_bo)[0]
    x = x + _L2_ffn_ref(_layernorm(x, axis=-1)[None], L2_ffn_shared_gate, L2_ffn_shared_up, L2_ffn_shared_down, L2_ffn_routed_gate, L2_ffn_routed_up, L2_ffn_routed_down, L2_ffn_router_w, L2_ffn_routing_bias)[0]
    xn = _layernorm(x, axis=-1)
    x = x + _L3_gnn_ref(xn, edge_index, L3_gnn_W, L3_gnn_b) + _L3_mix_ref(xn[None], L3_mix_qkv_w, L3_mix_qkv_b, L3_mix_proj_w, L3_mix_proj_b, L3_mix_fc1_w, L3_mix_fc1_b, L3_mix_fc2_w, L3_mix_fc2_b, L3_mix_ln1_w, L3_mix_ln1_b, L3_mix_ln2_w, L3_mix_ln2_b)[0]
    x = x + _L3_ffn_ref(_layernorm(x, axis=-1)[None], L3_ffn_router_w, L3_ffn_w1, L3_ffn_b1, L3_ffn_w2, L3_ffn_b2)[0]
    return x

_drawn_inputs = setup_inputs


def setup_inputs(seed=0):
    import zlib

    import numpy as np

    out = dict(_drawn_inputs(seed))
    spreads = {'L0_gnn_b1': (0.0, 0.1),
     'L0_gnn_b2': (0.0, 0.1),
     'L0_mix_ln1_g': (1.0, 0.2),
     'L0_mix_ln1_b': (0.0, 0.1),
     'L0_mix_qkv_b': (0.0, 0.1),
     'L0_mix_proj_b': (0.0, 0.1),
     'L0_mix_ln2_g': (1.0, 0.2),
     'L0_mix_ln2_b': (0.0, 0.1),
     'L0_mix_fc1_b': (0.0, 0.1),
     'L0_mix_fc2_b': (0.0, 0.1),
     'L0_ffn_gate_bias': (0.0, 0.1),
     'L1_gnn_b1': (0.0, 0.1),
     'L1_gnn_b2': (0.0, 0.1),
     'L1_mix_ln_gamma': (1.0, 0.2),
     'L1_mix_ln_beta': (0.0, 0.1),
     'L1_ffn_fc1_b': (0.0, 0.1),
     'L1_ffn_fc2_b': (0.0, 0.1),
     'L1_ffn_balance_bias': (0.0, 0.1),
     'L2_gnn_b': (0.0, 0.1),
     'L2_ffn_routing_bias': (0.0, 0.1),
     'L3_gnn_b': (0.0, 0.1),
     'L3_mix_qkv_b': (0.0, 0.1),
     'L3_mix_proj_b': (0.0, 0.1),
     'L3_mix_fc1_b': (0.0, 0.1),
     'L3_mix_fc2_b': (0.0, 0.1),
     'L3_mix_ln1_w': (1.0, 0.2),
     'L3_mix_ln1_b': (0.0, 0.1),
     'L3_mix_ln2_w': (1.0, 0.2),
     'L3_mix_ln2_b': (0.0, 0.1)}
    factors = {}
    for name, (base, spread) in spreads.items():
        noise = np.random.default_rng([zlib.crc32(name.encode()), seed]).standard_normal(out[name].shape)
        drawn = base * np.exp(spread * noise) if base else spread * noise
        out[name] = jnp.asarray(drawn.astype(out[name].dtype))
    for name, factor in factors.items():
        out[name] = (out[name] * factor).astype(out[name].dtype)
    return out
```

```python
from contextlib import ExitStack, contextmanager

import concourse.bass as bass
import numpy as np
from concourse import mybir

F32 = mybir.dt.float32
F32R = mybir.dt.float32r
BF16 = mybir.dt.bfloat16
I32 = mybir.dt.int32
I16 = mybir.dt.int16
ALU = mybir.AluOpType
ACT = mybir.ActivationFunctionType
AX_X = mybir.AxisListType.X

P = 128
N = 512
D = 768
KC = D // P
NT = N // P
EDGES = 16384
EC = EDGES // P
HEADS = 12
HD = D // HEADS
ORF = 384
GAT = 8
C1 = D // GAT
NCLS = 6
ATOMS = 5
PAIRS = [(0, 3), (0, 4), (1, 3), (1, 4), (2, 3), (2, 4)]
FF = 192
NO_EDGE = -1e30

COLUMNS = [
    ("L0_gnn_b1", 48), ("L0_gnn_b2", 6), ("L0_mix_ln1_g", 6), ("L0_mix_ln1_b", 6), ("L0_mix_qkv_b", 18),
    ("L0_mix_proj_b", 6), ("L0_mix_ln2_g", 6), ("L0_mix_ln2_b", 6), ("L0_mix_fc1_b", 24), ("L0_mix_fc2_b", 6),
    ("L1_gnn_b1", 6), ("L1_gnn_b2", 6), ("L1_mix_ln_gamma", 6), ("L1_mix_ln_beta", 6), ("L1_mix_b_proj", 6),
    ("L1_ffn_in_b", 12), ("L1_ffn_fc2_b", 6), ("L2_gnn_b", 6), ("L2_mix_bq", 6), ("L2_mix_bo", 6),
    ("L3_gnn_b", 6), ("L3_mix_qkv_b", 18), ("L3_mix_proj_b", 6), ("L3_mix_fc1_b", 24), ("L3_mix_fc2_b", 6),
    ("L3_mix_ln1_w", 6), ("L3_mix_ln1_b", 6), ("L3_mix_ln2_w", 6), ("L3_mix_ln2_b", 6),
    ("L3_ffn_b1", 16), ("L3_ffn_b2", 48), ("zero", 6),
]
COL = {}
for _name, _n in COLUMNS:
    COL[_name] = sum(n for _, n in COLUMNS[:len(COL)])
NCOL = sum(n for _, n in COLUMNS)
R0, R2, R3, GP = 0, 8, 12, 20
NSMALL = 32
ROW_L0, ROW_L0B, ROW_L1, ROW_L1B, ROW_KV0, ROW_KV1, ROW_KV2, ROW_KV3, NROWS = 0, 8, 9, 10, 11, 12, 13, 14, 15
V_GATE, V_ROUTE, V_BAL, NVEC = 0, 8, 12, 24
TURNS = dict(mix0=3 + 1 + 8, gnn0=16, ffn0=9, mix1=4, gnn1=2, ffn1=4, gnn2=1, mix2=4, ffn2=24, gnn3=1, mix3=12, ffn3=6)


class Side:

    def __init__(self, eng, name, own, events):
        self.eng, self.name, self.own, self.events = eng, name, own, events
        self.seen, self.i, self.per, self.pending = {}, None, {}, {}

    def due(self, sem, k=1):
        n = self.seen[sem.name] = self.seen.get(sem.name, 0) + k
        return n if self.i is None else self.i * self.per.get(sem.name, 0) + n

    def step(self, ins):
        ins.then_inc(self.own, 1)
        self.eng.wait_ge(self.own, self.due(self.own))

    @contextmanager
    def loop(self, what, n):
        key = f"{what}/{self.name}"
        self.per = self.events.get(key, {})
        before, held = dict(self.seen), dict(self.pending)
        with self.eng.Fori(0, n) as i:
            self.i = i
            yield i
            self.i = None
        per = {s: v - before.get(s, 0) for s, v in self.seen.items() if v != before.get(s, 0)}
        check_events(key, per, self.per)
        assert held == self.pending, (key, held, self.pending)
        for s, v in per.items():
            self.seen[s] += (n - 1) * v


def check_events(key, found, stated):
    assert found == stated, f"{key}: one iteration waits for {found}"


LOOP_EVENTS = {
    "edges/pe": {"dve_to_pe": 2},
    "performer/pe": {"dve_to_pe": 4, "act_to_pe": 4, "bank_free_by_dve0": 2, "bank_free_by_dve1": 2,
        "bank_free_by_dve2": 2, "bank_free_by_dve3": 4, "bank_free_by_dve7": 4, "w_split0": 1,
        "bank_free_by_act3": 8, "bank_free_by_act4": 8, "bank_free_by_act5": 8, "bank_free_by_act6": 4,
        "w_split1": 1},
    "mlp0/pe": {"dve_to_pe": 6, "bank_free_by_dve4": 1, "bank_free_by_dve5": 1, "bank_free_by_dve0": 1,
        "bank_free_by_dve1": 1, "bank_free_by_dve2": 1, "bank_free_by_dve3": 1, "w_split0": 2,
        "bank_free_by_act3": 1, "bank_free_by_act4": 1, "bank_free_by_act5": 1, "w_split1": 2,
        "bank_free_by_act0": 1, "bank_free_by_act1": 1, "bank_free_by_act2": 1},
    "performer/act": {"dve_to_act": 4, "tile_for_act": 28, "orf_in": 16, "bank_free_by_act3": 8,
        "bank_free_by_act4": 8, "bank_free_by_act5": 8, "bank_free_by_act6": 4},
    "mlp0/act": {"tile_for_act": 6, "bank_free_by_act3": 1, "bank_free_by_act4": 1, "bank_free_by_act5": 1,
        "bank_free_by_act0": 1, "bank_free_by_act1": 1, "bank_free_by_act2": 1},
    "edges/dve": {"tile_for_dve": 2},
    "performer/dve": {"dve_own": 8, "tile_for_dve": 14, "bank_free_by_dve0": 2, "bank_free_by_dve1": 2,
        "bank_free_by_dve2": 2, "bank_free_by_dve3": 4, "act_to_dve": 2, "bank_free_by_dve7": 4},
    "mlp0/dve": {"tile_for_dve": 6, "bank_free_by_dve0": 1, "bank_free_by_dve1": 1, "bank_free_by_dve2": 1,
        "bank_free_by_dve3": 1, "bank_free_by_dve4": 1, "bank_free_by_dve5": 1, "act_to_dve": 6},
    "gat0/pe": {"dve_to_pe": 13, "bank_free_by_dve4": 2, "bank_free_by_dve5": 2, "bank_free_by_dve0": 3,
        "bank_free_by_dve1": 3, "bank_free_by_dve2": 2, "bank_free_by_dve3": 2, "bank_free_by_dve6": 2,
        "w_split0": 2, "w_split1": 2, "bank_free_by_act0": 2, "bank_free_by_act1": 2, "bank_free_by_act2": 2,
        "bank_free_by_act3": 2, "bank_free_by_act4": 1, "bank_free_by_act5": 1},
    "gat0/act": {"dve_to_act": 17, "tile_for_act": 10, "bank_free_by_act3": 2, "bank_free_by_act4": 1,
        "bank_free_by_act5": 1, "bank_free_by_act0": 2, "bank_free_by_act1": 2, "bank_free_by_act2": 2,
        "rows_free": 1},
    "gat0/dve": {"dve_own": 18, "tile_for_dve": 16, "bank_free_by_dve0": 3, "bank_free_by_dve1": 3,
        "bank_free_by_dve2": 2, "bank_free_by_dve3": 2, "bank_free_by_dve4": 2, "bank_free_by_dve5": 2,
        "act_to_dve": 27, "bank_free_by_dve6": 2, "rows_in": 16},
    "experts0/pe": {"dve_to_pe": 7, "bank_free_by_dve4": 2, "bank_free_by_dve5": 2, "bank_free_by_dve0": 2,
        "bank_free_by_dve1": 2, "bank_free_by_dve2": 2, "bank_free_by_dve3": 2, "bank_free_by_dve6": 6,
        "w_split0": 3, "w_split1": 3, "bank_free_by_act0": 1, "bank_free_by_act1": 1, "bank_free_by_act2": 1,
        "bank_free_by_act3": 1, "bank_free_by_act4": 1, "bank_free_by_act5": 1},
    "experts0/act": {"dve_to_act": 6, "tile_for_act": 6, "bank_free_by_act0": 1, "bank_free_by_act1": 1,
        "bank_free_by_act2": 1, "bank_free_by_act3": 1, "bank_free_by_act4": 1, "bank_free_by_act5": 1},
    "experts0/dve": {"tile_for_dve": 18, "bank_free_by_dve0": 2, "bank_free_by_dve1": 2, "bank_free_by_dve2": 2,
        "bank_free_by_dve3": 2, "bank_free_by_dve4": 2, "bank_free_by_dve5": 2, "act_to_dve": 6,
        "bank_free_by_dve6": 6},
    "attention1/pe": {"dve_to_pe": 4, "bank_free_by_dve4": 2, "bank_free_by_dve5": 2, "bank_free_by_dve1": 2,
        "bank_free_by_dve2": 2, "bank_free_by_dve3": 2, "w_split0": 1, "w_split1": 1, "bank_free_by_act0": 2},
    "gat1/pe": {"dve_to_pe": 7, "bank_free_by_dve0": 1, "bank_free_by_dve1": 1, "bank_free_by_dve2": 1,
        "bank_free_by_dve3": 1, "bank_free_by_dve6": 1, "bank_free_by_act2": 1, "bank_free_by_act3": 1},
    "attention1/act": {"dve_to_act": 6, "tile_for_act": 2, "bank_free_by_act0": 2},
    "gat1/act": {"dve_to_act": 4, "tile_for_act": 2, "bank_free_by_act2": 1, "bank_free_by_act3": 1},
    "attention1/dve": {"dve_own": 2, "tile_for_dve": 10, "bank_free_by_dve1": 2, "bank_free_by_dve2": 2,
        "bank_free_by_dve3": 2, "bank_free_by_dve4": 2, "bank_free_by_dve5": 2, "act_to_dve": 8},
    "gat1/dve": {"dve_own": 19, "tile_for_dve": 5, "bank_free_by_dve0": 1, "bank_free_by_dve1": 1,
        "bank_free_by_dve2": 1, "bank_free_by_dve3": 1, "act_to_dve": 7, "bank_free_by_dve6": 1},
    "attention2/pe": {"dve_to_pe": 4, "bank_free_by_dve4": 2, "bank_free_by_dve5": 2, "bank_free_by_dve1": 2,
        "bank_free_by_dve2": 2, "bank_free_by_dve3": 2, "w_split0": 1, "w_split1": 1, "bank_free_by_act0": 2},
    "experts2/pe": {"dve_to_pe": 7, "bank_free_by_dve4": 2, "bank_free_by_dve5": 2, "bank_free_by_dve0": 2,
        "bank_free_by_dve1": 2, "bank_free_by_dve2": 2, "bank_free_by_dve3": 2, "bank_free_by_dve6": 1,
        "w_split0": 3, "bank_free_by_act3": 1, "bank_free_by_act4": 1, "bank_free_by_act5": 1, "w_split1": 3,
        "bank_free_by_act0": 1, "bank_free_by_act1": 1, "bank_free_by_act2": 1},
    "attention3/pe": {"dve_to_pe": 4, "bank_free_by_dve4": 2, "bank_free_by_dve5": 2, "bank_free_by_dve1": 2,
        "bank_free_by_dve2": 2, "bank_free_by_dve3": 2, "w_split0": 1, "w_split1": 1, "bank_free_by_act0": 2},
    "mlp3/pe": {"dve_to_pe": 6, "bank_free_by_dve4": 1, "bank_free_by_dve5": 1, "bank_free_by_dve0": 1,
        "bank_free_by_dve1": 1, "bank_free_by_dve2": 1, "bank_free_by_dve3": 1, "w_split0": 2,
        "bank_free_by_act3": 1, "bank_free_by_act4": 1, "bank_free_by_act5": 1, "w_split1": 2,
        "bank_free_by_act0": 1, "bank_free_by_act1": 1, "bank_free_by_act2": 1},
    "attention2/act": {"dve_to_act": 6, "tile_for_act": 2, "bank_free_by_act0": 2},
    "experts2/act": {"dve_to_act": 6, "tile_for_act": 6, "bank_free_by_act3": 1, "bank_free_by_act4": 1,
        "bank_free_by_act5": 1, "bank_free_by_act0": 1, "bank_free_by_act1": 1, "bank_free_by_act2": 1},
    "attention3/act": {"dve_to_act": 6, "tile_for_act": 2, "bank_free_by_act0": 2},
    "mlp3/act": {"tile_for_act": 6, "bank_free_by_act3": 1, "bank_free_by_act4": 1, "bank_free_by_act5": 1,
        "bank_free_by_act0": 1, "bank_free_by_act1": 1, "bank_free_by_act2": 1},
    "attention2/dve": {"dve_own": 2, "tile_for_dve": 10, "bank_free_by_dve1": 2, "bank_free_by_dve2": 2,
        "bank_free_by_dve3": 2, "bank_free_by_dve4": 2, "bank_free_by_dve5": 2, "act_to_dve": 8},
    "experts2/dve": {"tile_for_dve": 13, "bank_free_by_dve0": 2, "bank_free_by_dve1": 2, "bank_free_by_dve2": 2,
        "bank_free_by_dve3": 2, "bank_free_by_dve4": 2, "bank_free_by_dve5": 2, "act_to_dve": 6,
        "bank_free_by_dve6": 1},
    "attention3/dve": {"dve_own": 2, "tile_for_dve": 10, "bank_free_by_dve1": 2, "bank_free_by_dve2": 2,
        "bank_free_by_dve3": 2, "bank_free_by_dve4": 2, "bank_free_by_dve5": 2, "act_to_dve": 8},
    "mlp3/dve": {"tile_for_dve": 6, "bank_free_by_dve0": 1, "bank_free_by_dve1": 1, "bank_free_by_dve2": 1,
        "bank_free_by_dve3": 1, "bank_free_by_dve4": 1, "bank_free_by_dve5": 1, "act_to_dve": 6},
}


def build(nc, t, out, only=None, LOOP_EVENTS={}):
    parts = [p for p in TURNS if only is None or p in only]
    turns = sum(TURNS[p] for p in parts)
    ctx = ExitStack()
    with ctx:
        def sb(name, shape, dt=F32, where=ctx):
            return where.enter_context(nc.sbuf_tensor(name, shape, dt))

        def sem(name):
            return ctx.enter_context(nc.semaphore(name))

        raw = sb("raw", [P, 2, 3, KC, P])
        w_hi = sb("w_hi", [P, 2, 3, KC, P], F32R)
        w_lo = sb("w_lo", [P, 2, 3, KC, P], F32R)
        x = sb("x", [P, KC, N])
        acc = sb("acc", [P, KC, N])
        scr = sb("scr", [P, KC, N])
        aux = sb("aux", [P, 4, N])
        op = {n: (sb(f"{n}_hi", [P, KC, N], F32R), sb(f"{n}_lo", [P, KC, N], F32R)) for n in "ABH"}
        A, B, H = op["A"], op["B"], op["H"]
        row = sb("row", [P, N])
        rows = sb("rows", [P, 2, D])
        cols = sb("cols", [P, NCOL])
        small = sb("small", [P, KC, NSMALL])
        small_hi = sb("small_hi", [P, KC, NSMALL], F32R)
        small_lo = sb("small_lo", [P, KC, NSMALL], F32R)
        vecs = sb("vecs", [P, NVEC])
        counts = sb("counts", [P, NT, N], I16)
        no_edge = sb("no_edge", [P, NT, N], BF16)
        junk = sb("junk", [1, 16])
        ident = sb("ident", [P, P])
        ones = sb("ones", [P, P])
        ones_r = sb("ones_r", [P, P], F32R)
        ones_b = sb("ones_b", [P, 2], BF16)
        nv = sb("nv", [P, 16, NT])
        al = sb("al", [P, 2, NT, GAT])
        with ExitStack() as s:
            e_hi = sb("e_hi", [P, NT, N], F32R, s)
            e_lo = sb("e_lo", [P, NT, N], F32R, s)
        with ExitStack() as s:
            iota = sb("iota", [P, N], I16, s)
            src_i = sb("src_i", [P, EC], I32, s)
            dst_i = sb("dst_i", [P, EC], I32, s)
            src_f = sb("src_f", [P, EC], F32, s)
            dst_f = sb("dst_f", [P, EC], F32, s)
            hot = sb("hot", [P, 2, 2, N], BF16, s)
        with ExitStack() as s:
            q2 = sb("q2", [P, N], F32, s)
            k2 = sb("k2", [P, N], F32, s)
            orf = sb("orf", [P, 4, ORF], F32, s)
            k_feat = sb("k_feat", [P, NT, ORF], F32, s)
        with ExitStack() as s:
            k_n = sb("k_n", [P, NT, P], F32, s)
            v_n = sb("v_n", [P, NT, P + 2], F32, s)
            q_t = sb("q_t", [P, N], F32, s)
            kv = sb("kv", [P, P], F32, s)
            k_sum = sb("k_sum", [P, P], F32, s)
            same = sb("same", [P, P], F32, s)
        with ExitStack() as s:
            gate_s = sb("gate_s", [P, 12, NT, 8], F32, s)
            comb_n = sb("comb_n", [P, NT, 16], F32, s)
            with ExitStack() as s2:
                comb_t = sb("comb_t", [16, N], F32, s2)
                sel = sb("sel", [16, 3 * D], F32, s2)
                sel_now = sb("sel_now", [16, D], F32, s2)
            with ExitStack() as s2:
                tri = sb("tri", [P, P + 64], F32, s2)
                atom_b = sb("atom_b", [ATOMS, D], F32, s2)
                route = sb("route", [ATOMS, 12], F32, s2)
                cls_w = sb("cls_w", [ATOMS, 8], F32, s2)
                rt = sb("rt", [P, 6, 32], F32, s2)
        ps = ctx.enter_context(nc.psum_tensor("ps", [P, 8, N], F32))

        loaded, edges_in, rows_in, orf_in, sel_in = (sem(n) for n in ("loaded", "edges_in", "rows_in", "orf_in", "sel_in"))
        setup_done = sem("setup_done")
        pool_done = sem("pool_done")
        raw_in = [sem(f"raw_in{g}") for g in range(2)]
        hi_in = [sem(f"hi_in{g}") for g in range(2)]
        w_split = [sem(f"w_split{g}") for g in range(2)]
        w_used = [sem(f"w_used{g}") for g in range(2)]
        tile_for = {"act": sem("tile_for_act"), "dve": sem("tile_for_dve")}
        bank_free = {r: [sem(f"bank_free_by_{r}{b}") for b in range(8)] for r in ("act", "dve")}
        act_to_dve, act_to_pe = sem("act_to_dve"), sem("act_to_pe")
        dve_to_act, dve_to_pe = sem("dve_to_act"), sem("dve_to_pe")
        rows_free, orf_free = sem("rows_free"), sem("orf_free")
        act_own, dve_own = sem("act_own"), sem("dve_own")
        stored = sem("stored")

        block = ctx.enter_context(nc.Block())
        n_setup = 7

        @block.sync
        def _(sp):
            def load(n, g):
                sp.dma_start(raw[:, g], t["stream"][bass.ds(n * 2 + g, 1)].rearrange(
                    "o p (j k c) -> (o p) j k c", j=3, k=KC)).then_inc(raw_in[g], 16)

            for g in range(2):
                load(0, g)
            with sp.Fori(1, turns) as i:
                for g in range(2):
                    sp.wait_ge(w_split[g], i)
                    load(i, g)

        @block.gpsimd
        def _(pool):
            pool.memset(ident[:, :], 0.0).then_inc(pool_done, 1)
            pool.wait_ge(pool_done, 1)
            pool.affine_select(out=ident[:, :], in_=ident[:, :], compare_op=ALU.not_equal, fill=1.0, base=0,
                               pattern=[[-1, P]], channel_multiplier=1).then_inc(setup_done, 1)
            pool.iota(iota[:, :], pattern=[[1, N]], base=0, channel_multiplier=0).then_inc(setup_done, 1)
            pool.memset(ones[:, :], 1.0).then_inc(setup_done, 1)
            pool.memset(ones_r[:, :].bitcast(F32), 1.0).then_inc(setup_done, 1)
            pool.memset(ones_b[:, :], 1.0).then_inc(setup_done, 1)
            pool.memset(nv[:, :, :], 0.0).then_inc(setup_done, 1)
            pool.memset(hot[:, :, :, :], 0.0).then_inc(setup_done, 1)

            def high(i, g):
                pool.dma_start(w_hi[:, g], t["stream"][bass.ds(i * 2 + g, 1)].rearrange(
                    "o p (j k c) -> (o p) j k c", j=3, k=KC)).then_inc(hi_in[g], 16)

            def low(n, g):
                pool.wait_ge(raw_in[g], n * 16 + 16)
                pool.wait_ge(hi_in[g], n * 16 + 16)
                pool.tensor_tensor(w_lo[:, g], raw[:, g], w_hi[:, g], ALU.subtract).then_inc(w_split[g], 1)

            for g in range(2):
                high(0, g)
            for g in range(2):
                low(0, g)
            with pool.Fori(1, turns) as i:
                for g in range(2):
                    pool.wait_ge(w_used[g], i)
                    pool.wait_ge(setup_done, n_setup)
                    high(i, g)
                    low(i, g)

        @block.tensor
        def _(pe):
            S = Side(pe, "pe", None, LOOP_EVENTS)
            S.pending = {}

            def use(b):
                if S.pending.get(b):
                    reader = S.pending.pop(b)
                    pe.wait_ge(bank_free[reader][b], S.due(bank_free[reader][b]))

            def done(mm, b, reader):
                mm.then_inc(tile_for[reader], 1)
                S.pending[b] = reader

            def group(g):
                pe.wait_ge(w_split[g], S.due(w_split[g]))

            def group_end(g):
                pe.matmul(ps[0:2, 7, 0:2], ones_b[:, :], ones_b[:, :], start=True, stop=True,
                          skip_group_check=True).then_inc(w_used[g], 1)

            def mm3(o, wh, wl, xh, xl, first, last):
                pe.matmul(o, wh, xh, start=first, stop=False, skip_group_check=True)
                pe.matmul(o, wh, xl, start=False, stop=False, skip_group_check=True)
                return pe.matmul(o, wl, xh, start=False, stop=last, skip_group_check=True)

            def tile_t(b, g, j, X, reader, chunks=range(KC), c0=0, c1=N):
                use(b)
                for n, k in enumerate(chunks):
                    mm = mm3(ps[:, b, c0:c1], w_hi[:, g, j, k], w_lo[:, g, j, k], X[0][:, k, c0:c1], X[1][:, k, c0:c1],
                             n == 0, n == len(chunks) - 1)
                done(mm, b, reader)

            def turn_t(X, reader):
                for g in range(2):
                    group(g)
                    for j in range(3):
                        tile_t(3 * g + j, g, j, X, reader)
                    group_end(g)

            def turn_n(X, reader, mid=None):
                for g in range(2):
                    group(g)
                    for m in range(NT):
                        b = (4 * g + m) % 6
                        use(b)
                        o = ps[:, b, 0:384].rearrange("p (j c) -> p j c", j=3)
                        c = slice(m * P, m * P + P)
                        for k in range(KC):
                            mm3_ = mm3(o, X[0][:, k, c], X[1][:, k, c], w_hi[:, g, :, k], w_lo[:, g, :, k],
                                       k == 0, k == KC - 1)
                        done(mm3_, b, reader)
                    group_end(g)
                    if mid:
                        mid(g)

            def graph_t(reader):
                hn = [B[h][:, :, :].rearrange("p k n -> p (k n)").rearrange("p (m d) -> p m d", m=NT) for h in range(2)]
                for j in range(KC):
                    use(j)
                    for m in range(NT):
                        mm = mm3(ps[:, j], hn[0][:, m, j * P:j * P + P], hn[1][:, m, j * P:j * P + P],
                                 e_hi[:, m], e_lo[:, m], m == 0, m == NT - 1)
                    done(mm, j, reader)

            def norm():
                pe.wait_ge(dve_to_pe, S.due(dve_to_pe))
                use(6)
                for j in range(KC):
                    mm = pe.matmul(ps[:, 6], ones[:, :], norm_src[0][:, j], start=j == 0, stop=j == KC - 1,
                                   skip_group_check=True)
                done(mm, 6, "dve")
                use(7)
                for j in range(KC):
                    pe.wait_ge(act_to_pe, S.due(act_to_pe))
                    mm = pe.matmul(ps[:, 7], ones[:, :], aux[:, j % 4], start=j == 0, stop=j == KC - 1,
                                   skip_group_check=True)
                    if j < 2:
                        mm.then_inc(tile_for["act"], 1)
                done(mm, 7, "dve")
                pe.wait_ge(dve_to_pe, S.due(dve_to_pe, KC))

            norm_src = [x]

            def bcast(b, reader, ready=True, nlhs=P):
                pe.wait_ge(dve_to_pe, S.due(dve_to_pe))
                use(b)
                for m in range(NT):
                    mm = pe.matmul(ps[:, b, m * P:m * P + P], ones[:, :], aux[:, m, 0:P] if b != 3 else aux[:, m, P:2 * P],
                                   start=m == 0, stop=m == NT - 1, skip_group_check=True)
                done(mm, b, reader)

            def gat_rows(g):
                if g == 0:
                    bcast(6, "dve")
                else:
                    bcast(2, "act")
                    bcast(3, "act")

            def gat_den():
                pe.wait_ge(dve_to_pe, S.due(dve_to_pe, NT))
                use(6)
                for m in range(NT):
                    pe.matmul(ps[:, 6], ones_r[:, :], e_hi[:, m], start=m == 0, stop=False, skip_group_check=True)
                    mm = pe.matmul(ps[:, 6], ones_r[:, :], e_lo[:, m], start=False, stop=m == NT - 1,
                                   skip_group_check=True)
                done(mm, 6, "dve")

            def linear_attention(X, what):
                with S.loop(what, 3) as i:
                    for g in range(2):
                        group(g)
                        tile_t(0, g, 0, X, "act")
                        for m in range(NT):
                            b = 1 + m // 2
                            if m % 2 == 0:
                                use(b)
                            c = slice(m * P, m * P + P)
                            o = ps[:, b, (m % 2) * 256:(m % 2) * 256 + 256].rearrange("p (j c) -> p j c", j=2)
                            for k in range(KC):
                                mm = mm3(o, X[0][:, k, c], X[1][:, k, c], w_hi[:, g, 1:3, k], w_lo[:, g, 1:3, k],
                                         k == 0, k == KC - 1)
                            if m % 2 == 1:
                                done(mm, b, "dve")
                        group_end(g)
                        pe.wait_ge(dve_to_pe, S.due(dve_to_pe))
                        use(3)
                        for m in range(NT):
                            mm = pe.matmul(ps[:, 3, 0:P + 2], k_n[:, m], v_n[:, m], start=m == 0, stop=m == NT - 1,
                                           skip_group_check=True)
                        done(mm, 3, "dve")
                        use(3)
                        use(4)
                        done(pe.matmul(ps[:, 4], kv[:, :], q_t[:, :], start=True, stop=True), 4, "dve")
                        use(5)
                        done(pe.matmul(ps[:, 5], k_sum[:, :], q_t[:, :], start=True, stop=True), 5, "dve")
                        pe.wait_ge(dve_to_pe, S.due(dve_to_pe))
                    unpend()

            def performer(X, what):
                with S.loop(what, 3) as i:
                    for g in range(2):
                        group(g)
                        tile_t(0, g, 0, X, "dve")
                        tile_t(1, g, 1, X, "dve")
                        use(2)
                        for m in range(NT):
                            c = slice(m * P, m * P + P)
                            for k in range(KC):
                                mm = mm3(ps[:, 2, c], X[0][:, k, c], X[1][:, k, c], w_hi[:, g, 2, k], w_lo[:, g, 2, k],
                                         k == 0, k == KC - 1)
                        done(mm, 2, "dve")
                        group_end(g)
                        pe.wait_ge(dve_to_pe, S.due(dve_to_pe))
                        for h in range(2):
                            w = orf[:, 2 * g + h]
                            pe.wait_ge(act_to_pe, S.due(act_to_pe))
                            for m in range(NT):
                                use(3 + m % 2)
                                done(pe.matmul(ps[:, 3 + m % 2, 0:ORF], k2[:, m * P:m * P + P], w, start=True, stop=True),
                                     3 + m % 2, "act")
                            for r in range(3):
                                use(5 + r % 2)
                                done(pe.matmul(ps[:, 5 + r % 2], w[:, r * P:r * P + P], q2[:, :], start=True, stop=True),
                                     5 + r % 2, "act")
                            for b in (3, 4, 5, 6, 7):
                                use(b)
                            vh = aux[:, 0:2].rearrange("p a n -> p (a n)")[:, 0:NT * 2 * 66].rearrange(
                                "p (m h c) -> p m h c", m=NT, h=2)
                            for r in range(3):
                                for m in range(NT):
                                    mm = pe.matmul(ps[:, 7, r * 68:r * 68 + 66], k_feat[:, m, r * P:r * P + P],
                                                   vh[:, m, h], start=m == 0, stop=m == NT - 1, skip_group_check=True)
                            done(mm, 7, "dve")
                            use(7)
                            ktv = aux[:, 2, 0:ORF].rearrange("p (r c) -> p r c", r=3)
                            use(3)
                            for r in range(3):
                                mm = pe.matmul(ps[:, 3], ktv[:, r], scr[:, 3 + r], start=r == 0, stop=r == 2,
                                               skip_group_check=True)
                            done(mm, 3, "dve")
                        pe.wait_ge(dve_to_pe, S.due(dve_to_pe))
                    unpend()

            def gelu_mlp(X, what):
                with S.loop(what, 4) as i:
                    turn_t(X, "act")
                    pe.wait_ge(dve_to_pe, S.due(dve_to_pe, KC))
                    turn_t(H, "dve")
                    unpend()

            def router_n(X, c0, n):
                use(6)
                for m in range(NT):
                    for k in range(KC):
                        c = slice(m * P, m * P + P)
                        mm = mm3(ps[:, 6, m * 8:m * 8 + n], X[0][:, k, c], X[1][:, k, c], small_hi[:, k, c0:c0 + n],
                                 small_lo[:, k, c0:c0 + n], k == 0, k == KC - 1)
                done(mm, 6, "dve")

            def combine_rows():
                pe.wait_ge(dve_to_pe, S.due(dve_to_pe))
                use(6)
                for m in range(NT):
                    mm = pe.transpose(ps[0:16, 6, m * P:m * P + P], comb_n[:, m], ident[:, :])
                done(mm, 6, "dve")

            def experts(X, what, n, per_chunk):
                with S.loop(what, n) as i:
                    if not per_chunk:
                        pe.wait_ge(dve_to_pe, S.due(dve_to_pe))
                        use(6)
                        done(pe.matmul(ps[:, 6], sel_now[:, 0:P], comb_t[:, :], start=True, stop=True), 6, "dve")
                    turn_t(X, "act")
                    if per_chunk:
                        pe.wait_ge(dve_to_pe, S.due(dve_to_pe))
                    for g in range(2):
                        group(g)
                        for j in range(3):
                            f = 3 * g + j
                            if per_chunk:
                                use(6)
                                done(pe.matmul(ps[:, 6], sel_now[:, f * P:f * P + P], comb_t[:, :], start=True, stop=True),
                                     6, "dve")
                            tile_t(f, g, j, X, "dve")
                        group_end(g)
                    pe.wait_ge(dve_to_pe, S.due(dve_to_pe, KC))
                    turn_t(H, "dve")
                    unpend()

            def transposes(src, reader, dst_tile_free=True):
                for j in range(KC):
                    use(j)
                    for m in range(NT):
                        mm = pe.transpose(ps[:, j, m * P:m * P + P], src(m, j), ident[:, :])
                    done(mm, j, reader)

            def degrees():
                pe.wait_ge(dve_to_pe, S.due(dve_to_pe))
                use(6)
                for m in range(NT):
                    mm = pe.matmul(ps[:, 6], ones[:, :], aux[:, m], start=m == 0, stop=m == NT - 1, skip_group_check=True)
                done(mm, 6, "dve")

            def to_nodes(src):
                for g in range(2):
                    for m in range(NT):
                        b = (4 * g + m) % 6
                        use(b)
                        for c in range(3):
                            mm = pe.transpose(ps[:, b, c * P:c * P + P], src[:, 3 * g + c, m * P:m * P + P], ident[:, :])
                        done(mm, b, "act")
                        S.pending[b] = "dve"

            pe.wait_ge(setup_done, n_setup)
            for m in range(NT):
                mm = pe.matmul(ps[:, m], hot[:, 1, 0, 0:P], hot[:, 1, 0, :], start=True, stop=False, skip_group_check=True)
                if m >= 2:
                    mm.then_inc(tile_for["dve"], 1)
            with S.loop("edges", EC // 2) as i:
                for c in range(2):
                    pe.wait_ge(dve_to_pe, S.due(dve_to_pe))
                    for m in range(NT):
                        mm = pe.matmul(ps[:, m], hot[:, c, 0, m * P:m * P + P], hot[:, c, 1, :], start=False, stop=False,
                                       skip_group_check=True)
                    mm.then_inc(tile_for["dve"], 1)
            for m in range(NT):
                S.pending[m] = "dve"
            pe.wait_ge(dve_to_pe, S.due(dve_to_pe, NT))
            for m in range(NT):
                use(4 + m % 2)
                for k in range(NT):
                    mm = pe.transpose(ps[:, 4 + m % 2, k * P:k * P + P], aux[:, k, m * P:m * P + P], ident[:, :])
                done(mm, 4 + m % 2, "dve")

            def unpend():
                for b in list(S.pending):
                    use(b)

            def part(p):
                if p not in parts:
                    return False
                unpend()
                return True

            def norm_of(src):
                norm_src[0] = src
                norm()

            ran = lambda p: p in parts
            norm_of(x)
            if part("mix0"):
                norm_of(acc)
                unpend()
                performer(B, "performer")
                unpend()
                turn_t(H, "dve")
                norm_of(acc)
                unpend()
                gelu_mlp(B, "mlp0")
            if part("gnn0"):
                turn_n(A, "act")
                gat_rows(0)
                gat_rows(1)
                gat_den()
                graph_t("dve")
                unpend()
                with S.loop("gat0", GAT - 1) as i:
                    turn_n(A, "act")
                    pe.wait_ge(dve_to_pe, S.due(dve_to_pe, KC))
                    turn_n(H, "dve", gat_rows)
                    gat_den()
                    graph_t("dve")
                    unpend()
                pe.wait_ge(dve_to_pe, S.due(dve_to_pe, KC))
                turn_n(H, "dve")
                gat_rows(0)
                gat_rows(1)
                gat_den()
                graph_t("dve")
            if part("ffn0"):
                norm_of(x)
                router_n(A, R0, 8)
                combine_rows()
                unpend()
                experts(A, "experts0", 3, True)
            if ran("mix1") or ran("gnn1"):
                unpend()
                norm_of(x)
            if part("mix1"):
                norm_of(acc)
                unpend()
                linear_attention(B, "attention1")
                unpend()
                turn_t(H, "dve")
            if part("gnn1"):
                turn_n(A, "act")
                pe.wait_ge(dve_to_pe, S.due(dve_to_pe))
                unpend()
                with S.loop("gat1", GAT) as i:
                    gat_rows(0)
                    gat_rows(1)
                    pe.wait_ge(dve_to_pe, S.due(dve_to_pe, NT))
                    for m in range(NT):
                        b = m
                        use(b)
                        for k in range(NT):
                            c = slice(m * P, m * P + P)
                            hn = [B[h][:, :, :].rearrange("p k n -> p (k n)").rearrange("p (m d) -> p m d", m=NT)
                                  for h in range(2)]
                            f = bass.ds(i * C1, C1)
                            pe.matmul(ps[:, b, 0:C1], e_hi[:, k, c], hn[0][:, k, f], start=k == 0, stop=False,
                                      skip_group_check=True)
                            pe.matmul(ps[:, b, 0:C1], e_hi[:, k, c], hn[1][:, k, f], start=False, stop=False,
                                      skip_group_check=True)
                            pe.matmul(ps[:, b, C1:C1 + 2], e_hi[:, k, c], ones_r[:, 0:2], start=False, stop=False,
                                      skip_group_check=True)
                            pe.matmul(ps[:, b, 0:C1], e_lo[:, k, c], hn[0][:, k, f], start=False, stop=False,
                                      skip_group_check=True)
                            mm = pe.matmul(ps[:, b, C1:C1 + 2], e_lo[:, k, c], ones_r[:, 0:2], start=False,
                                           stop=k == NT - 1, skip_group_check=True)
                        done(mm, b, "dve")
                    unpend()
                pe.wait_ge(dve_to_pe, S.due(dve_to_pe))
                acc_n = acc[:, :, :].rearrange("p k n -> p (k n)").rearrange("p (m d) -> p m d", m=NT)
                transposes(lambda m, j: acc_n[:, m, j * P:j * P + P], "act")
                pe.wait_ge(dve_to_pe, S.due(dve_to_pe, KC))
                turn_n(H, "act")
                gat_rows(0)
                gat_rows(1)
                gat_den()
                graph_t("dve")
            if part("ffn1"):
                norm_of(x)
                unpend()
                pe.wait_ge(dve_to_pe, S.due(dve_to_pe))
                for k in range(KC):
                    mm = pe.matmul(ps[:, 6, 0:30], ones[:, :], aux[:, k % 4, (k // 4) * 32:(k // 4) * 32 + 30],
                                   start=k == 0, stop=k == KC - 1, skip_group_check=True)
                done(mm, 6, "dve")
                for n in range(2):
                    for g in range(2):
                        group(g)
                        for j in range(3):
                            q = 6 * n + 3 * g + j
                            tile_t(q % 6, g, j, A, "act", c1=N if q < 2 else 8)
                        group_end(g)
                pe.wait_ge(dve_to_pe, S.due(dve_to_pe, 3))
                for n in range(2):
                    for g in range(2):
                        group(g)
                        for j in range(3):
                            f = 3 * g + j
                            if n == 0:
                                tile_t(f, g, j, H, "dve", chunks=range(2))
                            if n == 0 and f == 0:
                                use(6)
                            for k in range(2, KC) if n == 0 else range(KC):
                                mm = mm3(ps[:, 6, (6 * n + f) * 8:(6 * n + f) * 8 + 8], w_hi[:, g, j, k], w_lo[:, g, j, k],
                                         H[0][:, 2, (6 * n + k) * 8 - 16:(6 * n + k) * 8 - 8],
                                         H[1][:, 2, (6 * n + k) * 8 - 16:(6 * n + k) * 8 - 8], k == (2 if n == 0 else 0), k == KC - 1)
                        group_end(g)
                for f in range(KC):
                    mm = pe.matmul(ps[:, 6, 96 + f * 8:104 + f * 8], atom_b[:, f * P:f * P + P], cls_w[:, :], start=True,
                                   stop=True, skip_group_check=True)
                done(mm, 6, "dve")
            if ran("gnn2") or ran("mix2"):
                unpend()
                norm_of(x)
            if part("gnn2"):
                degrees()
                turn_n(A, "act")
                pe.wait_ge(dve_to_pe, S.due(dve_to_pe))
                graph_t("dve")
            if part("mix2"):
                linear_attention(A, "attention2")
                unpend()
                turn_t(H, "dve")
            if part("ffn2"):
                norm_of(x)
                router_n(A, R2, 4)
                combine_rows()
                unpend()
                experts(A, "experts2", 8, False)
            if ran("gnn3") or ran("mix3"):
                unpend()
                norm_of(x)
            if part("gnn3"):
                degrees()
                turn_n(A, "act")
                pe.wait_ge(dve_to_pe, S.due(dve_to_pe))
                graph_t("dve")
            if part("mix3"):
                norm_of(acc)
                unpend()
                linear_attention(B, "attention3")
                unpend()
                turn_t(H, "dve")
                norm_of(acc)
                unpend()
                gelu_mlp(B, "mlp3")
            if part("ffn3"):
                norm_of(x)
                router_n(A, R3, 8)
                to_nodes(acc)
                pe.wait_ge(dve_to_pe, S.due(dve_to_pe))
                use(6)
                for m in range(NT):
                    for k in range(m + 1):
                        mm = pe.matmul(ps[:, 6, m * 8:m * 8 + 8], tri[:, 0:P] if k == m else ones[:, :], gate_s[:, 7, k],
                                       start=k == 0, stop=k == m, skip_group_check=True)
                done(mm, 6, "dve")
                pe.wait_ge(dve_to_pe, S.due(dve_to_pe))
                for j in range(KC):
                    use(j)
                    for h in range(2):
                        bn = B[h][:, :, :].rearrange("p k n -> p (k n)").rearrange("p (m d) -> p m d", m=NT)
                        for m in range(NT):
                            mm = pe.matmul(ps[:, j], bn[:, m, j * P:j * P + P], e_hi[:, m], start=h == 0 and m == 0,
                                           stop=h == 1 and m == NT - 1, skip_group_check=True)
                    done(mm, j, "act")
                pe.wait_ge(dve_to_pe, S.due(dve_to_pe, KC))
                for n in range(3):
                    for g in range(2):
                        group(g)
                        for j in range(3):
                            q = 6 * n + 3 * g + j
                            if q < 16:
                                tile_t(q % 6, g, j, A, "act", c0=64 * (q // 2), c1=64 * (q // 2) + 64)
                        group_end(g)
                pe.wait_ge(dve_to_pe, S.due(dve_to_pe, 16))
                for n in range(3):
                    for g in range(2):
                        group(g)
                        for j in range(3):
                            f = 3 * g + j
                            use(f)
                            for e in range(3 * n, min(3 * n + 3, 8)):
                                for h in range(2):
                                    k, q = 2 * (e - 3 * n) + h, 2 * e + h
                                    c = slice(q % 8 * 64, q % 8 * 64 + 64)
                                    mm = mm3(ps[:, f, e * 64:e * 64 + 64], w_hi[:, g, j, k], w_lo[:, g, j, k],
                                             H[0][:, q // 8, c], H[1][:, q // 8, c], h == 0, h == 1)
                            done(mm, f, "act")
                        group_end(g)
                for m in range(NT):
                    use(m)
                    for k in range(NT):
                        mm = pe.transpose(ps[:, m, k * P:k * P + P], aux[:, k, m * P:m * P + P], ident[:, :])
                    done(mm, m, "act")
                    S.pending[m] = "dve"
                pe.wait_ge(act_to_pe, S.due(act_to_pe))
                to_nodes(scr)
                pe.wait_ge(dve_to_pe, S.due(dve_to_pe))
                graph_t("dve")

        @block.scalar
        def _(act):
            S = Side(act, "act", act_own, LOOP_EVENTS)
            first_rows = [True]
            marks = [0]

            def freed(ins, b):
                ins.then_inc(bank_free["act"][b], 1)
                act.wait_ge(bank_free["act"][b], S.due(bank_free["act"][b]))

            def mark(sem):
                marks[0] = (marks[0] + 1) % 7
                act.activation(junk[:, marks[0]:marks[0] + 1], ones[0:1, 0:1], ACT.Copy).then_inc(sem, 1)

            def load_rows(n):
                if not first_rows[0]:
                    act.wait_ge(rows_free, S.due(rows_free))
                first_rows[0] = False
                n = bass.ds(n, 1)
                act.dma_start(rows[:, :, :], t["rows"][n].rearrange("o a d -> (o a) d").partition_broadcast(P))\
                   .then_inc(rows_in, 16)

            def col(name, n=0):
                c = COL[name] + n
                return cols[:, c:c + 1] if isinstance(c, int) else cols[:, bass.ds(c, 1)]

            def high(dst, src):
                act.wait_ge(dve_to_act, S.due(dve_to_act))
                act.copy(dst, src).then_inc(act_to_dve, 1)

            def norm(src, dst, X):
                for j in range(KC):
                    act.wait_ge(dve_to_act, S.due(dve_to_act))
                    if j >= 4:
                        act.wait_ge(tile_for["act"], S.due(tile_for["act"]))
                    act.activation(aux[:, j % 4], scr[:, j], ACT.Square).then_inc(act_to_pe, 1)
                act.wait_ge(dve_to_act, S.due(dve_to_act))
                act.activation(row[:, :], row[:, :], ACT.Sqrt).then_inc(act_to_dve, 1)
                for j in range(KC):
                    high(X[0][:, j], dst[:, j])

            def features_n():
                sn = scr[:, :, :].rearrange("p k n -> p (k n)").rearrange("p (m d) -> p m d", m=NT)
                bn = B[0][:, :, :].rearrange("p k n -> p (k n)").rearrange("p (m d) -> p m d", m=NT)
                for g in range(2):
                    for m in range(NT):
                        c = slice(384 * g, 384 * g + 384)
                        b = (4 * g + m) % 6
                        act.wait_ge(tile_for["act"], S.due(tile_for["act"]))
                        freed(act.copy(sn[:, m, c], ps[:, b, 0:384]), b)
                        act.copy(bn[:, m, c], sn[:, m, c]).then_inc(act_to_dve, 1)

            def edge_weights():
                act.wait_ge(tile_for["act"], S.due(tile_for["act"], 2))
                for m in range(NT):
                    q = 2 * (m % 2)
                    e1 = act.activation(aux[:, q], ps[:, 2], ACT.Exp, bias=nv[:, 0, m:m + 1])
                    if m == NT - 1:
                        freed(e1, 2)
                    e2 = act.activation(aux[:, q + 1], ps[:, 3], ACT.Exp, bias=nv[:, 3, m:m + 1])
                    if m < NT - 1:
                        e2.then_inc(act_to_dve, 1)
                    else:
                        freed(e2, 3)
                    if m >= 1:
                        high(e_hi[:, m - 1], scr[:, m - 1])
                high(e_hi[:, NT - 1], scr[:, NT - 1])

            def head_output(bias, from_psum=False):
                for s in range(KC + 1):
                    if s < KC:
                        q = 2 * (s % 2)
                        if from_psum:
                            act.wait_ge(tile_for["act"], S.due(tile_for["act"]))
                            src = ps[:, s]
                        else:
                            act.wait_ge(dve_to_act, S.due(dve_to_act))
                            src = scr[:, s]
                        act.activation(aux[:, q], src, ACT.Exp, bias=bias(s))
                        r = act.activation(aux[:, q + 1], src, ACT.Relu, bias=bias(s))
                        if from_psum:
                            freed(r, s)
                            mark(act_to_dve)
                        else:
                            r.then_inc(act_to_dve, 1)
                    if s >= 1:
                        act.wait_ge(dve_to_act, S.due(dve_to_act))
                        act.activation(H[0][:, s - 1], scr[:, s - 1], ACT.Identity, bias=-1.0).then_inc(act_to_dve, 1)

            def performer(what):
                with S.loop(what, 3) as i:
                    act.dma_start(orf[0:HD, :, :], t["orf"][bass.ds(i, 1)].rearrange("o c (h r) -> (o c) h r", h=4))\
                       .then_inc(orf_in, 16)
                    act.wait_ge(orf_in, S.due(orf_in, 16))
                    for g in range(2):
                        act.wait_ge(dve_to_act, S.due(dve_to_act))
                        for h in range(2):
                            r = slice(h * HD, h * HD + HD)
                            act.copy(q2[0:HD, :], scr[r, 0])
                            act.activation(q2[HD:P, :], scr[r, 0], ACT.Square)
                            act.copy(k2[0:HD, :], scr[r, 1])
                            act.activation(k2[HD:P, :], scr[r, 1], ACT.Square).then_inc(act_to_pe, 1)
                            for m in range(NT):
                                act.wait_ge(tile_for["act"], S.due(tile_for["act"]))
                                freed(act.activation(k_feat[:, m], ps[:, 3 + m % 2, 0:ORF], ACT.Exp), 3 + m % 2)
                            for m in range(3):
                                act.wait_ge(tile_for["act"], S.due(tile_for["act"]))
                                freed(act.activation(scr[:, 3 + m], ps[:, 5 + m % 2], ACT.Exp), 5 + m % 2)
                        high(H[0][:, bass.ds(2 * i + g, 1)].rearrange("p o n -> p (o n)"), aux[:, 3])

            def linear_attention(what, bq):
                with S.loop(what, 3) as i:
                    for g in range(2):
                        b = col(bq, i * 2 + g)
                        act.wait_ge(tile_for["act"], S.due(tile_for["act"]))
                        act.activation(scr[:, 0], ps[:, 0], ACT.Exp, bias=b)
                        freed(act.activation(scr[:, 1], ps[:, 0], ACT.Relu, bias=b), 0)
                        mark(act_to_dve)
                        for half in range(2):
                            act.wait_ge(dve_to_act, S.due(dve_to_act))
                            act.activation(scr[:, 2 + half, 0:256], aux[:, half, 0:256], ACT.Exp)
                            act.activation(scr[:, 2 + half, 256:512], aux[:, half, 0:256], ACT.Relu)\
                               .then_inc(act_to_dve, 1)
                        high(H[0][:, bass.ds(2 * i + g, 1)].rearrange("p o n -> p (o n)"), aux[:, 2])

            def gelu_mlp(what, bias, func):
                with S.loop(what, 4) as i:
                    for j in range(KC):
                        act.wait_ge(tile_for["act"], S.due(tile_for["act"]))
                        freed(act.activation(scr[:, j], ps[:, j], func, bias=col(bias, i * KC + j)), j)
                        act.copy(H[0][:, j], scr[:, j]).then_inc(act_to_dve, 1)

            def experts(what, n):
                with S.loop(what, n) as i:
                    for j in range(KC):
                        act.wait_ge(tile_for["act"], S.due(tile_for["act"]))
                        freed(act.activation(scr[:, j], ps[:, j], ACT.Silu), j)
                    for j in range(KC):
                        high(H[0][:, j], scr[:, j])

            def router_exp():
                act.wait_ge(dve_to_act, S.due(dve_to_act))
                act.activation(gate_s[:, 1], gate_s[:, 0], ACT.Exp).then_inc(act_to_dve, 1)

            act.dma_start(src_i[:, :], t["src"]).then_inc(edges_in, 16)
            act.dma_start(dst_i[:, :], t["dst"]).then_inc(edges_in, 16)
            act.dma_start(x[:, :, :], t["x"]).then_inc(loaded, 16)
            act.dma_start(cols[:, :], t["cols"]).then_inc(loaded, 16)
            act.dma_start(small[:, :, :], t["small"]).then_inc(loaded, 16)
            act.dma_start(vecs[:, :], t["vecs"].partition_broadcast(P)).then_inc(loaded, 16)
            act.wait_ge(loaded, 64)
            act.wait_ge(setup_done, n_setup)
            S.step(act.copy(small_hi[:, :, :], small[:, :, :]))
            mark(act_to_dve)
            norm(x, acc, A)
            if "mix0" in parts:
                load_rows(ROW_KV0)
                norm(acc, scr, B)
                performer("performer")
                norm(acc, scr, B)
                gelu_mlp("mlp0", "L0_mix_fc1_b", ACT.Gelu_apprx_tanh)
            if "gnn0" in parts:
                load_rows(0)
                features_n()
                edge_weights()
                head_output(lambda j: col("L0_gnn_b1", j))
                with S.loop("gat0", GAT - 1) as i:
                    load_rows(i + 1)
                    act.wait_ge(dve_to_act, S.due(dve_to_act))
                    features_n()
                    edge_weights()
                    head_output(lambda j: col("L0_gnn_b1", i * KC + KC + j))
                load_rows(ROW_L0B)
                act.wait_ge(dve_to_act, S.due(dve_to_act))
                an = acc[:, :, :].rearrange("p k n -> p (k n)").rearrange("p (m d) -> p m d", m=NT)
                bn = B[0][:, :, :].rearrange("p k n -> p (k n)").rearrange("p (m d) -> p m d", m=NT)
                for m in range(NT):
                    act.copy(bn[:, m], an[:, m]).then_inc(act_to_dve, 1)
                edge_weights()
            if "ffn0" in parts:
                norm(x, acc, A)
                act.wait_ge(dve_to_act, S.due(dve_to_act))
                act.activation(gate_s[:, 2], gate_s[:, 1], ACT.Exp, scale=-1.0).then_inc(act_to_dve, 1)
                act.wait_ge(dve_to_act, S.due(dve_to_act))
                S.step(act.activation(gate_s[:, 4], gate_s[:, 3], ACT.Ln))
                mark(act_to_dve)
                act.wait_ge(dve_to_act, S.due(dve_to_act))
                act.activation(gate_s[:, 6], gate_s[:, 5], ACT.Sqrt).then_inc(act_to_dve, 1)
                act.dma_start(sel[0:16, :], t["sel0"]).then_inc(sel_in, 16)
                experts("experts0", 3)

            if "mix1" in parts or "gnn1" in parts:
                norm(x, acc, A)
            if "mix1" in parts:
                load_rows(ROW_KV1)
                norm(acc, scr, B)
                linear_attention("attention1", "zero")
            if "gnn1" in parts:
                load_rows(ROW_L1)
                act.wait_ge(dve_to_act, S.due(dve_to_act))
                features_n()
                with S.loop("gat1", GAT) as i:
                    edge_weights()
                head_output(lambda j: col("L1_gnn_b1", j), True)
                load_rows(ROW_L1B)
                act.wait_ge(dve_to_act, S.due(dve_to_act))
                features_n()
                edge_weights()
            if "ffn1" in parts:
                norm(x, acc, A)
                act.dma_start(atom_b[:, :], t["atom_b"]).then_inc(sel_in, 16)
                act.dma_start(route[:, :], t["route"]).then_inc(sel_in, 16)
                act.wait_ge(dve_to_act, S.due(dve_to_act))
                act.activation(rt[:, 1, 12:30], rt[:, 0, 12:30], ACT.Sqrt).then_inc(act_to_dve, 1)
                act.wait_ge(dve_to_act, S.due(dve_to_act))
                act.activation(rt[:, 3, 0:6], rt[:, 2, 0:6], ACT.Exp).then_inc(act_to_dve, 1)
                for q in range(12):
                    act.wait_ge(tile_for["act"], S.due(tile_for["act"]))
                    b = col("L1_ffn_in_b", q)
                    if q < 2:
                        freed(act.activation(scr[:, q], ps[:, q], ACT.Gelu, bias=b), q)
                        act.copy(H[0][:, q], scr[:, q]).then_inc(act_to_dve, 1)
                    else:
                        freed(act.activation(scr[:, 2, q * 8 - 16:q * 8 - 8], ps[:, q % 6, 0:8], ACT.Gelu, bias=b), q % 6)
                mark(act_to_dve)
                high(H[0][:, 2, 0:80], scr[:, 3, 0:80])

            def gcn():
                act.wait_ge(dve_to_act, S.due(dve_to_act))
                act.activation(row[:, :], row[:, :], ACT.Sqrt).then_inc(act_to_dve, 1)
                for m in range(NT):
                    high(e_hi[:, m], scr[:, m])
                act.wait_ge(dve_to_act, S.due(dve_to_act))
                features_n()

            if "gnn2" in parts or "mix2" in parts:
                norm(x, acc, A)
            if "gnn2" in parts:
                gcn()
            if "mix2" in parts:
                load_rows(ROW_KV2)
                linear_attention("attention2", "L2_mix_bq")
            if "ffn2" in parts:
                norm(x, acc, A)
                act.wait_ge(dve_to_act, S.due(dve_to_act))
                act.activation(gate_s[:, 2, :, 0:3], gate_s[:, 1, :, 0:3], ACT.Exp, scale=-1.0).then_inc(act_to_dve, 1)
                act.dma_start(sel[0:16, :], t["sel2"]).then_inc(sel_in, 16)
                experts("experts2", 8)
            if "gnn3" in parts or "mix3" in parts:
                norm(x, acc, A)
            if "gnn3" in parts:
                gcn()
            if "mix3" in parts:
                load_rows(ROW_KV3)
                norm(acc, scr, B)
                linear_attention("attention3", "L3_mix_qkv_b")
                norm(acc, scr, B)
                gelu_mlp("mlp3", "L3_mix_fc1_b", ACT.Gelu)
            if "ffn3" in parts:
                def nodes_high():
                    bn = B[0][:, :, :].rearrange("p k n -> p (k n)").rearrange("p (m d) -> p m d", m=NT)
                    for g in range(2):
                        for m in range(NT):
                            act.wait_ge(tile_for["act"], S.due(tile_for["act"]))
                            act.copy(bn[:, m, 384 * g:384 * g + 384], ps[:, (4 * g + m) % 6, 0:384])\
                               .then_inc(act_to_dve, 1)

                norm(x, acc, A)
                act.dma_start(tri[:, :], t["tri"]).then_inc(sel_in, 16)
                act.wait_ge(dve_to_act, S.due(dve_to_act))
                act.activation(gate_s[:, 2], gate_s[:, 1], ACT.Exp).then_inc(act_to_dve, 1)
                nodes_high()
                for j in range(KC):
                    act.wait_ge(tile_for["act"], S.due(tile_for["act"]))
                    freed(act.copy(scr[:, j], ps[:, j]), j)
                    act.copy(A[0][:, j], scr[:, j]).then_inc(act_to_dve, 1)
                for q in range(16):
                    act.wait_ge(tile_for["act"], S.due(tile_for["act"]))
                    if q == 0:
                        act.wait_ge(dve_to_act, S.due(dve_to_act))
                    c, c0 = slice(q % 8 * 64, q % 8 * 64 + 64), 64 * (q // 2)
                    freed(act.activation(scr[:, q // 8, c], ps[:, q % 6, c0:c0 + 64], ACT.Gelu_apprx_tanh,
                                         bias=col("L3_ffn_b1", q)), q % 6)
                    act.copy(H[0][:, q // 8, c], scr[:, q // 8, c]).then_inc(act_to_dve, 1)
                for n in range(3):
                    for f in range(KC):
                        act.wait_ge(tile_for["act"], S.due(tile_for["act"]))
                        for e in range(3 * n, min(3 * n + 3, 8)):
                            c = slice(e * 64, e * 64 + 64)
                            ins = act.activation(scr[:, f, c], ps[:, f, c], ACT.Gelu_apprx_tanh, bias=col("L3_ffn_b2", e * KC + f))
                        freed(ins, f)
                mark(act_to_pe)
                for m in range(NT):
                    act.wait_ge(tile_for["act"], S.due(tile_for["act"]))
                    act.copy(e_hi[:, m], ps[:, m]).then_inc(act_to_dve, 1)
                nodes_high()
            act.wait_ge(dve_to_act, S.due(dve_to_act))
            act.dma_start(out, x[:, :, :]).then_inc(stored, 16)
            act.wait_ge(stored, 16)

        @block.vector
        def _(dve):
            S = Side(dve, "dve", dve_own, LOOP_EVENTS)
            A_hi, A_lo = A
            eps_inv = 1.0 / D
            marks = [0]

            def freed(ins, b):
                ins.then_inc(bank_free["dve"][b], 1)
                dve.wait_ge(bank_free["dve"][b], S.due(bank_free["dve"][b]))

            def mark(sem):
                marks[0] = (marks[0] + 1) % 7
                dve.memset(junk[:, 8 + marks[0]:9 + marks[0]], 0.0).then_inc(sem, 1)

            def col(name, n=0):
                c = COL[name] + n
                return cols[:, c:c + 1] if isinstance(c, int) else cols[:, bass.ds(c, 1)]

            def low(X, j, v):
                dve.wait_ge(act_to_dve, S.due(act_to_dve))
                dve.tensor_tensor(X[1][:, j], v, X[0][:, j], ALU.subtract).then_inc(dve_to_pe, 1)

            def norm(src, dst, X, eps, gamma=None, beta=None):
                mark(dve_to_pe)
                dve.wait_ge(tile_for["dve"], S.due(tile_for["dve"]))
                freed(dve.tensor_scalar(row[:, :], ps[:, 6], -eps_inv, None, ALU.mult), 6)
                for j in range(KC):
                    dve.tensor_tensor(scr[:, j], src[:, j], row[:, :], ALU.add).then_inc(dve_to_act, 1)
                dve.wait_ge(tile_for["dve"], S.due(tile_for["dve"]))
                freed(dve.tensor_scalar(row[:, :], ps[:, 7], eps_inv, eps, ALU.mult, ALU.add), 7)
                mark(dve_to_act)
                dve.wait_ge(act_to_dve, S.due(act_to_dve))
                S.step(dve.reciprocal(row[:, :], row[:, :]))
                for j in range(KC):
                    y = dve.tensor_tensor(dst[:, j], scr[:, j], row[:, :], ALU.mult)
                    if gamma:
                        S.step(y)
                        y = dve.tensor_scalar(dst[:, j], dst[:, j], col(gamma, j), col(beta, j), ALU.mult, ALU.add)
                    y.then_inc(dve_to_act, 1)
                for j in range(KC):
                    low(X, j, dst[:, j])

            sn = scr[:, :, :].rearrange("p k n -> p (k n)").rearrange("p (m d) -> p m d", m=NT)
            accn = acc[:, :, :].rearrange("p k n -> p (k n)").rearrange("p (m d) -> p m d", m=NT)
            bn = [B[h][:, :, :].rearrange("p k n -> p (k n)").rearrange("p (m d) -> p m d", m=NT) for h in range(2)]
            flat = aux[:, :, :].rearrange("p a n -> p (a n)")

            def features_n():
                for g in range(2):
                    for m in range(NT):
                        c = slice(384 * g, 384 * g + 384)
                        dve.wait_ge(act_to_dve, S.due(act_to_dve))
                        ins = dve.tensor_tensor(bn[1][:, m, c], sn[:, m, c], bn[0][:, m, c], ALU.subtract)
                return ins

            def terms(src):
                dve.wait_ge(rows_in, S.due(rows_in, 16))
                for m in range(NT):
                    for r in range(2):
                        S.step(dve.tensor_tensor_reduce(flat[:, 0:D], src[:, m], rows[:, r], 1.0, 0.0, ALU.mult, ALU.add,
                                                        nv[:, r, m:m + 1]))
                mark(rows_free)

            def source_row():
                for m in range(NT):
                    ins = dve.tensor_scalar(aux[:, m, 0:P], ident[:, :], nv[:, 0, m:m + 1], None, ALU.mult)
                ins.then_inc(dve_to_pe, 1)

            def target_rows():
                dve.wait_ge(tile_for["dve"], S.due(tile_for["dve"]))
                dve.memset(junk[:, 15:16], 0.0)
                for m in range(NT):
                    ins = dve.tensor_tensor_reduce(aux[:, m], ps[:, 6], no_edge[:, m], 1.0, -3e38, ALU.add, ALU.max,
                                                   nv[:, 2, m:m + 1])
                freed(ins, 6)
                S.step(dve.tensor_tensor(nv[:, 4], nv[:, 1], nv[:, 2], ALU.add))
                S.step(dve.scalar_tensor_tensor(out=nv[:, 5], in0=nv[:, 4], scalar=0.2, in1=nv[:, 4], op0=ALU.mult,
                                                op1=ALU.max))
                S.step(dve.tensor_tensor(nv[:, 6], nv[:, 1], nv[:, 5], ALU.subtract))
                S.step(dve.scalar_tensor_tensor(out=nv[:, 7], in0=nv[:, 1], scalar=0.2, in1=nv[:, 5], op0=ALU.mult,
                                                op1=ALU.subtract))
                S.step(dve.tensor_scalar(nv[:, 3], nv[:, 0], 0.2, None, ALU.mult))
                for r in range(2):
                    for m in range(NT):
                        ins = dve.tensor_scalar(aux[:, m, r * P:r * P + P], ident[:, :], nv[:, 6 + r, m:m + 1], None,
                                                ALU.mult)
                    ins.then_inc(dve_to_pe, 1)

            def edge_weights():
                def low_e(m):
                    dve.tensor_tensor(e_lo[:, m], scr[:, m], e_hi[:, m], ALU.subtract).then_inc(dve_to_pe, 1)

                for m in range(NT):
                    q = 2 * (m % 2)
                    dve.wait_ge(act_to_dve, S.due(act_to_dve))
                    S.step(dve.tensor_tensor(aux[:, q], aux[:, q], aux[:, q + 1], ALU.max))
                    dve.scalar_tensor_tensor(out=scr[:, m], in0=aux[:, q], scalar=1.0, in1=counts[:, m], op0=ALU.min,
                                             op1=ALU.mult).then_inc(dve_to_act, 1)
                    if 1 <= m < NT - 1:
                        dve.wait_ge(act_to_dve, S.due(act_to_dve))
                    if m >= 1:
                        low_e(m - 1)
                dve.wait_ge(act_to_dve, S.due(act_to_dve))
                low_e(NT - 1)

            def inverse_sums():
                dve.wait_ge(tile_for["dve"], S.due(tile_for["dve"]))
                freed(dve.tensor_scalar(row[:, :], ps[:, 6], 1e-16, None, ALU.add), 6)
                S.step(dve.reciprocal(row[:, :], row[:, :]))

            def head_output(from_psum=False):
                for s in range(KC + 2):
                    if s < KC and not from_psum:
                        dve.wait_ge(tile_for["dve"], S.due(tile_for["dve"]))
                        freed(dve.tensor_tensor(scr[:, s], ps[:, s], row[:, :], ALU.mult), s)
                        mark(dve_to_act)
                    if 1 <= s <= KC:
                        j = s - 1
                        q = 2 * (j % 2)
                        dve.wait_ge(act_to_dve, S.due(act_to_dve))
                        dve.scalar_tensor_tensor(out=scr[:, j], in0=aux[:, q], scalar=1.0, in1=aux[:, q + 1], op0=ALU.min,
                                                 op1=ALU.add).then_inc(dve_to_act, 1)
                    if s >= 2:
                        j = s - 2
                        dve.wait_ge(act_to_dve, S.due(act_to_dve))
                        dve.scalar_tensor_tensor(out=H[1][:, j], in0=scr[:, j], scalar=-1.0, in1=H[0][:, j], op0=ALU.add,
                                                 op1=ALU.subtract).then_inc(dve_to_pe, 1)

            def add_n(g):
                for m in range(NT):
                    b = (4 * g + m) % 6
                    c = slice(384 * g, 384 * g + 384)
                    dve.wait_ge(tile_for["dve"], S.due(tile_for["dve"]))
                    freed(dve.tensor_tensor(accn[:, m, c], ps[:, b, 0:384], accn[:, m, c], ALU.add), b)

            def add_t(dst, bias=None):
                for j in range(KC):
                    dve.wait_ge(tile_for["dve"], S.due(tile_for["dve"]))
                    if bias:
                        ins = dve.scalar_tensor_tensor(out=dst[:, j], in0=ps[:, j], scalar=col(bias, j), in1=dst[:, j],
                                                       op0=ALU.add, op1=ALU.add)
                    else:
                        ins = dve.tensor_tensor(dst[:, j], ps[:, j], dst[:, j], ALU.add)
                    freed(ins, j)

            def gat_sum(bias):
                for j in range(KC):
                    dve.wait_ge(tile_for["dve"], S.due(tile_for["dve"]))
                    freed(dve.tensor_tensor(scr[:, j], ps[:, j], row[:, :], ALU.mult), j)
                    S.step(dve.scalar_tensor_tensor(out=x[:, j], in0=scr[:, j], scalar=col(bias, j), in1=x[:, j],
                                                    op0=ALU.add, op1=ALU.add))

            def performer(what):
                scale = HD ** -0.25
                vh = flat[:, 0:NT * 132].rearrange("p (m h c) -> p m h c", m=NT, h=2)
                S.step(dve.memset(orf[HD:P, :, :], -0.5))
                dve.wait_ge(rows_in, S.due(rows_in, 16))
                with S.loop(what, 3) as i:
                    for g in range(2):
                        for b, c in ((0, 0), (1, KC)):
                            dve.wait_ge(tile_for["dve"], S.due(tile_for["dve"]))
                            freed(dve.tensor_scalar(scr[:, b], ps[:, b], col("L0_mix_qkv_b", i * 2 + (g + c)), scale,
                                                    ALU.add, ALU.mult), b)
                        mark(dve_to_act)
                        dve.wait_ge(tile_for["dve"], S.due(tile_for["dve"]))
                        for m in range(NT):
                            ins = dve.tensor_tensor(vh[:, m, :, 0:HD],
                                                    ps[:, 2, m * P:m * P + P].rearrange("p (h c) -> p h c", h=2),
                                                    rows[:, 1, bass.ds(i * 256 + g * P, P)].rearrange("p (h c) -> p h c", h=2),
                                                    ALU.add)
                        freed(ins, 2)
                        dve.memset(vh[:, :, :, HD:HD + 2], 1.0).then_inc(dve_to_pe, 1)
                        for h in range(2):
                            dve.wait_ge(tile_for["dve"], S.due(tile_for["dve"]))
                            for r in range(3):
                                dve.tensor_copy(aux[:, 2, r * P:r * P + HD], ps[:, 7, r * 68:r * 68 + HD])
                                ins = dve.tensor_scalar(aux[:, 2, r * P + HD:r * P + P], ones[:, 0:HD],
                                                        ps[:, 7, r * 68 + HD:r * 68 + HD + 1], None, ALU.mult)
                            freed(ins, 7)
                            dve.wait_ge(tile_for["dve"], S.due(tile_for["dve"]))
                            S.step(dve.tensor_scalar(row[0:HD, :], ps[HD:P, 3], 1e-8 * ORF, None, ALU.add))
                            S.step(dve.reciprocal(row[0:HD, :], row[0:HD, :]))
                            freed(dve.tensor_tensor(aux[h * HD:h * HD + HD, 3], ps[0:HD, 3], row[0:HD, :], ALU.mult), 3)
                        mark(dve_to_act)
                        dve.wait_ge(act_to_dve, S.due(act_to_dve))
                        f = bass.ds(2 * i + g, 1)
                        dve.tensor_tensor(H[1][:, f].rearrange("p o n -> p (o n)"), aux[:, 3],
                                          H[0][:, f].rearrange("p o n -> p (o n)"), ALU.subtract).then_inc(dve_to_pe, 1)
                mark(rows_free)

            def linear_attention(what, eps):
                S.step(dve.memset(kv[:, :], 0.0))
                S.step(dve.memset(same[:, :], 0.0))
                dve.memset(same[0:HD, 0:HD], 1.0)
                S.step(dve.memset(same[HD:P, HD:P], 1.0))
                S.step(dve.memset(v_n[:, :, P:P + 2], 1.0))
                dve.wait_ge(rows_in, S.due(rows_in, 16))
                with S.loop(what, 3) as i:
                    for g in range(2):
                        c = bass.ds(i * 256 + g * P, P)
                        dve.wait_ge(act_to_dve, S.due(act_to_dve))
                        dve.scalar_tensor_tensor(out=q_t[:, :], in0=scr[:, 0], scalar=1.0, in1=scr[:, 1], op0=ALU.min,
                                                 op1=ALU.add)
                        for half in range(2):
                            dve.wait_ge(tile_for["dve"], S.due(tile_for["dve"]))
                            for m in range(2):
                                o = m * 256
                                dve.tensor_tensor(aux[:, half, m * P:m * P + P], ps[:, 1 + half, o:o + P], rows[:, 0, c],
                                                  ALU.add)
                                ins = dve.tensor_tensor(v_n[:, 2 * half + m, 0:P], ps[:, 1 + half, o + P:o + 2 * P],
                                                        rows[:, 1, c], ALU.add)
                            freed(ins, 1 + half)
                            mark(dve_to_act)
                        for half in range(2):
                            dve.wait_ge(act_to_dve, S.due(act_to_dve))
                            ins = dve.scalar_tensor_tensor(
                                out=k_n[:, 2 * half:2 * half + 2].rearrange("p m c -> p (m c)"), in0=scr[:, 2 + half, 0:256],
                                scalar=1.0, in1=scr[:, 2 + half, 256:512], op0=ALU.min, op1=ALU.add)
                        ins.then_inc(dve_to_pe, 1)
                        dve.wait_ge(tile_for["dve"], S.due(tile_for["dve"]))
                        dve.tensor_copy(kv[0:HD, 0:HD], ps[0:HD, 3, 0:HD])
                        dve.tensor_copy(kv[HD:P, HD:P], ps[HD:P, 3, HD:P])
                        freed(dve.tensor_scalar(k_sum[:, :], same[:, :], ps[:, 3, P:P + 1], None, ALU.mult), 3)
                        dve.wait_ge(tile_for["dve"], S.due(tile_for["dve"], 2))
                        freed(dve.tensor_scalar(row[:, :], ps[:, 5], eps, None, ALU.add), 5)
                        S.step(dve.reciprocal(row[:, :], row[:, :]))
                        freed(dve.tensor_tensor(aux[:, 2], ps[:, 4], row[:, :], ALU.mult), 4)
                        mark(dve_to_act)
                        dve.wait_ge(act_to_dve, S.due(act_to_dve))
                        f = bass.ds(2 * i + g, 1)
                        dve.tensor_tensor(H[1][:, f].rearrange("p o n -> p (o n)"), aux[:, 2],
                                          H[0][:, f].rearrange("p o n -> p (o n)"), ALU.subtract).then_inc(dve_to_pe, 1)
                mark(rows_free)

            def gelu_mlp(what, bias):
                with S.loop(what, 4) as i:
                    for j in range(KC):
                        low(H, j, scr[:, j])
                    add_t(x)
                for j in range(KC):
                    ins = dve.scalar_tensor_tensor(out=x[:, j], in0=acc[:, j], scalar=col(bias, j), in1=x[:, j],
                                                   op0=ALU.add, op1=ALU.add)
                S.step(ins)

            def experts(what, n, limit, per_chunk, periods):
                with S.loop(what, n) as i:
                    dve.tensor_copy(sel_now[:, :], sel[:, bass.ds(i * D, D)]).then_inc(dve_to_pe, 1) if per_chunk else \
                        dve.tensor_copy(sel_now[:, 0:P], sel[:, bass.ds(i * P, P)]).then_inc(dve_to_pe, 1)
                    if not per_chunk:
                        dve.wait_ge(tile_for["dve"], S.due(tile_for["dve"]))
                        freed(dve.tensor_copy(row[:, :], ps[:, 6]), 6)
                    for j in range(KC):
                        if per_chunk:
                            dve.wait_ge(tile_for["dve"], S.due(tile_for["dve"], 2))
                            freed(dve.scalar_tensor_tensor(out=scr[:, j], in0=scr[:, j], scalar=silu_limit, in1=ps[:, 6],
                                                           op0=ALU.min, op1=ALU.mult), 6)
                            freed(dve.tensor_scalar(aux[:, j % 4], ps[:, j], limit, -limit, ALU.min, ALU.max), j)
                            dve.tensor_tensor(scr[:, j], scr[:, j], aux[:, j % 4], ALU.mult).then_inc(dve_to_act, 1)
                        else:
                            dve.wait_ge(tile_for["dve"], S.due(tile_for["dve"]))
                            freed(dve.tensor_tensor(scr[:, j], scr[:, j], ps[:, j], ALU.mult), j)
                            dve.tensor_tensor(scr[:, j], scr[:, j], row[:, :], ALU.mult).then_inc(dve_to_act, 1)
                    for j in range(KC):
                        low(H, j, scr[:, j])
                    add_t(x)

            silu_limit = 10.0 / (1.0 + float(np.exp(-10.0)))

            def best(src, eq, mask):
                S.step(dve.tensor_reduce(nv[:, 8], src, AX_X, ALU.max))
                S.step(dve.tensor_tensor(eq, src, nv[:, 8, :].unsqueeze(2).to_broadcast(list(src.shape)), ALU.is_equal))
                S.step(dve.scalar_tensor_tensor(out=eq, in0=eq, scalar=-100.0, in1=gate_s[:, 11, :, 0:src.shape[2]],
                                                op0=ALU.mult, op1=ALU.add))
                S.step(dve.tensor_reduce(nv[:, 8], eq, AX_X, ALU.min))
                S.step(dve.tensor_scalar(nv[:, 8], nv[:, 8], 100.0, None, ALU.add))
                S.step(dve.tensor_tensor(mask, gate_s[:, 11, :, 0:src.shape[2]],
                                         nv[:, 8, :].unsqueeze(2).to_broadcast(list(src.shape)), ALU.is_equal))

            def numbers():
                for e in range(8):
                    ins = dve.memset(gate_s[:, 11, :, e:e + 1], float(e))
                S.step(ins)

            def router_logits(n):
                dve.wait_ge(tile_for["dve"], S.due(tile_for["dve"]))
                freed(dve.tensor_copy(gate_s[:, 0, :, 0:n], ps[:, 6, 0:32].rearrange("p (m e) -> p m e", m=NT)[:, :, 0:n]), 6)

            def combine(n, score, rank):
                mask, two, tmp = gate_s[:, 7, :, 0:n], gate_s[:, 8, :, 0:n], gate_s[:, 9, :, 0:n]
                best(rank, tmp, two)
                S.step(dve.scalar_tensor_tensor(out=rank, in0=two, scalar=-3e38, in1=rank, op0=ALU.mult, op1=ALU.add))
                best(rank, tmp, mask)
                S.step(dve.tensor_tensor(two, two, mask, ALU.add))
                S.step(dve.tensor_tensor(two, two, score, ALU.mult))
                S.step(dve.tensor_reduce(nv[:, 9], two, AX_X, ALU.add))
                S.step(dve.tensor_scalar(nv[:, 9], nv[:, 9], 1e-6 if n == 8 else 0.0, None, ALU.max))
                S.step(dve.reciprocal(nv[:, 9], nv[:, 9]))
                S.step(dve.memset(comb_n[:, :, :], 0.0))
                S.step(dve.memset(comb_n[:, :, 8:9], 1.0))
                dve.tensor_tensor(comb_n[:, :, 0:n], two, nv[:, 9, :].unsqueeze(2).to_broadcast([P, NT, n]), ALU.mult)\
                   .then_inc(dve_to_pe, 1)
                dve.wait_ge(tile_for["dve"], S.due(tile_for["dve"]))
                freed(dve.tensor_copy(comb_t[:, :], ps[0:16, 6]), 6)
                dve.wait_ge(sel_in, S.due(sel_in, 16))

            dve.wait_ge(edges_in, 32)
            dve.wait_ge(setup_done, n_setup)
            dve.tensor_copy(src_f[:, :], src_i[:, :])
            S.step(dve.tensor_copy(dst_f[:, :], dst_i[:, :]))
            with S.loop("edges", EC // 2) as i:
                for c in range(2):
                    dve.wait_ge(tile_for["dve"], S.due(tile_for["dve"]))
                    for r, f in enumerate((src_f, dst_f)):
                        ins = dve.tensor_scalar(hot[:, c, r], iota[:, :], f[:, bass.ds(i * 2 + c, 1)], None, ALU.is_equal)
                    ins.then_inc(dve_to_pe, 1)
            dve.wait_ge(tile_for["dve"], S.due(tile_for["dve"], 2))
            for m in range(NT):
                dve.tensor_copy(aux[:, m], ps[:, m]).then_inc(bank_free["dve"][m], 1)
                dve.wait_ge(bank_free["dve"][m], S.due(bank_free["dve"][m]))
                dve.tensor_copy(counts[:, m], aux[:, m]).then_inc(dve_to_pe, 1)
            for m in range(NT):
                dve.wait_ge(tile_for["dve"], S.due(tile_for["dve"]))
                freed(dve.tensor_scalar(no_edge[:, m], ps[:, 4 + m % 2], 0.0, NO_EDGE, ALU.is_equal, ALU.mult), 4 + m % 2)
            dve.wait_ge(loaded, 64)
            dve.wait_ge(act_to_dve, S.due(act_to_dve))
            S.step(dve.tensor_tensor(small_lo[:, :, :], small[:, :, :], small_hi[:, :, :], ALU.subtract))

            norm(x, acc, A, 1e-5)
            if "mix0" in parts:
                norm(acc, scr, B, 1e-5, "L0_mix_ln1_g", "L0_mix_ln1_b")
                performer("performer")
                add_t(acc, "L0_mix_proj_b")
                norm(acc, scr, B, 1e-5, "L0_mix_ln2_g", "L0_mix_ln2_b")
                gelu_mlp("mlp0", "L0_mix_fc2_b")
            if "gnn0" in parts:
                S.step(dve.memset(acc[:, :, :], 0.0))
                features_n()
                terms(sn)
                source_row()
                target_rows()
                edge_weights()
                inverse_sums()
                head_output()
                with S.loop("gat0", GAT - 1) as i:
                    mark(dve_to_act)
                    features_n()
                    terms(sn)
                    source_row()
                    add_n(0)
                    target_rows()
                    add_n(1)
                    edge_weights()
                    inverse_sums()
                    head_output()
                add_n(0)
                add_n(1)
                mark(dve_to_act)
                for m in range(NT):
                    dve.wait_ge(act_to_dve, S.due(act_to_dve))
                    dve.tensor_tensor(bn[1][:, m], accn[:, m], bn[0][:, m], ALU.subtract)
                terms(accn)
                source_row()
                target_rows()
                edge_weights()
                inverse_sums()
                gat_sum("L0_gnn_b2")
            if "ffn0" in parts:
                norm(x, acc, A, 1e-5)
                numbers()
                router_logits(8)
                S.step(dve.tensor_scalar(gate_s[:, 1], gate_s[:, 0], -1.0, None, ALU.mult))
                dve.tensor_tensor(gate_s[:, 1], gate_s[:, 1], gate_s[:, 0], ALU.max).then_inc(dve_to_act, 1)
                dve.wait_ge(act_to_dve, S.due(act_to_dve))
                dve.tensor_scalar(gate_s[:, 3], gate_s[:, 2], 1.0, None, ALU.add).then_inc(dve_to_act, 1)
                dve.wait_ge(act_to_dve, S.due(act_to_dve))
                dve.scalar_tensor_tensor(out=gate_s[:, 5], in0=gate_s[:, 0], scalar=0.0, in1=gate_s[:, 4], op0=ALU.max,
                                         op1=ALU.add).then_inc(dve_to_act, 1)
                dve.wait_ge(act_to_dve, S.due(act_to_dve))
                for m in range(NT):
                    ins = dve.tensor_tensor(gate_s[:, 10, m], gate_s[:, 6, m], vecs[:, V_GATE:V_GATE + 8], ALU.add)
                S.step(ins)
                combine(8, gate_s[:, 6], gate_s[:, 10])
                experts("experts0", 3, 10.0, True, 3)

            if "mix1" in parts or "gnn1" in parts:
                norm(x, acc, A, 1e-5)
            if "mix1" in parts:
                norm(acc, scr, B, 1e-5, "L1_mix_ln_gamma", "L1_mix_ln_beta")
                linear_attention("attention1", 1e-6)
                add_t(x, "L1_mix_b_proj")
            if "gnn1" in parts:
                mark(dve_to_act)
                features_n()
                dve.wait_ge(rows_in, S.due(rows_in, 16))
                for m in range(NT):
                    for r in range(2):
                        S.step(dve.tensor_tensor(flat[:, 0:D], sn[:, m], rows[:, r], ALU.mult))
                        S.step(dve.tensor_reduce(al[:, r, m], flat[:, 0:D].rearrange("p (h c) -> p h c", h=GAT), AX_X, ALU.add))
                mark(rows_free)
                mark(dve_to_pe)
                with S.loop("gat1", GAT) as i:
                    for r in range(2):
                        S.step(dve.tensor_copy(nv[:, r], al[:, r, :, bass.ds(i, 1)].rearrange("p m o -> p (m o)")))
                    source_row()
                    target_rows()
                    edge_weights()
                    for m in range(NT):
                        dve.wait_ge(tile_for["dve"], S.due(tile_for["dve"]))
                        S.step(dve.tensor_scalar(nv[:, 10, m:m + 1], ps[:, m, C1:C1 + 1], 1e-16, None, ALU.add))
                        S.step(dve.reciprocal(nv[:, 10, m:m + 1], nv[:, 10, m:m + 1]))
                        freed(dve.tensor_scalar(accn[:, m, bass.ds(i * C1, C1)], ps[:, m, 0:C1], nv[:, 10, m:m + 1], None,
                                                ALU.mult), m)
                mark(dve_to_pe)
                head_output(True)
                mark(dve_to_act)
                features_n()
                terms(sn)
                source_row()
                target_rows()
                edge_weights()
                inverse_sums()
                gat_sum("L1_gnn_b2")
            if "ffn1" in parts:
                norm(x, acc, A, 1e-5)
                g3 = small[:, :, GP:GP + 12]
                for k in range(KC):
                    o = aux[:, k % 4, (k // 4) * 32:(k // 4) * 32 + 30]
                    xk = acc[:, k, 0:NCLS]
                    dve.tensor_tensor(o[:, 0:12].rearrange("p (n r) -> p n r", r=2), g3[:, k].rearrange("p (n r) -> p n r", r=2),
                                      xk.unsqueeze(2).to_broadcast([P, NCLS, 2]), ALU.mult)
                    dve.tensor_tensor(o[:, 12:24], g3[:, k], g3[:, k], ALU.mult)
                    ins = dve.tensor_tensor(o[:, 24:30], xk, xk, ALU.mult)
                ins.then_inc(dve_to_pe, 1)
                dve.wait_ge(tile_for["dve"], S.due(tile_for["dve"]))
                freed(dve.tensor_copy(rt[:, 0, 0:30], ps[:, 6, 0:30]), 6)
                mark(dve_to_act)
                dve.wait_ge(act_to_dve, S.due(act_to_dve))
                S.step(dve.tensor_scalar(rt[:, 1, 12:30], rt[:, 1, 12:30], 1e-12, None, ALU.max))
                S.step(dve.reciprocal(rt[:, 1, 12:30], rt[:, 1, 12:30]))
                S.step(dve.tensor_tensor(rt[:, 0, 0:12], rt[:, 0, 0:12], rt[:, 1, 12:24], ALU.mult))
                lg = rt[:, 0, 0:12].rearrange("p (n r) -> p n r", r=2)
                S.step(dve.tensor_tensor(lg, lg, rt[:, 1, 24:30].unsqueeze(2).to_broadcast([P, NCLS, 2]), ALU.mult))
                S.step(dve.tensor_tensor(rt[:, 0, 0:12], rt[:, 0, 0:12], vecs[:, V_BAL:V_BAL + 12], ALU.add))
                S.step(dve.tensor_tensor(rt[:, 4, 0:6], lg[:, :, 1], lg[:, :, 0], ALU.subtract))
                S.step(dve.tensor_scalar(rt[:, 2, 0:6], rt[:, 4, 0:6], -1.0, None, ALU.mult))
                dve.tensor_tensor(rt[:, 2, 0:6], rt[:, 2, 0:6], rt[:, 4, 0:6], ALU.min).then_inc(dve_to_act, 1)
                dve.wait_ge(act_to_dve, S.due(act_to_dve))
                S.step(dve.tensor_scalar(rt[:, 3, 0:6], rt[:, 3, 0:6], 1.0, None, ALU.add))
                S.step(dve.reciprocal(rt[:, 3, 0:6], rt[:, 3, 0:6]))
                w = rt[:, 5, 0:12].rearrange("p (n r) -> p n r", r=2)
                S.step(dve.tensor_scalar(rt[:, 4, 0:6], rt[:, 4, 0:6], 0.0, None, ALU.is_gt))
                S.step(dve.tensor_tensor(w[:, :, 1], rt[:, 4, 0:6], rt[:, 3, 0:6], ALU.mult))
                S.step(dve.tensor_tensor(w[:, :, 0], rt[:, 3, 0:6], w[:, :, 1], ALU.subtract))
                S.step(dve.memset(cls_w[:, :], 0.0))
                dve.wait_ge(sel_in, S.due(sel_in, 32))
                S.step(dve.tensor_tensor(route[:, :], route[:, :], rt[0:ATOMS, 5, 0:12], ALU.mult))
                S.step(dve.tensor_reduce(cls_w[:, 0:6], route[:, :].rearrange("p (n r) -> p n r", r=2), AX_X, ALU.add))
                for q in range(2):
                    low(H, q, scr[:, q])
                S.step(dve.memset(scr[:, 3, 0:80], 0.0))
                dve.wait_ge(act_to_dve, S.due(act_to_dve))
                hid = scr[:, 2, 0:80].rearrange("p (a h n) -> p a h n", a=ATOMS, h=2)
                wei = scr[:, 3, 0:80].rearrange("p (a h n) -> p a h n", a=ATOMS, h=2)
                for n in range(NCLS):
                    for r in range(2):
                        of, to = PAIRS[n][r], PAIRS[n][1 - r]
                        ins = dve.tensor_scalar(wei[:, to, :, n:n + 1], hid[:, of, :, n:n + 1], w[:, n, r:r + 1], None, ALU.mult)
                ins.then_inc(dve_to_act, 1)
                dve.wait_ge(act_to_dve, S.due(act_to_dve))
                dve.tensor_tensor(H[1][:, 2, 0:80], scr[:, 3, 0:80], H[0][:, 2, 0:80], ALU.subtract).then_inc(dve_to_pe, 1)
                for j in range(KC):
                    dve.wait_ge(tile_for["dve"], S.due(tile_for["dve"]))
                    freed(dve.scalar_tensor_tensor(out=x[:, j, NCLS:N], in0=ps[:, j, NCLS:N], scalar=col("L1_ffn_fc2_b", j),
                                                   in1=x[:, j, NCLS:N], op0=ALU.add, op1=ALU.add), j)
                dve.wait_ge(tile_for["dve"], S.due(tile_for["dve"]))
                for r, o in enumerate((0, 48, 96)):
                    ins = dve.tensor_tensor(x[:, :, 0:NCLS], x[:, :, 0:NCLS],
                                            ps[:, 6, o:o + 48].rearrange("p (f n) -> p f n", n=8)[:, :, 0:NCLS], ALU.add)
                    if r < 2:
                        S.step(ins)
                freed(ins, 6)

            def gcn(bias):
                for m in range(NT):
                    S.step(dve.tensor_copy(aux[:, m], counts[:, m]))
                    c = slice(m * P, m * P + P)
                    S.step(dve.tensor_tensor(aux[:, m, c], aux[:, m, c], ident[:, :], ALU.add))
                mark(dve_to_pe)
                dve.wait_ge(tile_for["dve"], S.due(tile_for["dve"]))
                freed(dve.tensor_copy(row[:, :], ps[:, 6]), 6)
                mark(dve_to_act)
                dve.wait_ge(act_to_dve, S.due(act_to_dve))
                S.step(dve.reciprocal(row[:, :], row[:, :]))
                for m in range(NT):
                    S.step(dve.tensor_tensor_reduce(flat_junk, ident[:, :], row[:, m * P:m * P + P], 1.0, 0.0, ALU.mult,
                                                    ALU.add, nv[:, 14, m:m + 1]))
                for m in range(NT):
                    dve.scalar_tensor_tensor(out=scr[:, m], in0=aux[:, m], scalar=nv[:, 14, m:m + 1], in1=row[:, :],
                                             op0=ALU.mult, op1=ALU.mult).then_inc(dve_to_act, 1)
                for m in range(NT):
                    dve.wait_ge(act_to_dve, S.due(act_to_dve))
                    dve.tensor_tensor(e_lo[:, m], scr[:, m], e_hi[:, m], ALU.subtract)
                mark(dve_to_act)
                features_n()
                mark(dve_to_pe)
                add_t(x, bias)

            flat_junk = scr[:, 5, 0:P]
            if "gnn2" in parts or "mix2" in parts:
                norm(x, acc, A, 1e-5)
            if "gnn2" in parts:
                gcn("L2_gnn_b")
            if "mix2" in parts:
                linear_attention("attention2", 0.0)
                add_t(x, "L2_mix_bo")
            if "ffn2" in parts:
                norm(x, acc, A, 1e-5)
                numbers()
                router_logits(3)
                for m in range(NT):
                    ins = dve.tensor_tensor(gate_s[:, 1, m, 0:3], gate_s[:, 0, m, 0:3], vecs[:, V_ROUTE:V_ROUTE + 3], ALU.add)
                ins.then_inc(dve_to_act, 1)
                dve.wait_ge(act_to_dve, S.due(act_to_dve))
                S.step(dve.tensor_scalar(gate_s[:, 6, :, 0:3], gate_s[:, 2, :, 0:3], 1.0, None, ALU.add))
                S.step(dve.reciprocal(gate_s[:, 6, :, 0:3], gate_s[:, 6, :, 0:3]))
                S.step(dve.tensor_copy(gate_s[:, 10, :, 0:3], gate_s[:, 6, :, 0:3]))
                combine(3, gate_s[:, 6, :, 0:3], gate_s[:, 10, :, 0:3])
                experts("experts2", 8, 0.0, False, 8)
            if "gnn3" in parts or "mix3" in parts:
                norm(x, acc, A, 1e-5)
            if "gnn3" in parts:
                gcn("L3_gnn_b")
            if "mix3" in parts:
                norm(acc, scr, B, 1e-8, "L3_mix_ln1_w", "L3_mix_ln1_b")
                linear_attention("attention3", 0.0)
                add_t(acc, "L3_mix_proj_b")
                norm(acc, scr, B, 1e-8, "L3_mix_ln2_w", "L3_mix_ln2_b")
                gelu_mlp("mlp3", "L3_mix_fc2_b")
            if "ffn3" in parts:
                def nodes_low():
                    for g in range(2):
                        for m in range(NT):
                            c = slice(384 * g, 384 * g + 384)
                            b = (4 * g + m) % 6
                            dve.wait_ge(act_to_dve, S.due(act_to_dve))
                            freed(dve.tensor_tensor(bn[1][:, m, c], ps[:, b, 0:384], bn[0][:, m, c], ALU.subtract), b)

                norm(x, acc, A, 1e-5)
                numbers()
                router_logits(8)
                wide = [P, NT, 8]
                S.step(dve.tensor_reduce(nv[:, 11], gate_s[:, 0], AX_X, ALU.max))
                dve.tensor_tensor(gate_s[:, 1], gate_s[:, 0], nv[:, 11, :].unsqueeze(2).to_broadcast(wide), ALU.subtract)\
                   .then_inc(dve_to_act, 1)
                dve.wait_ge(act_to_dve, S.due(act_to_dve))
                S.step(dve.tensor_reduce(nv[:, 12], gate_s[:, 2], AX_X, ALU.add))
                S.step(dve.reciprocal(nv[:, 12], nv[:, 12]))
                best(gate_s[:, 0], gate_s[:, 9], gate_s[:, 7])
                dve.wait_ge(sel_in, S.due(sel_in, 16))
                mark(dve_to_pe)
                nodes_low()
                dve.wait_ge(tile_for["dve"], S.due(tile_for["dve"]))
                S.step(dve.tensor_scalar(gate_s[:, 8], ps[:, 6, 0:32].rearrange("p (m e) -> p m e", m=NT), 64.0, None, ALU.is_lt))
                S.step(dve.tensor_tensor(gate_s[:, 8], gate_s[:, 8], gate_s[:, 7], ALU.mult))
                freed(dve.scalar_tensor_tensor(out=gate_s[:, 9], in0=ps[:, 6, 0:32].rearrange("p (m e) -> p m e", m=NT),
                                               scalar=1.0, in1=gate_s[:, 8], op0=ALU.add, op1=ALU.mult), 6)
                S.step(dve.tensor_scalar(al[:, 0], gate_s[:, 9], -1.0, None, ALU.add))
                slots = [P, 8, 64]
                for m in range(NT):
                    S.step(dve.tensor_tensor(aux[:, m].rearrange("p (e c) -> p e c", e=8),
                                             tri[:, P:P + 64].unsqueeze(1).to_broadcast(slots),
                                             al[:, 0, m].unsqueeze(2).to_broadcast(slots), ALU.is_equal))
                for m in range(NT):
                    S.step(dve.tensor_copy(e_hi[:, m], aux[:, m]))
                    S.step(dve.tensor_scalar(aux[:, m], aux[:, m], nv[:, 12, m:m + 1], None, ALU.mult))
                mark(dve_to_pe)
                for j in range(KC):
                    low(A, j, scr[:, j])
                mark(dve_to_act)
                for q in range(16):
                    dve.wait_ge(act_to_dve, S.due(act_to_dve))
                    c = slice(q % 8 * 64, q % 8 * 64 + 64)
                    dve.tensor_tensor(H[1][:, q // 8, c], scr[:, q // 8, c], H[0][:, q // 8, c], ALU.subtract)\
                       .then_inc(dve_to_pe, 1)
                for m in range(NT):
                    dve.wait_ge(act_to_dve, S.due(act_to_dve))
                    freed(dve.tensor_tensor(e_lo[:, m], ps[:, m], e_hi[:, m], ALU.subtract), m)
                nodes_low()
                mark(dve_to_pe)
                add_t(x)
            mark(dve_to_act)


def stacked(inputs, *names):
    return [np.asarray(inputs[n]) for n in names]


def padded(a, n, axis):
    shape = list(a.shape)
    shape[axis] = n - a.shape[axis]
    return np.concatenate([a, np.zeros(shape, a.dtype)], axis)


def weight_stream(v, parts):
    out = []

    def cols_of(w):
        out.extend(w[:, 384 * g:384 * g + 384] for g in range(w.shape[1] // 384))

    def thirds(q, k, u):
        for f in range(KC):
            c = slice(f * P, f * P + P)
            out.append(np.concatenate([q[:, c], k[:, c], u[:, c]], 1))

    def qkv(w):
        thirds(w[:, 0:D], w[:, D:2 * D], w[:, 2 * D:])

    def mlp(w1, w2):
        for i in range(w1.shape[1] // D):
            cols_of(w1[:, i * D:i * D + D])
            cols_of(w2[i * D:i * D + D])

    def gated(g, u, d):
        for i in range(g.shape[1] // D):
            cols_of(g[:, i * D:i * D + D])
            cols_of(u[:, i * D:i * D + D])
            cols_of(d[i * D:i * D + D])

    if "mix0" in parts:
        qkv(v["L0_mix_qkv_w"])
        cols_of(v["L0_mix_proj_w"])
        mlp(v["L0_mix_fc1_w"], v["L0_mix_fc2_w"])
    if "gnn0" in parts:
        w1, w2 = v["L0_gnn_W1"], v["L0_gnn_W2"]
        cols_of(w1[:, 0:D])
        for h in range(1, GAT):
            cols_of(w1[:, h * D:h * D + D])
            cols_of(w2[h * D - D:h * D])
        cols_of(w2[7 * D:])
    if "ffn0" in parts:
        def wide(w, s):
            return padded(np.concatenate(list(w) + [s], 1), 3 * D, 1)
        down = padded(np.concatenate(list(v["L0_ffn_w2"]) + [v["L0_ffn_w2s"]], 0), 3 * D, 0)
        gated(wide(v["L0_ffn_w1"], v["L0_ffn_w1s"]), wide(v["L0_ffn_w3"], v["L0_ffn_w3s"]), down)
    if "mix1" in parts:
        qkv(v["L1_mix_w_qkv"].T)
        cols_of(v["L1_mix_w_proj"].T)
    if "gnn1" in parts:
        cols_of(v["L1_gnn_W1"])
        cols_of(v["L1_gnn_W2"])
    if "ffn1" in parts:
        ups = [v["L1_ffn_fc1_w"].T] + [w.T for w in v["L1_ffn_atom_in_w"]]
        cols_of(np.concatenate([padded(w, 256, 1) for w in ups], 1))
        downs = [v["L1_ffn_fc2_w"].T] + [w.T for w in v["L1_ffn_atom_out_w"]]
        down = np.concatenate([padded(w, 256, 0) for w in downs], 0)
        cols_of(down[0:D])
        cols_of(down[D:])
    if "gnn2" in parts:
        cols_of(v["L2_gnn_W"])
    if "mix2" in parts:
        thirds(v["L2_mix_Wq"], v["L2_mix_Wk"], v["L2_mix_Wv"])
        cols_of(v["L2_mix_Wo"])
    if "ffn2" in parts:
        gated(v["L2_ffn_shared_gate"], v["L2_ffn_shared_up"], v["L2_ffn_shared_down"])
        for e in range(3):
            gated(v["L2_ffn_routed_gate"][e], v["L2_ffn_routed_up"][e], v["L2_ffn_routed_down"][e])
    if "gnn3" in parts:
        cols_of(v["L3_gnn_W"])
    if "mix3" in parts:
        qkv(v["L3_mix_qkv_w"])
        cols_of(v["L3_mix_proj_w"])
        mlp(v["L3_mix_fc1_w"], v["L3_mix_fc2_w"])
    if "ffn3" in parts:
        up = np.concatenate([padded(w, 256, 1) for w in v["L3_ffn_w1"]], 1)
        cols_of(padded(up, 3 * D, 1))
        down = padded(np.concatenate([padded(w, 256, 0) for w in v["L3_ffn_w2"]], 0), 3 * D, 0)
        for i in range(3):
            cols_of(down[i * D:i * D + D])
    return np.stack([w.reshape(KC, P, 3, P).transpose(1, 2, 0, 3).reshape(P, 3 * D) for w in out])


def column_table(v):
    def in_columns(a):
        return a.reshape(-1, P).T

    special = {
        "L1_ffn_in_b": lambda: padded(np.concatenate([v["L1_ffn_fc1_b"][None], v["L1_ffn_atom_in_b"]], 0), 256, 1),
        "L3_ffn_b1": lambda: padded(v["L3_ffn_b1"], 256, 1),
        "zero": lambda: np.zeros(D, np.float32),
    }
    return np.concatenate([in_columns(np.ascontiguousarray(special[n]() if n in special else v[n])) for n, _ in COLUMNS], 1)


def selectors(width, expert_of):
    s = np.zeros((16, 3 * D), np.float32)
    for c in range(width):
        s[expert_of(c), c] = 1.0
    return s


def lay_out(v, parts):
    def t_layout(a):
        return a.reshape(KC, P, -1).transpose(1, 0, 2)

    small = np.zeros((D, NSMALL), np.float32)
    small[:, R0:R0 + 8] = v["L0_ffn_gate_w"]
    small[:, R2:R2 + 3] = v["L2_ffn_router_w"]
    small[:, R3:R3 + 8] = v["L3_ffn_router_w"]
    small[:, GP:GP + 12] = v["L1_ffn_gate_pair"].reshape(12, D).T
    rows = np.zeros((NROWS, 2, D), np.float32)
    rows[0:8, 0], rows[0:8, 1] = v["L0_gnn_a_src1"], v["L0_gnn_a_dst1"]
    rows[ROW_L0B, 0], rows[ROW_L0B, 1] = v["L0_gnn_a_src2"][0], v["L0_gnn_a_dst2"][0]
    rows[ROW_L1, 0], rows[ROW_L1, 1] = v["L1_gnn_a_src1"].reshape(D), v["L1_gnn_a_dst1"].reshape(D)
    rows[ROW_L1B, 0], rows[ROW_L1B, 1] = v["L1_gnn_a_src2"][0], v["L1_gnn_a_dst2"][0]
    rows[ROW_KV0] = v["L0_mix_qkv_b"].reshape(3, D)[1:]
    rows[ROW_KV2, 0], rows[ROW_KV2, 1] = v["L2_mix_bk"], v["L2_mix_bv"]
    rows[ROW_KV3] = v["L3_mix_qkv_b"].reshape(3, D)[1:]
    vecs = np.zeros(NVEC, np.float32)
    vecs[V_GATE:V_GATE + 8] = v["L0_ffn_gate_bias"]
    vecs[V_ROUTE:V_ROUTE + 3] = v["L2_ffn_routing_bias"]
    vecs[V_BAL:V_BAL + 12] = v["L1_ffn_balance_bias"].reshape(12)
    made = {
        "x": t_layout(v["x"].T),
        "src": v["src"].reshape(P, EC),
        "dst": v["dst"].reshape(P, EC),
        "stream": weight_stream(v, parts),
        "cols": column_table(v),
        "small": t_layout(small),
        "rows": rows,
        "vecs": vecs,
        "orf": v["L0_mix_w_orf"].reshape(3, 4, HD, ORF).transpose(0, 2, 1, 3).reshape(3, HD, 4 * ORF),
        "sel0": selectors(9 * FF, lambda c: c // FF),
        "sel2": selectors(8 * P, lambda c: 8 if c < 2 * P else c // (2 * P) - 1),
        "atom_b": v["L1_ffn_atom_out_b"],
        "tri": np.concatenate([np.triu(np.ones((P, P))), np.tile(np.arange(64), (P, 1))], 1).astype(np.float32),
        "route": np.array([[float(PAIRS[n][1 - r] == a) for n in range(NCLS) for r in range(2)] for a in range(ATOMS)],
                          np.float32),
    }
    return {k: np.ascontiguousarray(a) for k, a in made.items()}


def kernel(**inputs):
    import concourse.bacc as bacc
    from concourse.bass_utils import run_bass_kernel_spmd

    arrays = lay_out({k: np.asarray(a) for k, a in inputs.items()}, list(TURNS))
    nc = bacc.Bacc("TRN2", target_bir_lowering=False, num_devices=1)
    t = {k: nc.dram_tensor(k + "_dram", a.shape, mybir.dt.from_np(a.dtype), kind="ExternalInput").ap()
         for k, a in arrays.items()}
    out = nc.dram_tensor("out_dram", (P, KC, N), F32, kind="ExternalOutput").ap()
    build(nc, t, out, list(TURNS), LOOP_EVENTS)
    r = run_bass_kernel_spmd(nc, [{k + "_dram": a for k, a in arrays.items()}], core_ids=[0])
    return r.results[0]["out_dram"].transpose(1, 0, 2).reshape(D, N).T
```

```python
from contextlib import ExitStack, contextmanager

import concourse.bass as bass
import numpy as np
from concourse import mybir

F32 = mybir.dt.float32
F32R = mybir.dt.float32r
BF16 = mybir.dt.bfloat16
I32 = mybir.dt.int32
I16 = mybir.dt.int16
ALU = mybir.AluOpType
ACT = mybir.ActivationFunctionType
AX_X = mybir.AxisListType.X

P = 128
N = 512
D = 768
KC = D // P
NT = N // P
EDGES = 16384
EC = EDGES // P
HEADS = 12
HD = D // HEADS
ORF = 384
GAT = 8
C1 = D // GAT
C2 = C1 + 2
NCLS = 6
ATOMS = 5
PAIRS = [(0, 3), (0, 4), (1, 3), (1, 4), (2, 3), (2, 4)]
FF = 192
NO_EDGE = -1e30

COLUMNS = [
    ("L0_gnn_b1", 48), ("L0_gnn_b2", 6), ("L0_mix_ln1_g", 6), ("L0_mix_ln1_b", 6), ("L0_mix_qkv_b", 18),
    ("L0_mix_proj_b", 6), ("L0_mix_ln2_g", 6), ("L0_mix_ln2_b", 6), ("L0_mix_fc1_b", 24), ("L0_mix_fc2_b", 6),
    ("L1_gnn_b1", 6), ("L1_gnn_b2", 6), ("L1_mix_ln_gamma", 6), ("L1_mix_ln_beta", 6), ("L1_mix_b_proj", 6),
    ("L1_ffn_in_b", 12), ("L1_ffn_fc2_b", 6), ("L2_gnn_b", 6), ("L2_mix_bq", 6), ("L2_mix_bo", 6),
    ("L3_gnn_b", 6), ("L3_mix_qkv_b", 18), ("L3_mix_proj_b", 6), ("L3_mix_fc1_b", 24), ("L3_mix_fc2_b", 6),
    ("L3_mix_ln1_w", 6), ("L3_mix_ln1_b", 6), ("L3_mix_ln2_w", 6), ("L3_mix_ln2_b", 6),
    ("L3_ffn_b1", 16), ("L3_ffn_b2", 48), ("zero", 6),
]
COL = {}
for _name, _n in COLUMNS:
    COL[_name] = sum(n for _, n in COLUMNS[:len(COL)])
NCOL = sum(n for _, n in COLUMNS)
R0, R2, R3, GP = 0, 8, 12, 20
NSMALL = 32
ROW_L0, ROW_L0B, ROW_L1, ROW_L1B, ROW_KV0, ROW_KV1, ROW_KV2, ROW_KV3, NROWS = 0, 8, 9, 10, 11, 12, 13, 14, 15
V_GATE, V_ROUTE, V_BAL, NVEC = 0, 8, 12, 24
TURNS = dict(mix0=3 + 1 + 8, gnn0=16, ffn0=9, mix1=4, gnn1=2, ffn1=4, gnn2=1, mix2=4, ffn2=24, gnn3=1, mix3=12, ffn3=6)


class Side:

    def __init__(self, eng, name, own, events):
        self.eng, self.name, self.own, self.events = eng, name, own, events
        self.seen, self.i, self.per, self.pending = {}, None, {}, {}

    def due(self, sem, k=1):
        n = self.seen[sem.name] = self.seen.get(sem.name, 0) + k
        return n if self.i is None else self.i * self.per.get(sem.name, 0) + n

    def coming(self, sem):
        n = self.seen.get(sem.name, 0) + 1
        return n if self.i is None else self.i * self.per.get(sem.name, 0) + n

    def step(self, ins):
        ins.then_inc(self.own, 1)
        self.eng.wait_ge(self.own, self.due(self.own))

    @contextmanager
    def loop(self, what, n):
        key = f"{what}/{self.name}"
        self.per = self.events.get(key, {})
        before, held = dict(self.seen), dict(self.pending)
        with self.eng.Fori(0, n) as i:
            self.i = i
            yield i
            self.i = None
        per = {s: v - before.get(s, 0) for s, v in self.seen.items() if v != before.get(s, 0)}
        check_events(key, per, self.per)
        assert held == self.pending, (key, held, self.pending)
        for s, v in per.items():
            self.seen[s] += (n - 1) * v


def check_events(key, found, stated):
    assert found == stated, f"{key}: one iteration waits for {found}"


LOOP_EVENTS = {
    "edges/pe": {"dve_to_pe": 2},
    "performer/pe": {"dve_to_pe": 4, "act_to_pe": 4, "bank_free_by_dve7": 4, "bank_free_by_dve0": 2,
        "bank_free_by_dve1": 2, "bank_free_by_dve2": 2, "bank_free_by_dve3": 4, "w_split": 6, "bank_free_by_act3": 8,
        "bank_free_by_act4": 8, "bank_free_by_act5": 8, "bank_free_by_act6": 4},
    "mlp0/pe": {"dve_to_pe": 6, "bank_free_by_dve4": 1, "bank_free_by_dve5": 1, "bank_free_by_dve0": 1,
        "bank_free_by_dve1": 1, "bank_free_by_dve2": 1, "bank_free_by_dve3": 1, "w_split": 12,
        "bank_free_by_act3": 1, "bank_free_by_act4": 1, "bank_free_by_act5": 1, "bank_free_by_act0": 1,
        "bank_free_by_act1": 1, "bank_free_by_act2": 1},
    "performer/act": {"dve_to_act": 4, "tile_for_act": 28, "orf_in": 16, "bank_free_by_act3": 8,
        "bank_free_by_act4": 8, "bank_free_by_act5": 8, "bank_free_by_act6": 4},
    "mlp0/act": {"tile_for_act": 6, "bank_free_by_act3": 1, "bank_free_by_act4": 1, "bank_free_by_act5": 1,
        "bank_free_by_act0": 1, "bank_free_by_act1": 1, "bank_free_by_act2": 1},
    "edges/dve": {"tile_for_dve": 2},
    "performer/dve": {"dve_own": 8, "tile_for_dve": 14, "bank_free_by_dve0": 2, "bank_free_by_dve1": 2,
        "bank_free_by_dve2": 2, "bank_free_by_dve3": 4, "act_to_dve": 2, "bank_free_by_dve7": 4},
    "mlp0/dve": {"tile_for_dve": 6, "bank_free_by_dve0": 1, "bank_free_by_dve1": 1, "bank_free_by_dve2": 1,
        "bank_free_by_dve3": 1, "bank_free_by_dve4": 1, "bank_free_by_dve5": 1, "act_to_dve": 6},
    "gat0/pe": {"dve_to_pe": 13, "bank_free_by_dve4": 2, "bank_free_by_dve5": 2, "bank_free_by_dve6": 2,
        "bank_free_by_dve0": 3, "bank_free_by_dve1": 3, "bank_free_by_dve2": 2, "bank_free_by_dve3": 2,
        "w_split": 12, "bank_free_by_act3": 2, "bank_free_by_act4": 1, "bank_free_by_act5": 1,
        "bank_free_by_act0": 2, "bank_free_by_act1": 2, "bank_free_by_act2": 2},
    "gat0/act": {"dve_to_act": 17, "tile_for_act": 10, "bank_free_by_act3": 2, "bank_free_by_act4": 1,
        "bank_free_by_act5": 1, "bank_free_by_act0": 2, "bank_free_by_act1": 2, "bank_free_by_act2": 2,
        "rows_free": 1},
    "gat0/dve": {"dve_own": 16, "tile_for_dve": 16, "bank_free_by_dve0": 3, "bank_free_by_dve1": 3,
        "bank_free_by_dve2": 2, "bank_free_by_dve3": 2, "bank_free_by_dve4": 2, "bank_free_by_dve5": 2,
        "act_to_dve": 27, "bank_free_by_dve6": 2, "rows_in": 16},
    "experts0/pe": {"dve_to_pe": 7, "bank_free_by_dve4": 2, "bank_free_by_dve5": 2, "bank_free_by_dve6": 6,
        "bank_free_by_dve0": 2, "bank_free_by_dve1": 2, "bank_free_by_dve2": 2, "bank_free_by_dve3": 2,
        "w_split": 18, "bank_free_by_act3": 1, "bank_free_by_act4": 1, "bank_free_by_act5": 1,
        "bank_free_by_act0": 1, "bank_free_by_act1": 1, "bank_free_by_act2": 1},
    "experts0/act": {"dve_to_act": 6, "tile_for_act": 6, "bank_free_by_act0": 1, "bank_free_by_act1": 1,
        "bank_free_by_act2": 1, "bank_free_by_act3": 1, "bank_free_by_act4": 1, "bank_free_by_act5": 1},
    "experts0/dve": {"tile_for_dve": 18, "bank_free_by_dve0": 2, "bank_free_by_dve1": 2, "bank_free_by_dve2": 2,
        "bank_free_by_dve3": 2, "bank_free_by_dve4": 2, "bank_free_by_dve5": 2, "act_to_dve": 6,
        "bank_free_by_dve6": 6},
    "attention1/pe": {"dve_to_pe": 4, "bank_free_by_dve4": 2, "bank_free_by_dve5": 1, "bank_free_by_dve6": 1,
        "bank_free_by_dve7": 1, "bank_free_by_dve0": 1, "bank_free_by_dve1": 2, "bank_free_by_dve2": 1,
        "bank_free_by_dve3": 1, "w_split": 6, "bank_free_by_act3": 1, "bank_free_by_act0": 1},
    "gat1/pe": {"dve_to_pe": 14, "bank_free_by_dve6": 1, "bank_free_by_dve7": 1, "bank_free_by_dve0": 1,
        "bank_free_by_dve1": 1, "bank_free_by_act2": 1, "bank_free_by_act3": 1, "bank_free_by_act4": 1,
        "bank_free_by_act5": 1},
    "attention1/act": {"dve_to_act": 6, "tile_for_act": 2, "bank_free_by_act3": 1, "bank_free_by_act0": 1},
    "gat1/act": {"tile_for_act": 4, "bank_free_by_act2": 1, "bank_free_by_act3": 1, "bank_free_by_act4": 1,
        "bank_free_by_act5": 1},
    "attention1/dve": {"dve_own": 2, "tile_for_dve": 10, "bank_free_by_dve0": 1, "bank_free_by_dve1": 2,
        "bank_free_by_dve2": 1, "bank_free_by_dve3": 1, "bank_free_by_dve4": 2, "bank_free_by_dve5": 1,
        "act_to_dve": 8, "bank_free_by_dve6": 1, "bank_free_by_dve7": 1},
    "gat1/dve": {"dve_own": 22, "tile_for_dve": 4, "bank_free_by_dve0": 1, "bank_free_by_dve1": 1, "act_to_dve": 8,
        "bank_free_by_dve6": 1, "bank_free_by_dve7": 1},
    "attention2/pe": {"dve_to_pe": 4, "bank_free_by_dve4": 2, "bank_free_by_dve5": 1, "bank_free_by_dve6": 1,
        "bank_free_by_dve7": 1, "bank_free_by_dve0": 1, "bank_free_by_dve1": 2, "bank_free_by_dve2": 1,
        "bank_free_by_dve3": 1, "w_split": 6, "bank_free_by_act3": 1, "bank_free_by_act0": 1},
    "experts2/pe": {"dve_to_pe": 7, "bank_free_by_dve4": 2, "bank_free_by_dve5": 2, "bank_free_by_dve6": 1,
        "bank_free_by_dve0": 2, "bank_free_by_dve1": 2, "bank_free_by_dve2": 2, "bank_free_by_dve3": 2,
        "w_split": 18, "bank_free_by_act3": 1, "bank_free_by_act4": 1, "bank_free_by_act5": 1,
        "bank_free_by_act0": 1, "bank_free_by_act1": 1, "bank_free_by_act2": 1},
    "attention3/pe": {"dve_to_pe": 4, "bank_free_by_dve4": 2, "bank_free_by_dve5": 1, "bank_free_by_dve6": 1,
        "bank_free_by_dve7": 1, "bank_free_by_dve0": 1, "bank_free_by_dve1": 2, "bank_free_by_dve2": 1,
        "bank_free_by_dve3": 1, "w_split": 6, "bank_free_by_act3": 1, "bank_free_by_act0": 1},
    "mlp3/pe": {"dve_to_pe": 6, "bank_free_by_dve4": 1, "bank_free_by_dve5": 1, "bank_free_by_dve0": 1,
        "bank_free_by_dve1": 1, "bank_free_by_dve2": 1, "bank_free_by_dve3": 1, "w_split": 12,
        "bank_free_by_act3": 1, "bank_free_by_act4": 1, "bank_free_by_act5": 1, "bank_free_by_act0": 1,
        "bank_free_by_act1": 1, "bank_free_by_act2": 1},
    "attention2/act": {"dve_to_act": 6, "tile_for_act": 2, "bank_free_by_act3": 1, "bank_free_by_act0": 1},
    "experts2/act": {"dve_to_act": 6, "tile_for_act": 6, "bank_free_by_act3": 1, "bank_free_by_act4": 1,
        "bank_free_by_act5": 1, "bank_free_by_act0": 1, "bank_free_by_act1": 1, "bank_free_by_act2": 1},
    "attention3/act": {"dve_to_act": 6, "tile_for_act": 2, "bank_free_by_act3": 1, "bank_free_by_act0": 1},
    "mlp3/act": {"tile_for_act": 6, "bank_free_by_act3": 1, "bank_free_by_act4": 1, "bank_free_by_act5": 1,
        "bank_free_by_act0": 1, "bank_free_by_act1": 1, "bank_free_by_act2": 1},
    "attention2/dve": {"dve_own": 2, "tile_for_dve": 10, "bank_free_by_dve0": 1, "bank_free_by_dve1": 2,
        "bank_free_by_dve2": 1, "bank_free_by_dve3": 1, "bank_free_by_dve4": 2, "bank_free_by_dve5": 1,
        "act_to_dve": 8, "bank_free_by_dve6": 1, "bank_free_by_dve7": 1},
    "experts2/dve": {"tile_for_dve": 13, "bank_free_by_dve0": 2, "bank_free_by_dve1": 2, "bank_free_by_dve2": 2,
        "bank_free_by_dve3": 2, "bank_free_by_dve4": 2, "bank_free_by_dve5": 2, "act_to_dve": 6,
        "bank_free_by_dve6": 1},
    "attention3/dve": {"dve_own": 2, "tile_for_dve": 10, "bank_free_by_dve0": 1, "bank_free_by_dve1": 2,
        "bank_free_by_dve2": 1, "bank_free_by_dve3": 1, "bank_free_by_dve4": 2, "bank_free_by_dve5": 1,
        "act_to_dve": 8, "bank_free_by_dve6": 1, "bank_free_by_dve7": 1},
    "mlp3/dve": {"tile_for_dve": 6, "bank_free_by_dve0": 1, "bank_free_by_dve1": 1, "bank_free_by_dve2": 1,
        "bank_free_by_dve3": 1, "bank_free_by_dve4": 1, "bank_free_by_dve5": 1, "act_to_dve": 6},
}


def build(nc, t, out, only=None, LOOP_EVENTS={}):
    parts = [p for p in TURNS if only is None or p in only]
    turns = sum(TURNS[p] for p in parts)
    ctx = ExitStack()
    with ctx:
        def sb(name, shape, dt=F32, where=ctx):
            return where.enter_context(nc.sbuf_tensor(name, shape, dt))

        def sem(name):
            return ctx.enter_context(nc.semaphore(name))

        raw = sb("raw", [P, 2, 3, KC, P])
        w_hi = sb("w_hi", [P, 2, 3, KC, P], F32R)
        w_lo = sb("w_lo", [P, 2, 3, KC, P], F32R)
        x = sb("x", [P, KC, N])
        acc = sb("acc", [P, KC, N])
        scr = sb("scr", [P, KC, N])
        aux = sb("aux", [P, 4, N])
        with ExitStack() as s:
            A, B, H = ((sb(f"{n}_hi", [P, KC, N], F32R, s), sb(f"{n}_lo", [P, KC, N], F32R, s)) for n in "ABH")
        exp_02, head_f, exp_1 = ((sb(f"{n}_0", [P, KC, N]), sb(f"{n}_1", [P, KC, N])) for n in ("exp_02", "head_f", "exp_1"))
        row = sb("row", [P, N])
        rows = sb("rows", [P, 2, D])
        cols = sb("cols", [P, NCOL])
        small = sb("small", [P, KC, NSMALL])
        small_hi = sb("small_hi", [P, KC, NSMALL], F32R)
        small_lo = sb("small_lo", [P, KC, NSMALL], F32R)
        vecs = sb("vecs", [P, NVEC])
        counts = sb("counts", [P, NT, N], I16)
        no_edge = sb("no_edge", [P, NT, N], BF16)
        junk = sb("junk", [1, 16])
        ident = sb("ident", [P, P])
        ones = sb("ones", [P, P])
        ones_r = sb("ones_r", [P, P], F32R)
        ones_b = sb("ones_b", [P, 2], BF16)
        nv = sb("nv", [P, 16, NT])
        al = sb("al", [P, 2, NT, GAT])
        with ExitStack() as s:
            e_hi = sb("e_hi", [P, NT, N], F32R, s)
            e_lo = sb("e_lo", [P, NT, N], F32R, s)
        with ExitStack() as s:
            edge_w = [sb(f"edge_w{u}", [P, NT, N], F32, s) for u in range(2)]
        with ExitStack() as s:
            iota = sb("iota", [P, N], I16, s)
            src_i = sb("src_i", [P, EC], I32, s)
            dst_i = sb("dst_i", [P, EC], I32, s)
            src_f = sb("src_f", [P, EC], F32, s)
            dst_f = sb("dst_f", [P, EC], F32, s)
            hot = sb("hot", [P, 2, 2, N], BF16, s)
        with ExitStack() as s:
            q2 = sb("q2", [P, N], F32, s)
            k2 = sb("k2", [P, N], F32, s)
            orf = sb("orf", [P, 4, ORF], F32, s)
            k_feat = sb("k_feat", [P, NT, ORF], F32, s)
        with ExitStack() as s:
            k_n = sb("k_n", [P, 2, NT, P], F32, s)
            v_n = sb("v_n", [P, 2, NT, P + 2], F32, s)
            q_t = sb("q_t", [P, 2, N], F32, s)
            kv = sb("kv", [P, 2, P], F32, s)
            k_sum = sb("k_sum", [P, 2, P], F32, s)
            same = sb("same", [P, P], F32, s)
        with ExitStack() as s:
            gate_s = sb("gate_s", [P, 12, NT, 8], F32, s)
            comb_n = sb("comb_n", [P, NT, 16], F32, s)
            with ExitStack() as s2:
                comb_t = sb("comb_t", [16, N], F32, s2)
                sel = sb("sel", [16, 3 * D], F32, s2)
                sel_now = sb("sel_now", [16, D], F32, s2)
            with ExitStack() as s2:
                tri = sb("tri", [P, P + 64], F32, s2)
                atom_b = sb("atom_b", [ATOMS, D], F32, s2)
                route = sb("route", [ATOMS, 12], F32, s2)
                cls_w = sb("cls_w", [ATOMS, 8], F32, s2)
                rt = sb("rt", [P, 6, 32], F32, s2)
        ps = ctx.enter_context(nc.psum_tensor("ps", [P, 8, N], F32))
        scr_n = scr[:, :, :].rearrange("p k n -> p (k n)").rearrange("p (m d) -> p m d", m=NT)
        head_n = [v[:, :, :].rearrange("p k n -> p (k n)")[:, 0:2 * GAT * C2].rearrange(
            "p (m h c) -> p m h c", m=2, h=GAT) for v in head_f]

        loaded, edges_in, rows_in, orf_in, sel_in = (sem(n) for n in ("loaded", "edges_in", "rows_in", "orf_in", "sel_in"))
        setup_done = sem("setup_done")
        pool_done = sem("pool_done")
        raw_in = [sem(f"raw_in{b}") for b in range(6)]
        w_high, w_split, w_used = sem("w_high"), sem("w_split"), sem("w_used")
        tile_for = {"act": sem("tile_for_act"), "dve": sem("tile_for_dve")}
        bank_free = {r: [sem(f"bank_free_by_{r}{b}") for b in range(8)] for r in ("act", "dve")}
        act_to_dve, act_to_pe = sem("act_to_dve"), sem("act_to_pe")
        dve_to_act, dve_to_pe = sem("dve_to_act"), sem("dve_to_pe")
        rows_free, orf_free = sem("rows_free"), sem("orf_free")
        act_own, dve_own = sem("act_own"), sem("dve_own")
        stored = sem("stored")

        block = ctx.enter_context(nc.Block())
        n_setup = 7

        @block.sync
        def _(sp):
            def load(n, b):
                sp.dma_start(raw[:, b // 3, b % 3], t["stream"][bass.ds(n * 6 + b, 1)].rearrange(
                    "o p (k c) -> (o p) k c", k=KC)).then_inc(raw_in[b], 16)

            for b in range(6):
                load(0, b)
            with sp.Fori(1, turns) as i:
                for b in range(6):
                    sp.wait_ge(w_split, i * 6 + (b - 5))
                    load(i, b)

        @block.gpsimd
        def _(pool):
            pool.memset(ident[:, :], 0.0).then_inc(pool_done, 1)
            pool.wait_ge(pool_done, 1)
            pool.affine_select(out=ident[:, :], in_=ident[:, :], compare_op=ALU.not_equal, fill=1.0, base=0,
                               pattern=[[-1, P]], channel_multiplier=1).then_inc(setup_done, 1)
            pool.iota(iota[:, :], pattern=[[1, N]], base=0, channel_multiplier=0).then_inc(setup_done, 1)
            pool.memset(ones[:, :], 1.0).then_inc(setup_done, 1)
            pool.memset(ones_r[:, :].bitcast(F32), 1.0).then_inc(setup_done, 1)
            pool.memset(ones_b[:, :], 1.0).then_inc(setup_done, 1)
            pool.memset(nv[:, :, :], 0.0).then_inc(setup_done, 1)
            pool.memset(hot[:, :, :, :], 0.0).then_inc(setup_done, 1)

            def split(n, b):
                pool.wait_ge(raw_in[b], n * 16 + 16)
                pool.tensor_tensor(w_hi[:, b // 3, b % 3], raw[:, b // 3, b % 3],
                                   ones[:, :].unsqueeze(1).to_broadcast([P, KC, P]), ALU.mult).then_inc(w_high, 1)
                pool.wait_ge(w_high, n * 6 + (b + 1))
                pool.tensor_tensor(w_lo[:, b // 3, b % 3], raw[:, b // 3, b % 3], w_hi[:, b // 3, b % 3], ALU.subtract)\
                    .then_inc(w_split, 1)

            pool.wait_ge(setup_done, n_setup)
            for b in range(6):
                split(0, b)
            with pool.Fori(1, turns) as i:
                for b in range(6):
                    pool.wait_ge(w_used, i * 6 + (b - 5))
                    split(i, b)

        @block.tensor
        def _(pe):
            S = Side(pe, "pe", None, LOOP_EVENTS)
            S.pending = {}

            def use(b):
                if S.pending.get(b):
                    reader = S.pending.pop(b)
                    pe.wait_ge(bank_free[reader][b], S.due(bank_free[reader][b]))

            def done(mm, b, reader):
                mm.then_inc(tile_for[reader], 1)
                S.pending[b] = reader

            def blocks(n=1):
                pe.wait_ge(w_split, S.due(w_split, n))

            def blocks_used(n=1):
                pe.matmul(ps[0:2, 7, 0:2], ones_b[:, :], ones_b[:, :], start=True, stop=True,
                          skip_group_check=True).then_inc(w_used, n)

            def mm3(o, wh, wl, xh, xl, first, last):
                pe.matmul(o, wh, xh, start=first, stop=False, skip_group_check=True)
                pe.matmul(o, wh, xl, start=False, stop=False, skip_group_check=True)
                return pe.matmul(o, wl, xh, start=False, stop=last, skip_group_check=True)

            def tile_t(b, g, j, X, reader, chunks=range(KC), c0=0, c1=N, since=None):
                use(b)
                for n, k in enumerate(chunks):
                    if since:
                        pe.wait_ge(dve_to_pe, since[k])
                    mm = mm3(ps[:, b, c0:c1], w_hi[:, g, j, k], w_lo[:, g, j, k], X[0][:, k, c0:c1], X[1][:, k, c0:c1],
                             n == 0, n == len(chunks) - 1)
                done(mm, b, reader)

            def chunks_due():
                return [S.due(dve_to_pe) for k in range(KC)]

            def turn_t(X, reader, since=None):
                for g in range(2):
                    for j in range(3):
                        blocks()
                        tile_t(3 * g + j, g, j, X, reader, since=since if g == j == 0 else None)
                        blocks_used()

            def turn_n(X, reader, mid=None, since=None):
                for g in range(2):
                    blocks(3)
                    for m in range(NT):
                        b = (4 * g + m) % 6
                        use(b)
                        o = ps[:, b, 0:384].rearrange("p (j c) -> p j c", j=3)
                        c = slice(m * P, m * P + P)
                        for k in range(KC):
                            if since and g == m == 0:
                                pe.wait_ge(dve_to_pe, since[k])
                            mm3_ = mm3(o, X[0][:, k, c], X[1][:, k, c], w_hi[:, g, :, k], w_lo[:, g, :, k],
                                       k == 0, k == KC - 1)
                        done(mm3_, b, reader)
                        if mid:
                            mid(g, m)
                    blocks_used(3)

            def graph_t(reader):
                hn = [B[h][:, :, :].rearrange("p k n -> p (k n)").rearrange("p (m d) -> p m d", m=NT) for h in range(2)]
                for j in range(KC):
                    use(j)
                    for m in range(NT):
                        mm = mm3(ps[:, j], hn[0][:, m, j * P:j * P + P], hn[1][:, m, j * P:j * P + P],
                                 e_hi[:, m], e_lo[:, m], m == 0, m == NT - 1)
                    done(mm, j, reader)

            def norm(since=None):
                use(6)
                for j in range(KC):
                    if since:
                        pe.wait_ge(dve_to_pe, since[j])
                    elif j in S.pending:
                        pe.wait_ge(bank_free["dve"][j], S.seen.get(bank_free["dve"][j].name, 0) + 1)
                    mm = pe.matmul(ps[:, 6], ones[:, :], norm_src[0][:, j], start=j == 0, stop=j == KC - 1,
                                   skip_group_check=True)
                done(mm, 6, "dve")
                use(7)
                for j in range(KC):
                    pe.wait_ge(act_to_pe, S.due(act_to_pe))
                    mm = pe.matmul(ps[:, 7], ones[:, :], aux[:, j % 4], start=j == 0, stop=j == KC - 1,
                                   skip_group_check=True)
                    if j < 2:
                        mm.then_inc(tile_for["act"], 1)
                done(mm, 7, "dve")
                normed[:] = chunks_due()

            norm_src, normed = [x], [0] * KC

            def bcast(b, reader, block=0):
                pe.wait_ge(dve_to_pe, S.due(dve_to_pe))
                use(b)
                done(pe.matmul(ps[:, b], ones[:, :], aux[:, :, block * P:block * P + P], start=True, stop=True), b, reader)

            def gat_rows(g):
                if g == 0:
                    bcast(6, "dve")
                else:
                    bcast(2, "act")
                    bcast(3, "act", 1)

            def gat_den():
                pe.wait_ge(dve_to_pe, S.due(dve_to_pe, NT))
                use(6)
                for m in range(NT):
                    pe.matmul(ps[:, 6], ones_r[:, :], e_hi[:, m], start=m == 0, stop=False, skip_group_check=True)
                    mm = pe.matmul(ps[:, 6], ones_r[:, :], e_lo[:, m], start=False, stop=m == NT - 1,
                                   skip_group_check=True)
                done(mm, 6, "dve")

            def linear_attention(X, what):
                with S.loop(what, 3) as i:
                    for g in range(2):
                        blocks(2)
                        for m in range(NT):
                            b = 3 * g + 1 + m // 2
                            if m % 2 == 0:
                                use(b)
                            c = slice(m * P, m * P + P)
                            o = ps[:, b, (m % 2) * 256:(m % 2) * 256 + 256].rearrange("p (j c) -> p j c", j=2)
                            for k in range(KC):
                                if g == m == 0:
                                    pe.wait_ge(dve_to_pe, normed[k])
                                mm = mm3(o, X[0][:, k, c], X[1][:, k, c], w_hi[:, g, 0:2, k], w_lo[:, g, 0:2, k],
                                         k == 0, k == KC - 1)
                            if m % 2 == 1:
                                done(mm, b, "dve")
                        blocks_used(2)
                        blocks()
                        tile_t(3 * g, g, 2, X, "act")
                        blocks_used()
                    for g in range(2):
                        pe.wait_ge(dve_to_pe, S.due(dve_to_pe))
                        use(6 + g)
                        for m in range(NT):
                            mm = pe.matmul(ps[:, 6 + g, 0:P + 2], k_n[:, g, m], v_n[:, g, m], start=m == 0, stop=m == NT - 1,
                                           skip_group_check=True)
                        done(mm, 6 + g, "dve")
                    for g in range(2):
                        pe.wait_ge(bank_free["dve"][6 + g], S.coming(bank_free["dve"][6 + g]))
                        use(3 * g)
                        done(pe.matmul(ps[:, 3 * g], kv[:, g], q_t[:, g], start=True, stop=True), 3 * g, "dve")
                        use(3 * g + 1)
                        done(pe.matmul(ps[:, 3 * g + 1], k_sum[:, g], q_t[:, g], start=True, stop=True), 3 * g + 1, "dve")
                    S.due(dve_to_pe, 2)
                n = S.seen[dve_to_pe.name]
                return [n - 4] * 4 + [n - 1, n]

            def performer(X, what):
                with S.loop(what, 3) as i:
                    for g in range(2):
                        blocks()
                        tile_t(0, g, 0, X, "dve", since=normed if g == 0 else None)
                        blocks_used()
                        blocks()
                        tile_t(1, g, 1, X, "dve")
                        blocks_used()
                        blocks()
                        use(2)
                        for m in range(NT):
                            c = slice(m * P, m * P + P)
                            for k in range(KC):
                                mm = mm3(ps[:, 2, c], X[0][:, k, c], X[1][:, k, c], w_hi[:, g, 2, k], w_lo[:, g, 2, k],
                                         k == 0, k == KC - 1)
                        done(mm, 2, "dve")
                        blocks_used()
                        pe.wait_ge(dve_to_pe, S.due(dve_to_pe))
                        for h in range(2):
                            w = orf[:, 2 * g + h]
                            pe.wait_ge(act_to_pe, S.due(act_to_pe))
                            for m in range(NT):
                                use(3 + m % 2)
                                done(pe.matmul(ps[:, 3 + m % 2, 0:ORF], k2[:, m * P:m * P + P], w, start=True, stop=True),
                                     3 + m % 2, "act")
                            for r in range(3):
                                use(5 + r % 2)
                                done(pe.matmul(ps[:, 5 + r % 2], w[:, r * P:r * P + P], q2[:, :], start=True, stop=True),
                                     5 + r % 2, "act")
                            for b in (3, 4, 5, 6, 7):
                                use(b)
                            vh = aux[:, 0:2].rearrange("p a n -> p (a n)")[:, 0:NT * 2 * 66].rearrange(
                                "p (m h c) -> p m h c", m=NT, h=2)
                            for r in range(3):
                                for m in range(NT):
                                    mm = pe.matmul(ps[:, 7, r * 68:r * 68 + 66], k_feat[:, m, r * P:r * P + P],
                                                   vh[:, m, h], start=m == 0, stop=m == NT - 1, skip_group_check=True)
                            done(mm, 7, "dve")
                            use(7)
                            ktv = aux[:, 2, 0:ORF].rearrange("p (r c) -> p r c", r=3)
                            use(3)
                            for r in range(3):
                                mm = pe.matmul(ps[:, 3], ktv[:, r], scr[:, 3 + r], start=r == 0, stop=r == 2,
                                               skip_group_check=True)
                            done(mm, 3, "dve")
                        pe.wait_ge(dve_to_pe, S.due(dve_to_pe))
                    unpend()

            def gelu_mlp(X, what):
                with S.loop(what, 4) as i:
                    turn_t(X, "act", normed)
                    turn_t(H, "dve", chunks_due())

            def router_n(X, c0, n):
                use(6)
                for m in range(NT):
                    for k in range(KC):
                        if m == 0:
                            pe.wait_ge(dve_to_pe, normed[k])
                        c = slice(m * P, m * P + P)
                        mm = mm3(ps[:, 6, m * 8:m * 8 + n], X[0][:, k, c], X[1][:, k, c], small_hi[:, k, c0:c0 + n],
                                 small_lo[:, k, c0:c0 + n], k == 0, k == KC - 1)
                done(mm, 6, "dve")

            def combine_rows():
                pe.wait_ge(dve_to_pe, S.due(dve_to_pe))
                use(6)
                for m in range(NT):
                    mm = pe.transpose(ps[0:16, 6, m * P:m * P + P], comb_n[:, m], ident[:, :])
                done(mm, 6, "dve")

            def experts(X, what, n, per_chunk):
                with S.loop(what, n) as i:
                    turn_t(X, "act", normed)
                    pe.wait_ge(dve_to_pe, S.due(dve_to_pe))
                    if not per_chunk:
                        use(6)
                        done(pe.matmul(ps[:, 6], sel_now[:, 0:P], comb_t[:, :], start=True, stop=True), 6, "dve")
                    for g in range(2):
                        for j in range(3):
                            blocks()
                            f = 3 * g + j
                            if per_chunk:
                                use(6)
                                done(pe.matmul(ps[:, 6], sel_now[:, f * P:f * P + P], comb_t[:, :], start=True, stop=True),
                                     6, "dve")
                            tile_t(f, g, j, X, "dve")
                            blocks_used()
                    turn_t(H, "dve", chunks_due())

            def transposes(src, reader, dst_tile_free=True):
                for j in range(KC):
                    use(j)
                    for m in range(NT):
                        mm = pe.transpose(ps[:, j, m * P:m * P + P], src(m, j), ident[:, :])
                    done(mm, j, reader)

            def degrees():
                pe.wait_ge(dve_to_pe, S.due(dve_to_pe))
                use(6)
                for m in range(NT):
                    mm = pe.matmul(ps[:, 6], ones[:, :], aux[:, m], start=m == 0, stop=m == NT - 1, skip_group_check=True)
                done(mm, 6, "dve")

            def to_nodes(src):
                for g in range(2):
                    for m in range(NT):
                        b = (4 * g + m) % 6
                        use(b)
                        for c in range(3):
                            mm = pe.transpose(ps[:, b, c * P:c * P + P], src[:, 3 * g + c, m * P:m * P + P], ident[:, :])
                        done(mm, b, "act")
                        S.pending[b] = "dve"

            pe.wait_ge(setup_done, n_setup)
            for m in range(NT):
                mm = pe.matmul(ps[:, m], hot[:, 1, 0, 0:P], hot[:, 1, 0, :], start=True, stop=False, skip_group_check=True)
                if m >= 2:
                    mm.then_inc(tile_for["dve"], 1)
            with S.loop("edges", EC // 2) as i:
                for c in range(2):
                    pe.wait_ge(dve_to_pe, S.due(dve_to_pe))
                    for m in range(NT):
                        mm = pe.matmul(ps[:, m], hot[:, c, 0, m * P:m * P + P], hot[:, c, 1, :], start=False, stop=False,
                                       skip_group_check=True)
                    mm.then_inc(tile_for["dve"], 1)
            for m in range(NT):
                S.pending[m] = "dve"
            pe.wait_ge(dve_to_pe, S.due(dve_to_pe, NT))
            for m in range(NT):
                use(4 + m % 2)
                for k in range(NT):
                    mm = pe.transpose(ps[:, 4 + m % 2, k * P:k * P + P], aux[:, k, m * P:m * P + P], ident[:, :])
                done(mm, 4 + m % 2, "dve")

            def unpend():
                for b in list(S.pending):
                    use(b)

            def part(p):
                return p in parts

            def norm_of(src, since=None):
                norm_src[0] = src
                norm(since)

            ran = lambda p: p in parts
            pe.wait_ge(loaded, 64)
            norm_of(x)
            if part("mix0"):
                norm_of(acc, list(normed))
                unpend()
                performer(B, "performer")
                unpend()
                turn_t(H, "dve")
                norm_of(acc)
                gelu_mlp(B, "mlp0")
            if part("gnn0"):
                turn_n(A, "act", since=normed)
                gat_rows(0)
                gat_rows(1)
                gat_den()
                graph_t("dve")
                unpend()
                with S.loop("gat0", GAT - 1) as i:
                    head = chunks_due()
                    turn_n(A, "act")
                    turn_n(H, "dve", lambda g, m: gat_rows(g) if (g, m) in ((0, 3), (1, 1)) else None, head)
                    gat_den()
                    graph_t("dve")
                    unpend()
                turn_n(H, "dve", since=chunks_due())
                gat_rows(0)
                gat_rows(1)
                gat_den()
                graph_t("dve")
            if part("ffn0"):
                norm_of(x)
                router_n(A, R0, 8)
                combine_rows()
                experts(A, "experts0", 3, True)
            if ran("mix1") or ran("gnn1"):
                norm_of(x)
            if part("mix1"):
                norm_of(acc, list(normed))
                turn_t(H, "dve", linear_attention(B, "attention1"))
            if part("gnn1"):
                turn_n(A, "act", since=normed)
                pe.wait_ge(dve_to_pe, S.due(dve_to_pe))
                unpend()
                with S.loop("gat1", GAT // 2) as i:
                    for u in range(2):
                        bcast(6 + u, "dve", 2 * u)
                    for u in range(2):
                        for r in range(2):
                            bcast(2 + 2 * u + r, "act", 2 * u + r)
                    for u in range(2):
                        use(u)
                        for k in range(NT):
                            pe.wait_ge(dve_to_pe, S.due(dve_to_pe))
                        for m in range(NT):
                            for k in range(NT):
                                mm = pe.matmul(ps[:, u, m * P:m * P + C2], edge_w[u][:, k, m * P:m * P + P],
                                               head_n[k // 2][:, k % 2, bass.ds(i * 2 + u, 1)].rearrange("p o c -> p (o c)"),
                                               start=k == 0, stop=k == NT - 1, skip_group_check=True)
                        done(mm, u, "dve")
                    unpend()
                pe.wait_ge(dve_to_pe, S.due(dve_to_pe))
                acc_n = acc[:, :, :].rearrange("p k n -> p (k n)").rearrange("p (m d) -> p m d", m=NT)
                transposes(lambda m, j: acc_n[:, m, j * P:j * P + P], "act")
                turn_n(H, "act", since=chunks_due())
                gat_rows(0)
                gat_rows(1)
                gat_den()
                graph_t("dve")
            if part("ffn1"):
                norm_of(x)
                unpend()
                pe.wait_ge(dve_to_pe, S.due(dve_to_pe))
                for k in range(KC):
                    mm = pe.matmul(ps[:, 6, 0:30], ones[:, :], aux[:, k % 4, (k // 4) * 32:(k // 4) * 32 + 30],
                                   start=k == 0, stop=k == KC - 1, skip_group_check=True)
                done(mm, 6, "dve")
                for n in range(2):
                    for g in range(2):
                        for j in range(3):
                            blocks()
                            q = 6 * n + 3 * g + j
                            tile_t(q % 6, g, j, A, "act", c1=N if q < 2 else 8, since=normed if q == 0 else None)
                            blocks_used()
                pe.wait_ge(dve_to_pe, S.due(dve_to_pe, 3))
                for n in range(2):
                    for g in range(2):
                        for j in range(3):
                            blocks()
                            f = 3 * g + j
                            if n == 0:
                                tile_t(f, g, j, H, "dve", chunks=range(2))
                            if n == 0 and f == 0:
                                use(6)
                            for k in range(2, KC) if n == 0 else range(KC):
                                mm = mm3(ps[:, 6, (6 * n + f) * 8:(6 * n + f) * 8 + 8], w_hi[:, g, j, k], w_lo[:, g, j, k],
                                         H[0][:, 2, (6 * n + k) * 8 - 16:(6 * n + k) * 8 - 8],
                                         H[1][:, 2, (6 * n + k) * 8 - 16:(6 * n + k) * 8 - 8], k == (2 if n == 0 else 0), k == KC - 1)
                            blocks_used()
                for f in range(KC):
                    mm = pe.matmul(ps[:, 6, 96 + f * 8:104 + f * 8], atom_b[:, f * P:f * P + P], cls_w[:, :], start=True,
                                   stop=True, skip_group_check=True)
                done(mm, 6, "dve")
            if ran("gnn2") or ran("mix2"):
                norm_of(x)
            if part("gnn2"):
                degrees()
                turn_n(A, "act", since=normed)
                pe.wait_ge(dve_to_pe, S.due(dve_to_pe))
                graph_t("dve")
            if part("mix2"):
                turn_t(H, "dve", linear_attention(A, "attention2"))
            if part("ffn2"):
                norm_of(x)
                router_n(A, R2, 4)
                combine_rows()
                experts(A, "experts2", 8, False)
            if ran("gnn3") or ran("mix3"):
                norm_of(x)
            if part("gnn3"):
                degrees()
                turn_n(A, "act", since=normed)
                pe.wait_ge(dve_to_pe, S.due(dve_to_pe))
                graph_t("dve")
            if part("mix3"):
                norm_of(acc, list(normed))
                turn_t(H, "dve", linear_attention(B, "attention3"))
                norm_of(acc)
                gelu_mlp(B, "mlp3")
            if part("ffn3"):
                norm_of(x)
                router_n(A, R3, 8)
                to_nodes(acc)
                pe.wait_ge(dve_to_pe, S.due(dve_to_pe))
                use(6)
                for m in range(NT):
                    for k in range(m + 1):
                        mm = pe.matmul(ps[:, 6, m * 8:m * 8 + 8], tri[:, 0:P] if k == m else ones[:, :], gate_s[:, 7, k],
                                       start=k == 0, stop=k == m, skip_group_check=True)
                done(mm, 6, "dve")
                pe.wait_ge(dve_to_pe, S.due(dve_to_pe))
                for j in range(KC):
                    use(j)
                    for h in range(2):
                        bn = B[h][:, :, :].rearrange("p k n -> p (k n)").rearrange("p (m d) -> p m d", m=NT)
                        for m in range(NT):
                            mm = pe.matmul(ps[:, j], bn[:, m, j * P:j * P + P], e_hi[:, m], start=h == 0 and m == 0,
                                           stop=h == 1 and m == NT - 1, skip_group_check=True)
                    done(mm, j, "act")
                pe.wait_ge(dve_to_pe, S.due(dve_to_pe, KC))
                for n in range(3):
                    for g in range(2):
                        for j in range(3):
                            blocks()
                            q = 6 * n + 3 * g + j
                            if q < 16:
                                tile_t(q % 6, g, j, A, "act", c0=64 * (q // 2), c1=64 * (q // 2) + 64)
                            blocks_used()
                pe.wait_ge(dve_to_pe, S.due(dve_to_pe, 16))
                for n in range(3):
                    for g in range(2):
                        for j in range(3):
                            blocks()
                            f = 3 * g + j
                            use(f)
                            for e in range(3 * n, min(3 * n + 3, 8)):
                                for h in range(2):
                                    k, q = 2 * (e - 3 * n) + h, 2 * e + h
                                    c = slice(q % 8 * 64, q % 8 * 64 + 64)
                                    mm = mm3(ps[:, f, e * 64:e * 64 + 64], w_hi[:, g, j, k], w_lo[:, g, j, k],
                                             H[0][:, q // 8, c], H[1][:, q // 8, c], h == 0, h == 1)
                            done(mm, f, "act")
                            blocks_used()
                for m in range(NT):
                    use(m)
                    for k in range(NT):
                        mm = pe.transpose(ps[:, m, k * P:k * P + P], aux[:, k, m * P:m * P + P], ident[:, :])
                    done(mm, m, "act")
                    S.pending[m] = "dve"
                pe.wait_ge(act_to_pe, S.due(act_to_pe))
                to_nodes(scr)
                pe.wait_ge(dve_to_pe, S.due(dve_to_pe))
                graph_t("dve")

        @block.scalar
        def _(act):
            S = Side(act, "act", act_own, LOOP_EVENTS)
            first_rows = [True]
            marks = [0]

            def freed(ins, b):
                ins.then_inc(bank_free["act"][b], 1)
                act.wait_ge(bank_free["act"][b], S.due(bank_free["act"][b]))

            def mark(sem):
                marks[0] = (marks[0] + 1) % 7
                act.activation(junk[:, marks[0]:marks[0] + 1], ones[0:1, 0:1], ACT.Copy).then_inc(sem, 1)

            def load_rows(n):
                if not first_rows[0]:
                    act.wait_ge(rows_free, S.due(rows_free))
                first_rows[0] = False
                n = bass.ds(n, 1)
                act.dma_start(rows[:, :, :], t["rows"][n].rearrange("o a d -> (o a) d").partition_broadcast(P))\
                   .then_inc(rows_in, 16)

            def col(name, n=0):
                c = COL[name] + n
                return cols[:, c:c + 1] if isinstance(c, int) else cols[:, bass.ds(c, 1)]

            def high(dst, src):
                act.wait_ge(dve_to_act, S.due(dve_to_act))
                act.copy(dst, src).then_inc(act_to_dve, 1)

            def norm(src, dst, X):
                for j in range(KC):
                    act.wait_ge(dve_to_act, S.due(dve_to_act))
                    if j >= 4:
                        act.wait_ge(tile_for["act"], S.due(tile_for["act"]))
                    act.activation(aux[:, j % 4], scr[:, j], ACT.Square).then_inc(act_to_pe, 1)
                act.wait_ge(dve_to_act, S.due(dve_to_act))
                act.activation(row[:, :], row[:, :], ACT.Sqrt).then_inc(act_to_dve, 1)
                for j in range(KC):
                    high(X[0][:, j], dst[:, j])

            def features_n():
                sn = scr[:, :, :].rearrange("p k n -> p (k n)").rearrange("p (m d) -> p m d", m=NT)
                bn = B[0][:, :, :].rearrange("p k n -> p (k n)").rearrange("p (m d) -> p m d", m=NT)
                for g in range(2):
                    for m in range(NT):
                        c = slice(384 * g, 384 * g + 384)
                        b = (4 * g + m) % 6
                        act.wait_ge(tile_for["act"], S.due(tile_for["act"]))
                        freed(act.copy(sn[:, m, c], ps[:, b, 0:384]), b)
                        act.copy(bn[:, m, c], sn[:, m, c]).then_inc(act_to_dve, 1)

            def edge_weights():
                act.wait_ge(tile_for["act"], S.due(tile_for["act"], 2))
                for m in range(NT):
                    q = 2 * (m % 2)
                    e1 = act.activation(aux[:, q], ps[:, 2], ACT.Exp, bias=nv[:, 0, m:m + 1])
                    if m == NT - 1:
                        freed(e1, 2)
                    e2 = act.activation(aux[:, q + 1], ps[:, 3], ACT.Exp, bias=nv[:, 3, m:m + 1])
                    if m < NT - 1:
                        e2.then_inc(act_to_dve, 1)
                    else:
                        freed(e2, 3)
                    if m >= 1:
                        high(e_hi[:, m - 1], scr[:, m - 1])
                high(e_hi[:, NT - 1], scr[:, NT - 1])

            def head_output(bias, from_psum=False):
                for s in range(KC + 1):
                    if s < KC:
                        q = 2 * (s % 2)
                        if from_psum:
                            act.wait_ge(tile_for["act"], S.due(tile_for["act"]))
                            src = ps[:, s]
                        else:
                            act.wait_ge(dve_to_act, S.due(dve_to_act))
                            src = scr[:, s]
                        act.activation(aux[:, q], src, ACT.Exp, bias=bias(s))
                        r = act.activation(aux[:, q + 1], src, ACT.Relu, bias=bias(s))
                        if from_psum:
                            freed(r, s)
                            mark(act_to_dve)
                        else:
                            r.then_inc(act_to_dve, 1)
                    if s >= 1:
                        act.wait_ge(dve_to_act, S.due(dve_to_act))
                        act.activation(H[0][:, s - 1], scr[:, s - 1], ACT.Identity, bias=-1.0).then_inc(act_to_dve, 1)

            def performer(what):
                with S.loop(what, 3) as i:
                    act.dma_start(orf[0:HD, :, :], t["orf"][bass.ds(i, 1)].rearrange("o c (h r) -> (o c) h r", h=4))\
                       .then_inc(orf_in, 16)
                    act.wait_ge(orf_in, S.due(orf_in, 16))
                    for g in range(2):
                        act.wait_ge(dve_to_act, S.due(dve_to_act))
                        for h in range(2):
                            r = slice(h * HD, h * HD + HD)
                            act.copy(q2[0:HD, :], scr[r, 0])
                            act.activation(q2[HD:P, :], scr[r, 0], ACT.Square)
                            act.copy(k2[0:HD, :], scr[r, 1])
                            act.activation(k2[HD:P, :], scr[r, 1], ACT.Square).then_inc(act_to_pe, 1)
                            for m in range(NT):
                                act.wait_ge(tile_for["act"], S.due(tile_for["act"]))
                                freed(act.activation(k_feat[:, m], ps[:, 3 + m % 2, 0:ORF], ACT.Exp), 3 + m % 2)
                            for m in range(3):
                                act.wait_ge(tile_for["act"], S.due(tile_for["act"]))
                                freed(act.activation(scr[:, 3 + m], ps[:, 5 + m % 2], ACT.Exp), 5 + m % 2)
                        high(H[0][:, bass.ds(2 * i + g, 1)].rearrange("p o n -> p (o n)"), aux[:, 3])

            def linear_attention(what, bq):
                with S.loop(what, 3) as i:
                    for g in range(2):
                        for half in range(2):
                            act.wait_ge(dve_to_act, S.due(dve_to_act))
                            act.activation(scr[:, 2 + half, 0:256], aux[:, half, 0:256], ACT.Exp)
                            act.activation(scr[:, 2 + half, 256:512], aux[:, half, 0:256], ACT.Relu)\
                               .then_inc(act_to_dve, 1)
                        b = col(bq, i * 2 + g)
                        act.wait_ge(tile_for["act"], S.due(tile_for["act"]))
                        act.activation(scr[:, 0], ps[:, 3 * g], ACT.Exp, bias=b)
                        freed(act.activation(scr[:, 1], ps[:, 3 * g], ACT.Relu, bias=b), 3 * g)
                        mark(act_to_dve)
                    for g in range(2):
                        high(H[0][:, bass.ds(2 * i + g, 1)].rearrange("p o n -> p (o n)"), aux[:, 2 + g])

            def gelu_mlp(what, bias, func):
                with S.loop(what, 4) as i:
                    for j in range(KC):
                        act.wait_ge(tile_for["act"], S.due(tile_for["act"]))
                        freed(act.activation(scr[:, j], ps[:, j], func, bias=col(bias, i * KC + j)), j)
                        act.copy(H[0][:, j], scr[:, j]).then_inc(act_to_dve, 1)

            def experts(what, n):
                with S.loop(what, n) as i:
                    for j in range(KC):
                        act.wait_ge(tile_for["act"], S.due(tile_for["act"]))
                        freed(act.activation(scr[:, j], ps[:, j], ACT.Silu), j)
                    for j in range(KC):
                        high(H[0][:, j], scr[:, j])

            def router_exp():
                act.wait_ge(dve_to_act, S.due(dve_to_act))
                act.activation(gate_s[:, 1], gate_s[:, 0], ACT.Exp).then_inc(act_to_dve, 1)

            act.dma_start(src_i[:, :], t["src"]).then_inc(edges_in, 16)
            act.dma_start(dst_i[:, :], t["dst"]).then_inc(edges_in, 16)
            act.dma_start(x[:, :, :], t["x"]).then_inc(loaded, 16)
            act.dma_start(cols[:, :], t["cols"]).then_inc(loaded, 16)
            act.dma_start(small[:, :, :], t["small"]).then_inc(loaded, 16)
            act.dma_start(vecs[:, :], t["vecs"].partition_broadcast(P)).then_inc(loaded, 16)
            act.wait_ge(loaded, 64)
            act.wait_ge(setup_done, n_setup)
            S.step(act.copy(small_hi[:, :, :], small[:, :, :]))
            mark(act_to_dve)
            norm(x, acc, A)
            if "mix0" in parts:
                load_rows(ROW_KV0)
                norm(acc, scr, B)
                performer("performer")
                norm(acc, scr, B)
                gelu_mlp("mlp0", "L0_mix_fc1_b", ACT.Gelu_apprx_tanh)
            if "gnn0" in parts:
                load_rows(0)
                features_n()
                edge_weights()
                head_output(lambda j: col("L0_gnn_b1", j))
                with S.loop("gat0", GAT - 1) as i:
                    load_rows(i + 1)
                    act.wait_ge(dve_to_act, S.due(dve_to_act))
                    features_n()
                    edge_weights()
                    head_output(lambda j: col("L0_gnn_b1", i * KC + KC + j))
                load_rows(ROW_L0B)
                act.wait_ge(dve_to_act, S.due(dve_to_act))
                an = acc[:, :, :].rearrange("p k n -> p (k n)").rearrange("p (m d) -> p m d", m=NT)
                bn = B[0][:, :, :].rearrange("p k n -> p (k n)").rearrange("p (m d) -> p m d", m=NT)
                for m in range(NT):
                    act.copy(bn[:, m], an[:, m]).then_inc(act_to_dve, 1)
                edge_weights()
            if "ffn0" in parts:
                norm(x, acc, A)
                act.wait_ge(dve_to_act, S.due(dve_to_act))
                act.activation(gate_s[:, 2], gate_s[:, 1], ACT.Exp, scale=-1.0).then_inc(act_to_dve, 1)
                act.wait_ge(dve_to_act, S.due(dve_to_act))
                S.step(act.activation(gate_s[:, 4], gate_s[:, 3], ACT.Ln))
                mark(act_to_dve)
                act.wait_ge(dve_to_act, S.due(dve_to_act))
                act.activation(gate_s[:, 6], gate_s[:, 5], ACT.Sqrt).then_inc(act_to_dve, 1)
                act.dma_start(sel[0:16, :], t["sel0"]).then_inc(sel_in, 16)
                experts("experts0", 3)

            if "mix1" in parts or "gnn1" in parts:
                norm(x, acc, A)
            if "mix1" in parts:
                load_rows(ROW_KV1)
                norm(acc, scr, B)
                linear_attention("attention1", "zero")
            if "gnn1" in parts:
                load_rows(ROW_L1)
                act.wait_ge(dve_to_act, S.due(dve_to_act))
                for g in range(2):
                    for m in range(NT):
                        b = (4 * g + m) % 6
                        act.wait_ge(tile_for["act"], S.due(tile_for["act"]))
                        freed(act.copy(head_n[m // 2][:, m % 2, 4 * g:4 * g + 4, 0:C1],
                                       ps[:, b, 0:384].rearrange("p (h c) -> p h c", h=4)), b)
                        mark(act_to_dve)
                with S.loop("gat1", GAT // 2) as i:
                    for u in range(2):
                        act.wait_ge(tile_for["act"], S.due(tile_for["act"], 2))
                        for m in range(NT):
                            e1 = act.activation(exp_1[u][:, m], ps[:, 2 + 2 * u], ACT.Exp, bias=nv[:, 8 * u, m:m + 1])
                            e2 = act.activation(exp_02[u][:, m], ps[:, 3 + 2 * u], ACT.Exp, bias=nv[:, 8 * u + 3, m:m + 1])
                            if m < NT - 1:
                                e2.then_inc(act_to_dve, 1)
                        e1.then_inc(bank_free["act"][2 + 2 * u], 1)
                        freed(e2, 3 + 2 * u)
                        act.wait_ge(bank_free["act"][2 + 2 * u], S.due(bank_free["act"][2 + 2 * u]))
                        mark(act_to_dve)
                head_output(lambda j: col("L1_gnn_b1", j), True)
                load_rows(ROW_L1B)
                act.wait_ge(dve_to_act, S.due(dve_to_act))
                features_n()
                edge_weights()
            if "ffn1" in parts:
                norm(x, acc, A)
                act.dma_start(atom_b[:, :], t["atom_b"]).then_inc(sel_in, 16)
                act.dma_start(route[:, :], t["route"]).then_inc(sel_in, 16)
                act.wait_ge(dve_to_act, S.due(dve_to_act))
                act.activation(rt[:, 1, 12:30], rt[:, 0, 12:30], ACT.Sqrt).then_inc(act_to_dve, 1)
                act.wait_ge(dve_to_act, S.due(dve_to_act))
                act.activation(rt[:, 3, 0:6], rt[:, 2, 0:6], ACT.Exp).then_inc(act_to_dve, 1)
                for q in range(12):
                    act.wait_ge(tile_for["act"], S.due(tile_for["act"]))
                    b = col("L1_ffn_in_b", q)
                    if q < 2:
                        freed(act.activation(scr[:, q], ps[:, q], ACT.Gelu, bias=b), q)
                        act.copy(H[0][:, q], scr[:, q]).then_inc(act_to_dve, 1)
                    else:
                        freed(act.activation(scr[:, 2, q * 8 - 16:q * 8 - 8], ps[:, q % 6, 0:8], ACT.Gelu, bias=b), q % 6)
                mark(act_to_dve)
                high(H[0][:, 2, 0:80], scr[:, 3, 0:80])

            def gcn():
                act.wait_ge(dve_to_act, S.due(dve_to_act))
                act.activation(row[:, :], row[:, :], ACT.Sqrt).then_inc(act_to_dve, 1)
                for m in range(NT):
                    high(e_hi[:, m], scr[:, m])
                act.wait_ge(dve_to_act, S.due(dve_to_act))
                features_n()

            if "gnn2" in parts or "mix2" in parts:
                norm(x, acc, A)
            if "gnn2" in parts:
                gcn()
            if "mix2" in parts:
                load_rows(ROW_KV2)
                linear_attention("attention2", "L2_mix_bq")
            if "ffn2" in parts:
                norm(x, acc, A)
                act.wait_ge(dve_to_act, S.due(dve_to_act))
                act.activation(gate_s[:, 2, :, 0:3], gate_s[:, 1, :, 0:3], ACT.Exp, scale=-1.0).then_inc(act_to_dve, 1)
                act.dma_start(sel[0:16, :], t["sel2"]).then_inc(sel_in, 16)
                experts("experts2", 8)
            if "gnn3" in parts or "mix3" in parts:
                norm(x, acc, A)
            if "gnn3" in parts:
                gcn()
            if "mix3" in parts:
                load_rows(ROW_KV3)
                norm(acc, scr, B)
                linear_attention("attention3", "L3_mix_qkv_b")
                norm(acc, scr, B)
                gelu_mlp("mlp3", "L3_mix_fc1_b", ACT.Gelu)
            if "ffn3" in parts:
                def nodes_high():
                    bn = B[0][:, :, :].rearrange("p k n -> p (k n)").rearrange("p (m d) -> p m d", m=NT)
                    for g in range(2):
                        for m in range(NT):
                            act.wait_ge(tile_for["act"], S.due(tile_for["act"]))
                            act.copy(bn[:, m, 384 * g:384 * g + 384], ps[:, (4 * g + m) % 6, 0:384])\
                               .then_inc(act_to_dve, 1)

                norm(x, acc, A)
                act.dma_start(tri[:, :], t["tri"]).then_inc(sel_in, 16)
                act.wait_ge(dve_to_act, S.due(dve_to_act))
                act.activation(gate_s[:, 2], gate_s[:, 1], ACT.Exp).then_inc(act_to_dve, 1)
                nodes_high()
                for j in range(KC):
                    act.wait_ge(tile_for["act"], S.due(tile_for["act"]))
                    freed(act.copy(scr[:, j], ps[:, j]), j)
                    act.copy(A[0][:, j], scr[:, j]).then_inc(act_to_dve, 1)
                for q in range(16):
                    act.wait_ge(tile_for["act"], S.due(tile_for["act"]))
                    if q == 0:
                        act.wait_ge(dve_to_act, S.due(dve_to_act))
                    c, c0 = slice(q % 8 * 64, q % 8 * 64 + 64), 64 * (q // 2)
                    freed(act.activation(scr[:, q // 8, c], ps[:, q % 6, c0:c0 + 64], ACT.Gelu_apprx_tanh,
                                         bias=col("L3_ffn_b1", q)), q % 6)
                    act.copy(H[0][:, q // 8, c], scr[:, q // 8, c]).then_inc(act_to_dve, 1)
                for n in range(3):
                    for f in range(KC):
                        act.wait_ge(tile_for["act"], S.due(tile_for["act"]))
                        for e in range(3 * n, min(3 * n + 3, 8)):
                            c = slice(e * 64, e * 64 + 64)
                            ins = act.activation(scr[:, f, c], ps[:, f, c], ACT.Gelu_apprx_tanh, bias=col("L3_ffn_b2", e * KC + f))
                        freed(ins, f)
                mark(act_to_pe)
                for m in range(NT):
                    act.wait_ge(tile_for["act"], S.due(tile_for["act"]))
                    act.copy(e_hi[:, m], ps[:, m]).then_inc(act_to_dve, 1)
                nodes_high()
            act.wait_ge(dve_to_act, S.due(dve_to_act))
            act.dma_start(out, x[:, :, :]).then_inc(stored, 16)
            act.wait_ge(stored, 16)

        @block.vector
        def _(dve):
            S = Side(dve, "dve", dve_own, LOOP_EVENTS)
            A_hi, A_lo = A
            eps_inv = 1.0 / D
            marks = [0]

            def freed(ins, b):
                ins.then_inc(bank_free["dve"][b], 1)
                dve.wait_ge(bank_free["dve"][b], S.due(bank_free["dve"][b]))

            def mark(sem):
                marks[0] = (marks[0] + 1) % 7
                dve.memset(junk[:, 8 + marks[0]:9 + marks[0]], 0.0).then_inc(sem, 1)

            def col(name, n=0):
                c = COL[name] + n
                return cols[:, c:c + 1] if isinstance(c, int) else cols[:, bass.ds(c, 1)]

            def low(X, j, v):
                dve.wait_ge(act_to_dve, S.due(act_to_dve))
                dve.tensor_tensor(X[1][:, j], v, X[0][:, j], ALU.subtract).then_inc(dve_to_pe, 1)

            def norm(src, dst, X, eps, gamma=None, beta=None):
                dve.wait_ge(tile_for["dve"], S.due(tile_for["dve"]))
                freed(dve.tensor_scalar(row[:, :], ps[:, 6], -eps_inv, None, ALU.mult), 6)
                for j in range(KC):
                    dve.tensor_tensor(scr[:, j], src[:, j], row[:, :], ALU.add).then_inc(dve_to_act, 1)
                dve.wait_ge(tile_for["dve"], S.due(tile_for["dve"]))
                freed(dve.tensor_scalar(row[:, :], ps[:, 7], eps_inv, eps, ALU.mult, ALU.add), 7)
                mark(dve_to_act)
                dve.wait_ge(act_to_dve, S.due(act_to_dve))
                S.step(dve.reciprocal(row[:, :], row[:, :]))
                for j in range(KC):
                    y = dve.tensor_tensor(dst[:, j], scr[:, j], row[:, :], ALU.mult)
                    if gamma:
                        S.step(y)
                        y = dve.tensor_scalar(dst[:, j], dst[:, j], col(gamma, j), col(beta, j), ALU.mult, ALU.add)
                    y.then_inc(dve_to_act, 1)
                    if j >= 1:
                        low(X, j - 1, dst[:, j - 1])
                low(X, KC - 1, dst[:, KC - 1])

            sn = scr[:, :, :].rearrange("p k n -> p (k n)").rearrange("p (m d) -> p m d", m=NT)
            accn = acc[:, :, :].rearrange("p k n -> p (k n)").rearrange("p (m d) -> p m d", m=NT)
            bn = [B[h][:, :, :].rearrange("p k n -> p (k n)").rearrange("p (m d) -> p m d", m=NT) for h in range(2)]
            flat = aux[:, :, :].rearrange("p a n -> p (a n)")

            def features_n():
                for g in range(2):
                    for m in range(NT):
                        c = slice(384 * g, 384 * g + 384)
                        dve.wait_ge(act_to_dve, S.due(act_to_dve))
                        ins = dve.tensor_tensor(bn[1][:, m, c], sn[:, m, c], bn[0][:, m, c], ALU.subtract)
                return ins

            def terms(src):
                dve.wait_ge(rows_in, S.due(rows_in, 16))
                for m in range(NT):
                    for r in range(2):
                        S.step(dve.tensor_tensor_reduce(flat[:, 0:D], src[:, m], rows[:, r], 1.0, 0.0, ALU.mult, ALU.add,
                                                        nv[:, r, m:m + 1]))
                mark(rows_free)

            def source_row(u=0):
                for m in range(NT):
                    ins = dve.tensor_scalar(aux[:, m, 2 * u * P:2 * u * P + P], ident[:, :], nv[:, 8 * u, m:m + 1], None,
                                            ALU.mult)
                ins.then_inc(dve_to_pe, 1)

            def target_rows(u=0, spare=aux):
                src, tgt, most, src_02, total, top, row_1, row_02 = (nv[:, 8 * u + n] for n in range(8))
                dve.wait_ge(tile_for["dve"], S.due(tile_for["dve"]))
                dve.memset(junk[:, 15:16], 0.0)
                for m in range(NT):
                    ins = dve.tensor_tensor_reduce(spare[:, m], ps[:, 6 + u], no_edge[:, m], 1.0, -3e38, ALU.add, ALU.max,
                                                   most[:, m:m + 1])
                freed(ins, 6 + u)
                S.step(dve.tensor_tensor(total, tgt, most, ALU.add))
                S.step(dve.scalar_tensor_tensor(out=top, in0=total, scalar=0.2, in1=total, op0=ALU.mult, op1=ALU.max))
                dve.tensor_scalar(src_02, src, 0.2, None, ALU.mult)
                dve.tensor_tensor(row_1, tgt, top, ALU.subtract)
                S.step(dve.scalar_tensor_tensor(out=row_02, in0=tgt, scalar=0.2, in1=top, op0=ALU.mult, op1=ALU.subtract))
                for r, v in enumerate((row_1, row_02)):
                    c = slice((2 * u + r) * P, (2 * u + r) * P + P)
                    for m in range(NT):
                        ins = dve.tensor_scalar(aux[:, m, c], ident[:, :], v[:, m:m + 1], None, ALU.mult)
                    ins.then_inc(dve_to_pe, 1)

            def edge_weights():
                def low_e(m):
                    dve.tensor_tensor(e_lo[:, m], scr[:, m], e_hi[:, m], ALU.subtract).then_inc(dve_to_pe, 1)

                for m in range(NT):
                    q = 2 * (m % 2)
                    dve.wait_ge(act_to_dve, S.due(act_to_dve))
                    S.step(dve.tensor_tensor(aux[:, q], aux[:, q], aux[:, q + 1], ALU.max))
                    dve.scalar_tensor_tensor(out=scr[:, m], in0=aux[:, q], scalar=1.0, in1=counts[:, m], op0=ALU.min,
                                             op1=ALU.mult).then_inc(dve_to_act, 1)
                    if 1 <= m < NT - 1:
                        dve.wait_ge(act_to_dve, S.due(act_to_dve))
                    if m >= 1:
                        low_e(m - 1)
                dve.wait_ge(act_to_dve, S.due(act_to_dve))
                low_e(NT - 1)

            def inverse_sums():
                dve.wait_ge(tile_for["dve"], S.due(tile_for["dve"]))
                freed(dve.tensor_scalar(row[:, :], ps[:, 6], 1e-16, None, ALU.add), 6)
                S.step(dve.reciprocal(row[:, :], row[:, :]))

            def head_output(from_psum=False):
                for s in range(KC + 2):
                    if s < KC and not from_psum:
                        dve.wait_ge(tile_for["dve"], S.due(tile_for["dve"]))
                        freed(dve.tensor_tensor(scr[:, s], ps[:, s], row[:, :], ALU.mult), s)
                        mark(dve_to_act)
                    if 1 <= s <= KC:
                        j = s - 1
                        q = 2 * (j % 2)
                        dve.wait_ge(act_to_dve, S.due(act_to_dve))
                        dve.scalar_tensor_tensor(out=scr[:, j], in0=aux[:, q], scalar=1.0, in1=aux[:, q + 1], op0=ALU.min,
                                                 op1=ALU.add).then_inc(dve_to_act, 1)
                    if s >= 2:
                        j = s - 2
                        dve.wait_ge(act_to_dve, S.due(act_to_dve))
                        dve.scalar_tensor_tensor(out=H[1][:, j], in0=scr[:, j], scalar=-1.0, in1=H[0][:, j], op0=ALU.add,
                                                 op1=ALU.subtract).then_inc(dve_to_pe, 1)

            def add_n(g):
                for m in range(NT):
                    b = (4 * g + m) % 6
                    c = slice(384 * g, 384 * g + 384)
                    dve.wait_ge(tile_for["dve"], S.due(tile_for["dve"]))
                    freed(dve.tensor_tensor(accn[:, m, c], ps[:, b, 0:384], accn[:, m, c], ALU.add), b)

            def add_t(dst, bias=None):
                for j in range(KC):
                    dve.wait_ge(tile_for["dve"], S.due(tile_for["dve"]))
                    if bias:
                        ins = dve.scalar_tensor_tensor(out=dst[:, j], in0=ps[:, j], scalar=col(bias, j), in1=dst[:, j],
                                                       op0=ALU.add, op1=ALU.add)
                    else:
                        ins = dve.tensor_tensor(dst[:, j], ps[:, j], dst[:, j], ALU.add)
                    freed(ins, j)

            def gat_sum(bias):
                for j in range(KC):
                    dve.wait_ge(tile_for["dve"], S.due(tile_for["dve"]))
                    S.step(dve.tensor_tensor(scr[:, j], ps[:, j], row[:, :], ALU.mult))
                    freed(dve.scalar_tensor_tensor(out=x[:, j], in0=scr[:, j], scalar=col(bias, j), in1=x[:, j],
                                                   op0=ALU.add, op1=ALU.add), j)

            def performer(what):
                scale = HD ** -0.25
                vh = flat[:, 0:NT * 132].rearrange("p (m h c) -> p m h c", m=NT, h=2)
                S.step(dve.memset(orf[HD:P, :, :], -0.5))
                dve.wait_ge(rows_in, S.due(rows_in, 16))
                with S.loop(what, 3) as i:
                    for g in range(2):
                        for b, c in ((0, 0), (1, KC)):
                            dve.wait_ge(tile_for["dve"], S.due(tile_for["dve"]))
                            freed(dve.tensor_scalar(scr[:, b], ps[:, b], col("L0_mix_qkv_b", i * 2 + (g + c)), scale,
                                                    ALU.add, ALU.mult), b)
                        mark(dve_to_act)
                        dve.wait_ge(tile_for["dve"], S.due(tile_for["dve"]))
                        for m in range(NT):
                            ins = dve.tensor_tensor(vh[:, m, :, 0:HD],
                                                    ps[:, 2, m * P:m * P + P].rearrange("p (h c) -> p h c", h=2),
                                                    rows[:, 1, bass.ds(i * 256 + g * P, P)].rearrange("p (h c) -> p h c", h=2),
                                                    ALU.add)
                        freed(ins, 2)
                        dve.memset(vh[:, :, :, HD:HD + 2], 1.0).then_inc(dve_to_pe, 1)
                        for h in range(2):
                            dve.wait_ge(tile_for["dve"], S.due(tile_for["dve"]))
                            for r in range(3):
                                dve.tensor_copy(aux[:, 2, r * P:r * P + HD], ps[:, 7, r * 68:r * 68 + HD])
                                ins = dve.tensor_scalar(aux[:, 2, r * P + HD:r * P + P], ones[:, 0:HD],
                                                        ps[:, 7, r * 68 + HD:r * 68 + HD + 1], None, ALU.mult)
                            freed(ins, 7)
                            dve.wait_ge(tile_for["dve"], S.due(tile_for["dve"]))
                            S.step(dve.tensor_scalar(row[0:HD, :], ps[HD:P, 3], 1e-8 * ORF, None, ALU.add))
                            S.step(dve.reciprocal(row[0:HD, :], row[0:HD, :]))
                            freed(dve.tensor_tensor(aux[h * HD:h * HD + HD, 3], ps[0:HD, 3], row[0:HD, :], ALU.mult), 3)
                        mark(dve_to_act)
                        dve.wait_ge(act_to_dve, S.due(act_to_dve))
                        f = bass.ds(2 * i + g, 1)
                        dve.tensor_tensor(H[1][:, f].rearrange("p o n -> p (o n)"), aux[:, 3],
                                          H[0][:, f].rearrange("p o n -> p (o n)"), ALU.subtract).then_inc(dve_to_pe, 1)
                mark(rows_free)

            def linear_attention(what, eps):
                S.step(dve.memset(kv[:, :, :], 0.0))
                S.step(dve.memset(same[:, :], 0.0))
                dve.memset(same[0:HD, 0:HD], 1.0)
                S.step(dve.memset(same[HD:P, HD:P], 1.0))
                S.step(dve.memset(v_n[:, :, :, P:P + 2], 1.0))
                dve.wait_ge(rows_in, S.due(rows_in, 16))
                with S.loop(what, 3) as i:
                    for g in range(2):
                        c = bass.ds(i * 256 + g * P, P)
                        for half in range(2):
                            b = 3 * g + 1 + half
                            dve.wait_ge(tile_for["dve"], S.due(tile_for["dve"]))
                            for m in range(2):
                                o = m * 256
                                dve.tensor_tensor(aux[:, half, m * P:m * P + P], ps[:, b, o:o + P], rows[:, 0, c], ALU.add)
                                ins = dve.tensor_tensor(v_n[:, g, 2 * half + m, 0:P], ps[:, b, o + P:o + 2 * P],
                                                        rows[:, 1, c], ALU.add)
                            freed(ins, b)
                            mark(dve_to_act)
                        for half in range(2):
                            dve.wait_ge(act_to_dve, S.due(act_to_dve))
                            dve.scalar_tensor_tensor(
                                out=k_n[:, g, 2 * half:2 * half + 2].rearrange("p m c -> p (m c)"),
                                in0=scr[:, 2 + half, 0:256], scalar=1.0, in1=scr[:, 2 + half, 256:512], op0=ALU.min,
                                op1=ALU.add)
                        dve.wait_ge(act_to_dve, S.due(act_to_dve))
                        dve.scalar_tensor_tensor(out=q_t[:, g], in0=scr[:, 0], scalar=1.0, in1=scr[:, 1], op0=ALU.min,
                                                 op1=ALU.add).then_inc(dve_to_pe, 1)
                    for g in range(2):
                        dve.wait_ge(tile_for["dve"], S.due(tile_for["dve"]))
                        dve.tensor_copy(kv[0:HD, g, 0:HD], ps[0:HD, 6 + g, 0:HD])
                        dve.tensor_copy(kv[HD:P, g, HD:P], ps[HD:P, 6 + g, HD:P])
                        freed(dve.tensor_scalar(k_sum[:, g], same[:, :], ps[:, 6 + g, P:P + 1], None, ALU.mult), 6 + g)
                    for g in range(2):
                        dve.wait_ge(tile_for["dve"], S.due(tile_for["dve"], 2))
                        freed(dve.tensor_scalar(row[:, :], ps[:, 3 * g + 1], eps, None, ALU.add), 3 * g + 1)
                        S.step(dve.reciprocal(row[:, :], row[:, :]))
                        freed(dve.tensor_tensor(aux[:, 2 + g], ps[:, 3 * g], row[:, :], ALU.mult), 3 * g)
                        mark(dve_to_act)
                    for g in range(2):
                        dve.wait_ge(act_to_dve, S.due(act_to_dve))
                        f = bass.ds(2 * i + g, 1)
                        dve.tensor_tensor(H[1][:, f].rearrange("p o n -> p (o n)"), aux[:, 2 + g],
                                          H[0][:, f].rearrange("p o n -> p (o n)"), ALU.subtract).then_inc(dve_to_pe, 1)
                mark(rows_free)

            def gelu_mlp(what, bias):
                for j in range(KC):
                    ins = dve.scalar_tensor_tensor(out=x[:, j], in0=acc[:, j], scalar=col(bias, j), in1=x[:, j],
                                                   op0=ALU.add, op1=ALU.add)
                S.step(ins)
                with S.loop(what, 4) as i:
                    for j in range(KC):
                        low(H, j, scr[:, j])
                    add_t(x)

            def experts(what, n, limit, per_chunk, periods):
                with S.loop(what, n) as i:
                    dve.tensor_copy(sel_now[:, :], sel[:, bass.ds(i * D, D)]).then_inc(dve_to_pe, 1) if per_chunk else \
                        dve.tensor_copy(sel_now[:, 0:P], sel[:, bass.ds(i * P, P)]).then_inc(dve_to_pe, 1)
                    if not per_chunk:
                        dve.wait_ge(tile_for["dve"], S.due(tile_for["dve"]))
                        freed(dve.tensor_copy(row[:, :], ps[:, 6]), 6)
                    for j in range(KC):
                        if per_chunk:
                            dve.wait_ge(tile_for["dve"], S.due(tile_for["dve"], 2))
                            freed(dve.scalar_tensor_tensor(out=scr[:, j], in0=scr[:, j], scalar=silu_limit, in1=ps[:, 6],
                                                           op0=ALU.min, op1=ALU.mult), 6)
                            freed(dve.tensor_scalar(aux[:, j % 4], ps[:, j], limit, -limit, ALU.min, ALU.max), j)
                            dve.tensor_tensor(scr[:, j], scr[:, j], aux[:, j % 4], ALU.mult).then_inc(dve_to_act, 1)
                        else:
                            dve.wait_ge(tile_for["dve"], S.due(tile_for["dve"]))
                            freed(dve.tensor_tensor(scr[:, j], scr[:, j], ps[:, j], ALU.mult), j)
                            dve.tensor_tensor(scr[:, j], scr[:, j], row[:, :], ALU.mult).then_inc(dve_to_act, 1)
                        if j >= 1:
                            low(H, j - 1, scr[:, j - 1])
                    low(H, KC - 1, scr[:, KC - 1])
                    add_t(x)

            silu_limit = 10.0 / (1.0 + float(np.exp(-10.0)))

            def best(src, eq, mask):
                S.step(dve.tensor_reduce(nv[:, 8], src, AX_X, ALU.max))
                S.step(dve.tensor_tensor(eq, src, nv[:, 8, :].unsqueeze(2).to_broadcast(list(src.shape)), ALU.is_equal))
                S.step(dve.scalar_tensor_tensor(out=eq, in0=eq, scalar=-100.0, in1=gate_s[:, 11, :, 0:src.shape[2]],
                                                op0=ALU.mult, op1=ALU.add))
                S.step(dve.tensor_reduce(nv[:, 8], eq, AX_X, ALU.min))
                S.step(dve.tensor_scalar(nv[:, 8], nv[:, 8], 100.0, None, ALU.add))
                S.step(dve.tensor_tensor(mask, gate_s[:, 11, :, 0:src.shape[2]],
                                         nv[:, 8, :].unsqueeze(2).to_broadcast(list(src.shape)), ALU.is_equal))

            def numbers():
                for e in range(8):
                    ins = dve.memset(gate_s[:, 11, :, e:e + 1], float(e))
                S.step(ins)

            def router_logits(n):
                dve.wait_ge(tile_for["dve"], S.due(tile_for["dve"]))
                freed(dve.tensor_copy(gate_s[:, 0, :, 0:n], ps[:, 6, 0:32].rearrange("p (m e) -> p m e", m=NT)[:, :, 0:n]), 6)

            def combine(n, score, rank):
                mask, two, tmp = gate_s[:, 7, :, 0:n], gate_s[:, 8, :, 0:n], gate_s[:, 9, :, 0:n]
                best(rank, tmp, two)
                S.step(dve.scalar_tensor_tensor(out=rank, in0=two, scalar=-3e38, in1=rank, op0=ALU.mult, op1=ALU.add))
                best(rank, tmp, mask)
                S.step(dve.tensor_tensor(two, two, mask, ALU.add))
                S.step(dve.tensor_tensor(two, two, score, ALU.mult))
                S.step(dve.tensor_reduce(nv[:, 9], two, AX_X, ALU.add))
                S.step(dve.tensor_scalar(nv[:, 9], nv[:, 9], 1e-6 if n == 8 else 0.0, None, ALU.max))
                S.step(dve.reciprocal(nv[:, 9], nv[:, 9]))
                S.step(dve.memset(comb_n[:, :, :], 0.0))
                S.step(dve.memset(comb_n[:, :, 8:9], 1.0))
                dve.tensor_tensor(comb_n[:, :, 0:n], two, nv[:, 9, :].unsqueeze(2).to_broadcast([P, NT, n]), ALU.mult)\
                   .then_inc(dve_to_pe, 1)
                dve.wait_ge(tile_for["dve"], S.due(tile_for["dve"]))
                freed(dve.tensor_copy(comb_t[:, :], ps[0:16, 6]), 6)
                dve.wait_ge(sel_in, S.due(sel_in, 16))

            dve.wait_ge(edges_in, 32)
            dve.wait_ge(setup_done, n_setup)
            dve.tensor_copy(src_f[:, :], src_i[:, :])
            S.step(dve.tensor_copy(dst_f[:, :], dst_i[:, :]))
            with S.loop("edges", EC // 2) as i:
                for c in range(2):
                    dve.wait_ge(tile_for["dve"], S.due(tile_for["dve"]))
                    for r, f in enumerate((src_f, dst_f)):
                        ins = dve.tensor_scalar(hot[:, c, r], iota[:, :], f[:, bass.ds(i * 2 + c, 1)], None, ALU.is_equal)
                    ins.then_inc(dve_to_pe, 1)
            dve.wait_ge(tile_for["dve"], S.due(tile_for["dve"], 2))
            for m in range(NT):
                dve.tensor_copy(aux[:, m], ps[:, m]).then_inc(bank_free["dve"][m], 1)
                dve.wait_ge(bank_free["dve"][m], S.due(bank_free["dve"][m]))
                dve.tensor_copy(counts[:, m], aux[:, m]).then_inc(dve_to_pe, 1)
            for m in range(NT):
                dve.wait_ge(tile_for["dve"], S.due(tile_for["dve"]))
                freed(dve.tensor_scalar(no_edge[:, m], ps[:, 4 + m % 2], 0.0, NO_EDGE, ALU.is_equal, ALU.mult), 4 + m % 2)
            dve.wait_ge(loaded, 64)
            dve.wait_ge(act_to_dve, S.due(act_to_dve))
            S.step(dve.tensor_tensor(small_lo[:, :, :], small[:, :, :], small_hi[:, :, :], ALU.subtract))

            norm(x, acc, A, 1e-5)
            if "mix0" in parts:
                norm(acc, scr, B, 1e-5, "L0_mix_ln1_g", "L0_mix_ln1_b")
                performer("performer")
                add_t(acc, "L0_mix_proj_b")
                norm(acc, scr, B, 1e-5, "L0_mix_ln2_g", "L0_mix_ln2_b")
                gelu_mlp("mlp0", "L0_mix_fc2_b")
            if "gnn0" in parts:
                S.step(dve.memset(acc[:, :, :], 0.0))
                features_n()
                terms(sn)
                source_row()
                target_rows()
                edge_weights()
                inverse_sums()
                head_output()
                with S.loop("gat0", GAT - 1) as i:
                    mark(dve_to_act)
                    features_n()
                    terms(sn)
                    source_row()
                    add_n(0)
                    target_rows()
                    edge_weights()
                    add_n(1)
                    inverse_sums()
                    head_output()
                add_n(0)
                add_n(1)
                mark(dve_to_act)
                for m in range(NT):
                    dve.wait_ge(act_to_dve, S.due(act_to_dve))
                    dve.tensor_tensor(bn[1][:, m], accn[:, m], bn[0][:, m], ALU.subtract)
                terms(accn)
                source_row()
                target_rows()
                edge_weights()
                inverse_sums()
                gat_sum("L0_gnn_b2")
            if "ffn0" in parts:
                norm(x, acc, A, 1e-5)
                numbers()
                router_logits(8)
                S.step(dve.tensor_scalar(gate_s[:, 1], gate_s[:, 0], -1.0, None, ALU.mult))
                dve.tensor_tensor(gate_s[:, 1], gate_s[:, 1], gate_s[:, 0], ALU.max).then_inc(dve_to_act, 1)
                dve.wait_ge(act_to_dve, S.due(act_to_dve))
                dve.tensor_scalar(gate_s[:, 3], gate_s[:, 2], 1.0, None, ALU.add).then_inc(dve_to_act, 1)
                dve.wait_ge(act_to_dve, S.due(act_to_dve))
                dve.scalar_tensor_tensor(out=gate_s[:, 5], in0=gate_s[:, 0], scalar=0.0, in1=gate_s[:, 4], op0=ALU.max,
                                         op1=ALU.add).then_inc(dve_to_act, 1)
                dve.wait_ge(act_to_dve, S.due(act_to_dve))
                for m in range(NT):
                    ins = dve.tensor_tensor(gate_s[:, 10, m], gate_s[:, 6, m], vecs[:, V_GATE:V_GATE + 8], ALU.add)
                S.step(ins)
                combine(8, gate_s[:, 6], gate_s[:, 10])
                experts("experts0", 3, 10.0, True, 3)

            if "mix1" in parts or "gnn1" in parts:
                norm(x, acc, A, 1e-5)
            if "mix1" in parts:
                norm(acc, scr, B, 1e-5, "L1_mix_ln_gamma", "L1_mix_ln_beta")
                linear_attention("attention1", 1e-6)
                add_t(x, "L1_mix_b_proj")
            if "gnn1" in parts:
                mark(dve_to_act)
                for v in head_n:
                    dve.memset(v[:, :, :, C1:C2], 1.0)
                dve.wait_ge(rows_in, S.due(rows_in, 16))
                for g in range(2):
                    for m in range(NT):
                        dve.wait_ge(act_to_dve, S.due(act_to_dve))
                        c = slice(384 * g, 384 * g + 384)
                        for r in range(2):
                            S.step(dve.tensor_tensor(flat[:, 0:384].rearrange("p (h c) -> p h c", h=4),
                                                     head_n[m // 2][:, m % 2, 4 * g:4 * g + 4, 0:C1],
                                                     rows[:, r, c].rearrange("p (h c) -> p h c", h=4), ALU.mult))
                            S.step(dve.tensor_reduce(al[:, r, m, 4 * g:4 * g + 4],
                                                     flat[:, 0:384].rearrange("p (h c) -> p h c", h=4), AX_X, ALU.add))
                mark(rows_free)
                mark(dve_to_pe)
                with S.loop("gat1", GAT // 2) as i:
                    for u in range(2):
                        for r in range(2):
                            S.step(dve.tensor_copy(nv[:, 8 * u + r],
                                                   al[:, r, :, bass.ds(i * 2 + u, 1)].rearrange("p m o -> p (m o)")))
                        source_row(u)
                    for u in range(2):
                        target_rows(u, edge_w[u])
                    for u in range(2):
                        for m in range(NT + 1):
                            if m < NT:
                                dve.wait_ge(act_to_dve, S.due(act_to_dve))
                                dve.tensor_tensor(exp_1[u][:, m], exp_1[u][:, m], exp_02[u][:, m], ALU.max)\
                                   .then_inc(dve_own, 1)
                            if m >= 1:
                                dve.wait_ge(dve_own, S.due(dve_own))
                                dve.scalar_tensor_tensor(out=edge_w[u][:, m - 1], in0=exp_1[u][:, m - 1], scalar=1.0,
                                                         in1=counts[:, m - 1], op0=ALU.min, op1=ALU.mult)\
                                   .then_inc(dve_to_pe, 1)
                    for u in range(2):
                        inv = row[:, 4 * u:4 * u + 4]
                        o = ps[:, u, :].rearrange("p (m c) -> p m c", m=NT)
                        dve.wait_ge(tile_for["dve"], S.due(tile_for["dve"]))
                        S.step(dve.tensor_scalar(inv, o[:, :, C1], 1e-16, None, ALU.add))
                        S.step(dve.reciprocal(inv, inv))
                        for m in range(NT):
                            ins = dve.tensor_scalar(accn[:, m, bass.ds((i * 2 + u) * C1, C1)], o[:, m, 0:C1],
                                                    inv[:, m:m + 1], None, ALU.mult)
                        freed(ins, u)
                mark(dve_to_pe)
                head_output(True)
                mark(dve_to_act)
                features_n()
                terms(sn)
                source_row()
                target_rows()
                edge_weights()
                inverse_sums()
                gat_sum("L1_gnn_b2")
            if "ffn1" in parts:
                norm(x, acc, A, 1e-5)
                g3 = small[:, :, GP:GP + 12]
                for k in range(KC):
                    o = aux[:, k % 4, (k // 4) * 32:(k // 4) * 32 + 30]
                    xk = acc[:, k, 0:NCLS]
                    dve.tensor_tensor(o[:, 0:12].rearrange("p (n r) -> p n r", r=2), g3[:, k].rearrange("p (n r) -> p n r", r=2),
                                      xk.unsqueeze(2).to_broadcast([P, NCLS, 2]), ALU.mult)
                    dve.tensor_tensor(o[:, 12:24], g3[:, k], g3[:, k], ALU.mult)
                    ins = dve.tensor_tensor(o[:, 24:30], xk, xk, ALU.mult)
                ins.then_inc(dve_to_pe, 1)
                dve.wait_ge(tile_for["dve"], S.due(tile_for["dve"]))
                freed(dve.tensor_copy(rt[:, 0, 0:30], ps[:, 6, 0:30]), 6)
                mark(dve_to_act)
                dve.wait_ge(act_to_dve, S.due(act_to_dve))
                S.step(dve.tensor_scalar(rt[:, 1, 12:30], rt[:, 1, 12:30], 1e-12, None, ALU.max))
                S.step(dve.reciprocal(rt[:, 1, 12:30], rt[:, 1, 12:30]))
                S.step(dve.tensor_tensor(rt[:, 0, 0:12], rt[:, 0, 0:12], rt[:, 1, 12:24], ALU.mult))
                lg = rt[:, 0, 0:12].rearrange("p (n r) -> p n r", r=2)
                S.step(dve.tensor_tensor(lg, lg, rt[:, 1, 24:30].unsqueeze(2).to_broadcast([P, NCLS, 2]), ALU.mult))
                S.step(dve.tensor_tensor(rt[:, 0, 0:12], rt[:, 0, 0:12], vecs[:, V_BAL:V_BAL + 12], ALU.add))
                S.step(dve.tensor_tensor(rt[:, 4, 0:6], lg[:, :, 1], lg[:, :, 0], ALU.subtract))
                S.step(dve.tensor_scalar(rt[:, 2, 0:6], rt[:, 4, 0:6], -1.0, None, ALU.mult))
                dve.tensor_tensor(rt[:, 2, 0:6], rt[:, 2, 0:6], rt[:, 4, 0:6], ALU.min).then_inc(dve_to_act, 1)
                dve.wait_ge(act_to_dve, S.due(act_to_dve))
                S.step(dve.tensor_scalar(rt[:, 3, 0:6], rt[:, 3, 0:6], 1.0, None, ALU.add))
                S.step(dve.reciprocal(rt[:, 3, 0:6], rt[:, 3, 0:6]))
                w = rt[:, 5, 0:12].rearrange("p (n r) -> p n r", r=2)
                S.step(dve.tensor_scalar(rt[:, 4, 0:6], rt[:, 4, 0:6], 0.0, None, ALU.is_gt))
                S.step(dve.tensor_tensor(w[:, :, 1], rt[:, 4, 0:6], rt[:, 3, 0:6], ALU.mult))
                S.step(dve.tensor_tensor(w[:, :, 0], rt[:, 3, 0:6], w[:, :, 1], ALU.subtract))
                S.step(dve.memset(cls_w[:, :], 0.0))
                dve.wait_ge(sel_in, S.due(sel_in, 32))
                S.step(dve.tensor_tensor(route[:, :], route[:, :], rt[0:ATOMS, 5, 0:12], ALU.mult))
                S.step(dve.tensor_reduce(cls_w[:, 0:6], route[:, :].rearrange("p (n r) -> p n r", r=2), AX_X, ALU.add))
                for q in range(2):
                    low(H, q, scr[:, q])
                S.step(dve.memset(scr[:, 3, 0:80], 0.0))
                dve.wait_ge(act_to_dve, S.due(act_to_dve))
                hid = scr[:, 2, 0:80].rearrange("p (a h n) -> p a h n", a=ATOMS, h=2)
                wei = scr[:, 3, 0:80].rearrange("p (a h n) -> p a h n", a=ATOMS, h=2)
                for n in range(NCLS):
                    for r in range(2):
                        of, to = PAIRS[n][r], PAIRS[n][1 - r]
                        ins = dve.tensor_scalar(wei[:, to, :, n:n + 1], hid[:, of, :, n:n + 1], w[:, n, r:r + 1], None, ALU.mult)
                ins.then_inc(dve_to_act, 1)
                dve.wait_ge(act_to_dve, S.due(act_to_dve))
                dve.tensor_tensor(H[1][:, 2, 0:80], scr[:, 3, 0:80], H[0][:, 2, 0:80], ALU.subtract).then_inc(dve_to_pe, 1)
                for j in range(KC):
                    dve.wait_ge(tile_for["dve"], S.due(tile_for["dve"]))
                    freed(dve.scalar_tensor_tensor(out=x[:, j, NCLS:N], in0=ps[:, j, NCLS:N], scalar=col("L1_ffn_fc2_b", j),
                                                   in1=x[:, j, NCLS:N], op0=ALU.add, op1=ALU.add), j)
                dve.wait_ge(tile_for["dve"], S.due(tile_for["dve"]))
                for r, o in enumerate((0, 48, 96)):
                    ins = dve.tensor_tensor(x[:, :, 0:NCLS], x[:, :, 0:NCLS],
                                            ps[:, 6, o:o + 48].rearrange("p (f n) -> p f n", n=8)[:, :, 0:NCLS], ALU.add)
                    if r < 2:
                        S.step(ins)
                freed(ins, 6)

            def gcn(bias):
                for m in range(NT):
                    S.step(dve.tensor_copy(aux[:, m], counts[:, m]))
                    c = slice(m * P, m * P + P)
                    S.step(dve.tensor_tensor(aux[:, m, c], aux[:, m, c], ident[:, :], ALU.add))
                mark(dve_to_pe)
                dve.wait_ge(tile_for["dve"], S.due(tile_for["dve"]))
                freed(dve.tensor_copy(row[:, :], ps[:, 6]), 6)
                mark(dve_to_act)
                dve.wait_ge(act_to_dve, S.due(act_to_dve))
                S.step(dve.reciprocal(row[:, :], row[:, :]))
                for m in range(NT):
                    S.step(dve.tensor_tensor_reduce(flat_junk, ident[:, :], row[:, m * P:m * P + P], 1.0, 0.0, ALU.mult,
                                                    ALU.add, nv[:, 14, m:m + 1]))
                for m in range(NT):
                    dve.scalar_tensor_tensor(out=scr[:, m], in0=aux[:, m], scalar=nv[:, 14, m:m + 1], in1=row[:, :],
                                             op0=ALU.mult, op1=ALU.mult).then_inc(dve_to_act, 1)
                for m in range(NT):
                    dve.wait_ge(act_to_dve, S.due(act_to_dve))
                    dve.tensor_tensor(e_lo[:, m], scr[:, m], e_hi[:, m], ALU.subtract)
                mark(dve_to_act)
                features_n()
                mark(dve_to_pe)
                add_t(x, bias)

            flat_junk = scr[:, 5, 0:P]
            if "gnn2" in parts or "mix2" in parts:
                norm(x, acc, A, 1e-5)
            if "gnn2" in parts:
                gcn("L2_gnn_b")
            if "mix2" in parts:
                linear_attention("attention2", 0.0)
                add_t(x, "L2_mix_bo")
            if "ffn2" in parts:
                norm(x, acc, A, 1e-5)
                numbers()
                router_logits(3)
                for m in range(NT):
                    ins = dve.tensor_tensor(gate_s[:, 1, m, 0:3], gate_s[:, 0, m, 0:3], vecs[:, V_ROUTE:V_ROUTE + 3], ALU.add)
                ins.then_inc(dve_to_act, 1)
                dve.wait_ge(act_to_dve, S.due(act_to_dve))
                S.step(dve.tensor_scalar(gate_s[:, 6, :, 0:3], gate_s[:, 2, :, 0:3], 1.0, None, ALU.add))
                S.step(dve.reciprocal(gate_s[:, 6, :, 0:3], gate_s[:, 6, :, 0:3]))
                S.step(dve.tensor_copy(gate_s[:, 10, :, 0:3], gate_s[:, 6, :, 0:3]))
                combine(3, gate_s[:, 6, :, 0:3], gate_s[:, 10, :, 0:3])
                experts("experts2", 8, 0.0, False, 8)
            if "gnn3" in parts or "mix3" in parts:
                norm(x, acc, A, 1e-5)
            if "gnn3" in parts:
                gcn("L3_gnn_b")
            if "mix3" in parts:
                norm(acc, scr, B, 1e-8, "L3_mix_ln1_w", "L3_mix_ln1_b")
                linear_attention("attention3", 0.0)
                add_t(acc, "L3_mix_proj_b")
                norm(acc, scr, B, 1e-8, "L3_mix_ln2_w", "L3_mix_ln2_b")
                gelu_mlp("mlp3", "L3_mix_fc2_b")
            if "ffn3" in parts:
                def nodes_low():
                    for g in range(2):
                        for m in range(NT):
                            c = slice(384 * g, 384 * g + 384)
                            b = (4 * g + m) % 6
                            dve.wait_ge(act_to_dve, S.due(act_to_dve))
                            freed(dve.tensor_tensor(bn[1][:, m, c], ps[:, b, 0:384], bn[0][:, m, c], ALU.subtract), b)

                norm(x, acc, A, 1e-5)
                numbers()
                router_logits(8)
                wide = [P, NT, 8]
                S.step(dve.tensor_reduce(nv[:, 11], gate_s[:, 0], AX_X, ALU.max))
                dve.tensor_tensor(gate_s[:, 1], gate_s[:, 0], nv[:, 11, :].unsqueeze(2).to_broadcast(wide), ALU.subtract)\
                   .then_inc(dve_to_act, 1)
                dve.wait_ge(act_to_dve, S.due(act_to_dve))
                S.step(dve.tensor_reduce(nv[:, 12], gate_s[:, 2], AX_X, ALU.add))
                S.step(dve.reciprocal(nv[:, 12], nv[:, 12]))
                best(gate_s[:, 0], gate_s[:, 9], gate_s[:, 7])
                dve.wait_ge(sel_in, S.due(sel_in, 16))
                mark(dve_to_pe)
                nodes_low()
                dve.wait_ge(tile_for["dve"], S.due(tile_for["dve"]))
                S.step(dve.tensor_scalar(gate_s[:, 8], ps[:, 6, 0:32].rearrange("p (m e) -> p m e", m=NT), 64.0, None, ALU.is_lt))
                S.step(dve.tensor_tensor(gate_s[:, 8], gate_s[:, 8], gate_s[:, 7], ALU.mult))
                freed(dve.scalar_tensor_tensor(out=gate_s[:, 9], in0=ps[:, 6, 0:32].rearrange("p (m e) -> p m e", m=NT),
                                               scalar=1.0, in1=gate_s[:, 8], op0=ALU.add, op1=ALU.mult), 6)
                S.step(dve.tensor_scalar(al[:, 0], gate_s[:, 9], -1.0, None, ALU.add))
                slots = [P, 8, 64]
                for m in range(NT):
                    S.step(dve.tensor_tensor(aux[:, m].rearrange("p (e c) -> p e c", e=8),
                                             tri[:, P:P + 64].unsqueeze(1).to_broadcast(slots),
                                             al[:, 0, m].unsqueeze(2).to_broadcast(slots), ALU.is_equal))
                for m in range(NT):
                    S.step(dve.tensor_copy(e_hi[:, m], aux[:, m]))
                    S.step(dve.tensor_scalar(aux[:, m], aux[:, m], nv[:, 12, m:m + 1], None, ALU.mult))
                mark(dve_to_pe)
                for j in range(KC):
                    low(A, j, scr[:, j])
                mark(dve_to_act)
                for q in range(16):
                    dve.wait_ge(act_to_dve, S.due(act_to_dve))
                    c = slice(q % 8 * 64, q % 8 * 64 + 64)
                    dve.tensor_tensor(H[1][:, q // 8, c], scr[:, q // 8, c], H[0][:, q // 8, c], ALU.subtract)\
                       .then_inc(dve_to_pe, 1)
                for m in range(NT):
                    dve.wait_ge(act_to_dve, S.due(act_to_dve))
                    freed(dve.tensor_tensor(e_lo[:, m], ps[:, m], e_hi[:, m], ALU.subtract), m)
                nodes_low()
                mark(dve_to_pe)
                add_t(x)
            mark(dve_to_act)


def stacked(inputs, *names):
    return [np.asarray(inputs[n]) for n in names]


def padded(a, n, axis):
    shape = list(a.shape)
    shape[axis] = n - a.shape[axis]
    return np.concatenate([a, np.zeros(shape, a.dtype)], axis)


def weight_stream(v, parts):
    out = []

    def cols_of(w):
        out.extend(w[:, 384 * g:384 * g + 384] for g in range(w.shape[1] // 384))

    def thirds(q, k, u):
        for f in range(KC):
            c = slice(f * P, f * P + P)
            out.append(np.concatenate([q[:, c], k[:, c], u[:, c]], 1))

    def kvq(w):
        thirds(w[:, D:2 * D], w[:, 2 * D:], w[:, 0:D])

    def mlp(w1, w2):
        for i in range(w1.shape[1] // D):
            cols_of(w1[:, i * D:i * D + D])
            cols_of(w2[i * D:i * D + D])

    def gated(g, u, d):
        for i in range(g.shape[1] // D):
            cols_of(g[:, i * D:i * D + D])
            cols_of(u[:, i * D:i * D + D])
            cols_of(d[i * D:i * D + D])

    if "mix0" in parts:
        w = v["L0_mix_qkv_w"]
        thirds(w[:, 0:D], w[:, D:2 * D], w[:, 2 * D:])
        cols_of(v["L0_mix_proj_w"])
        mlp(v["L0_mix_fc1_w"], v["L0_mix_fc2_w"])
    if "gnn0" in parts:
        w1, w2 = v["L0_gnn_W1"], v["L0_gnn_W2"]
        cols_of(w1[:, 0:D])
        for h in range(1, GAT):
            cols_of(w1[:, h * D:h * D + D])
            cols_of(w2[h * D - D:h * D])
        cols_of(w2[7 * D:])
    if "ffn0" in parts:
        def wide(w, s):
            return padded(np.concatenate(list(w) + [s], 1), 3 * D, 1)
        down = padded(np.concatenate(list(v["L0_ffn_w2"]) + [v["L0_ffn_w2s"]], 0), 3 * D, 0)
        gated(wide(v["L0_ffn_w1"], v["L0_ffn_w1s"]), wide(v["L0_ffn_w3"], v["L0_ffn_w3s"]), down)
    if "mix1" in parts:
        kvq(v["L1_mix_w_qkv"].T)
        cols_of(v["L1_mix_w_proj"].T)
    if "gnn1" in parts:
        cols_of(v["L1_gnn_W1"])
        cols_of(v["L1_gnn_W2"])
    if "ffn1" in parts:
        ups = [v["L1_ffn_fc1_w"].T] + [w.T for w in v["L1_ffn_atom_in_w"]]
        cols_of(np.concatenate([padded(w, 256, 1) for w in ups], 1))
        downs = [v["L1_ffn_fc2_w"].T] + [w.T for w in v["L1_ffn_atom_out_w"]]
        down = np.concatenate([padded(w, 256, 0) for w in downs], 0)
        cols_of(down[0:D])
        cols_of(down[D:])
    if "gnn2" in parts:
        cols_of(v["L2_gnn_W"])
    if "mix2" in parts:
        thirds(v["L2_mix_Wk"], v["L2_mix_Wv"], v["L2_mix_Wq"])
        cols_of(v["L2_mix_Wo"])
    if "ffn2" in parts:
        gated(v["L2_ffn_shared_gate"], v["L2_ffn_shared_up"], v["L2_ffn_shared_down"])
        for e in range(3):
            gated(v["L2_ffn_routed_gate"][e], v["L2_ffn_routed_up"][e], v["L2_ffn_routed_down"][e])
    if "gnn3" in parts:
        cols_of(v["L3_gnn_W"])
    if "mix3" in parts:
        kvq(v["L3_mix_qkv_w"])
        cols_of(v["L3_mix_proj_w"])
        mlp(v["L3_mix_fc1_w"], v["L3_mix_fc2_w"])
    if "ffn3" in parts:
        up = np.concatenate([padded(w, 256, 1) for w in v["L3_ffn_w1"]], 1)
        cols_of(padded(up, 3 * D, 1))
        down = padded(np.concatenate([padded(w, 256, 0) for w in v["L3_ffn_w2"]], 0), 3 * D, 0)
        for i in range(3):
            cols_of(down[i * D:i * D + D])
    return np.concatenate([w.reshape(KC, P, 3, P).transpose(2, 1, 0, 3).reshape(3, P, D) for w in out])


def column_table(v):
    def in_columns(a):
        return a.reshape(-1, P).T

    special = {
        "L1_ffn_in_b": lambda: padded(np.concatenate([v["L1_ffn_fc1_b"][None], v["L1_ffn_atom_in_b"]], 0), 256, 1),
        "L3_ffn_b1": lambda: padded(v["L3_ffn_b1"], 256, 1),
        "zero": lambda: np.zeros(D, np.float32),
    }
    return np.concatenate([in_columns(np.ascontiguousarray(special[n]() if n in special else v[n])) for n, _ in COLUMNS], 1)


def selectors(width, expert_of):
    s = np.zeros((16, 3 * D), np.float32)
    for c in range(width):
        s[expert_of(c), c] = 1.0
    return s


def lay_out(v, parts):
    def t_layout(a):
        return a.reshape(KC, P, -1).transpose(1, 0, 2)

    small = np.zeros((D, NSMALL), np.float32)
    small[:, R0:R0 + 8] = v["L0_ffn_gate_w"]
    small[:, R2:R2 + 3] = v["L2_ffn_router_w"]
    small[:, R3:R3 + 8] = v["L3_ffn_router_w"]
    small[:, GP:GP + 12] = v["L1_ffn_gate_pair"].reshape(12, D).T
    rows = np.zeros((NROWS, 2, D), np.float32)
    rows[0:8, 0], rows[0:8, 1] = v["L0_gnn_a_src1"], v["L0_gnn_a_dst1"]
    rows[ROW_L0B, 0], rows[ROW_L0B, 1] = v["L0_gnn_a_src2"][0], v["L0_gnn_a_dst2"][0]
    rows[ROW_L1, 0], rows[ROW_L1, 1] = v["L1_gnn_a_src1"].reshape(D), v["L1_gnn_a_dst1"].reshape(D)
    rows[ROW_L1B, 0], rows[ROW_L1B, 1] = v["L1_gnn_a_src2"][0], v["L1_gnn_a_dst2"][0]
    rows[ROW_KV0] = v["L0_mix_qkv_b"].reshape(3, D)[1:]
    rows[ROW_KV2, 0], rows[ROW_KV2, 1] = v["L2_mix_bk"], v["L2_mix_bv"]
    rows[ROW_KV3] = v["L3_mix_qkv_b"].reshape(3, D)[1:]
    vecs = np.zeros(NVEC, np.float32)
    vecs[V_GATE:V_GATE + 8] = v["L0_ffn_gate_bias"]
    vecs[V_ROUTE:V_ROUTE + 3] = v["L2_ffn_routing_bias"]
    vecs[V_BAL:V_BAL + 12] = v["L1_ffn_balance_bias"].reshape(12)
    made = {
        "x": t_layout(v["x"].T),
        "src": v["src"].reshape(P, EC),
        "dst": v["dst"].reshape(P, EC),
        "stream": weight_stream(v, parts),
        "cols": column_table(v),
        "small": t_layout(small),
        "rows": rows,
        "vecs": vecs,
        "orf": v["L0_mix_w_orf"].reshape(3, 4, HD, ORF).transpose(0, 2, 1, 3).reshape(3, HD, 4 * ORF),
        "sel0": selectors(9 * FF, lambda c: c // FF),
        "sel2": selectors(8 * P, lambda c: 8 if c < 2 * P else c // (2 * P) - 1),
        "atom_b": v["L1_ffn_atom_out_b"],
        "tri": np.concatenate([np.triu(np.ones((P, P))), np.tile(np.arange(64), (P, 1))], 1).astype(np.float32),
        "route": np.array([[float(PAIRS[n][1 - r] == a) for n in range(NCLS) for r in range(2)] for a in range(ATOMS)],
                          np.float32),
    }
    return {k: np.ascontiguousarray(a) for k, a in made.items()}


def kernel(**inputs):
    import concourse.bacc as bacc
    from concourse.bass_utils import run_bass_kernel_spmd

    arrays = lay_out({k: np.asarray(a) for k, a in inputs.items()}, list(TURNS))
    nc = bacc.Bacc("TRN2", target_bir_lowering=False, num_devices=1)
    t = {k: nc.dram_tensor(k + "_dram", a.shape, mybir.dt.from_np(a.dtype), kind="ExternalInput").ap()
         for k, a in arrays.items()}
    out = nc.dram_tensor("out_dram", (P, KC, N), F32, kind="ExternalOutput").ap()
    build(nc, t, out, list(TURNS), LOOP_EVENTS)
    r = run_bass_kernel_spmd(nc, [{k + "_dram": a for k, a in arrays.items()}], core_ids=[0])
    return r.results[0]["out_dram"].transpose(1, 0, 2).reshape(D, N).T
```

```python
from contextlib import ExitStack, contextmanager

import concourse.bass as bass
import numpy as np
from concourse import mybir

F32 = mybir.dt.float32
F32R = mybir.dt.float32r
BF16 = mybir.dt.bfloat16
I32 = mybir.dt.int32
I16 = mybir.dt.int16
ALU = mybir.AluOpType
ACT = mybir.ActivationFunctionType
AX_X = mybir.AxisListType.X

P = 128
N = 512
D = 768
KC = D // P
NT = N // P
EDGES = 16384
EC = EDGES // P
HEADS = 12
HD = D // HEADS
ORF = 384
GAT = 8
C1 = D // GAT
C2 = C1 + 2
NCLS = 6
ATOMS = 5
PAIRS = [(0, 3), (0, 4), (1, 3), (1, 4), (2, 3), (2, 4)]
FF = 192
NO_EDGE = -1e30

COLUMNS = [
    ("L0_gnn_b1", 48), ("L0_gnn_b2", 6), ("L0_mix_ln1_g", 6), ("L0_mix_ln1_b", 6), ("L0_mix_qkv_b", 18),
    ("L0_mix_proj_b", 6), ("L0_mix_ln2_g", 6), ("L0_mix_ln2_b", 6), ("L0_mix_fc1_b", 24), ("L0_mix_fc2_b", 6),
    ("L1_gnn_b1", 6), ("L1_gnn_b2", 6), ("L1_mix_ln_gamma", 6), ("L1_mix_ln_beta", 6), ("L1_mix_b_proj", 6),
    ("L1_ffn_in_b", 12), ("L1_ffn_fc2_b", 6), ("L2_gnn_b", 6), ("L2_mix_bq", 6), ("L2_mix_bo", 6),
    ("L3_gnn_b", 6), ("L3_mix_qkv_b", 18), ("L3_mix_proj_b", 6), ("L3_mix_fc1_b", 24), ("L3_mix_fc2_b", 6),
    ("L3_mix_ln1_w", 6), ("L3_mix_ln1_b", 6), ("L3_mix_ln2_w", 6), ("L3_mix_ln2_b", 6),
    ("L3_ffn_b1", 16), ("L3_ffn_b2", 48), ("zero", 6),
]
COL = {}
for _name, _n in COLUMNS:
    COL[_name] = sum(n for _, n in COLUMNS[:len(COL)])
NCOL = sum(n for _, n in COLUMNS)
R0, R2, R3, GP = 0, 8, 12, 20
NSMALL = 32
ROW_L0, ROW_L0B, ROW_L1, ROW_L1B, ROW_KV0, ROW_KV1, ROW_KV2, ROW_KV3, NROWS = 0, 8, 9, 10, 11, 12, 13, 14, 15
V_GATE, V_ROUTE, V_BAL, NVEC = 0, 8, 12, 24
TURNS = dict(mix0=3 + 1 + 8, gnn0=16, ffn0=7, mix1=4, gnn1=2, ffn1=4, gnn2=1, mix2=4, ffn2=24, gnn3=1, mix3=12, ffn3=6)
WHOLE = ("ffn1", "ffn3")


class Side:

    def __init__(self, eng, name, own, events):
        self.eng, self.name, self.own, self.events = eng, name, own, events
        self.seen, self.i, self.per, self.pending = {}, None, {}, {}

    def due(self, sem, k=1):
        n = self.seen[sem.name] = self.seen.get(sem.name, 0) + k
        return n if self.i is None else self.i * self.per.get(sem.name, 0) + n

    def coming(self, sem):
        n = self.seen.get(sem.name, 0) + 1
        return n if self.i is None else self.i * self.per.get(sem.name, 0) + n

    def step(self, ins):
        ins.then_inc(self.own, 1)
        self.eng.wait_ge(self.own, self.due(self.own))

    @contextmanager
    def loop(self, what, n):
        key = f"{what}/{self.name}"
        self.per = self.events.get(key, {})
        before, held = dict(self.seen), dict(self.pending)
        with self.eng.Fori(0, n) as i:
            self.i = i
            yield i
            self.i = None
        per = {s: v - before.get(s, 0) for s, v in self.seen.items() if v != before.get(s, 0)}
        check_events(key, per, self.per)
        assert held == self.pending, (key, held, self.pending)
        for s, v in per.items():
            self.seen[s] += (n - 1) * v


def check_events(key, found, stated):
    assert found == stated, f"{key}: one iteration waits for {found}"


LOOP_EVENTS = {
    "edges/pe": {"dve_to_pe": 2},
    "performer/pe": {"dve_to_pe": 4, "act_to_pe": 4, "bank_free_by_dve7": 4, "w_split": 6, "bank_free_by_dve0": 4,
        "bank_free_by_dve1": 4, "bank_free_by_dve2": 2, "bank_free_by_act3": 8, "bank_free_by_act4": 8,
        "bank_free_by_act5": 8, "bank_free_by_act6": 4},
    "mlp0/pe": {"dve_to_pe": 6, "bank_free_by_dve4": 1, "bank_free_by_dve5": 1, "bank_free_by_dve0": 1,
        "bank_free_by_dve1": 1, "bank_free_by_dve2": 1, "bank_free_by_dve3": 1, "w_split": 12,
        "bank_free_by_act3": 1, "bank_free_by_act4": 1, "bank_free_by_act5": 1, "bank_free_by_act0": 1,
        "bank_free_by_act1": 1, "bank_free_by_act2": 1},
    "performer/act": {"dve_to_act": 4, "tile_for_act": 28, "orf_in": 16, "bank_free_by_act3": 8,
        "bank_free_by_act4": 8, "bank_free_by_act5": 8, "bank_free_by_act6": 4},
    "mlp0/act": {"tile_for_act": 6, "bank_free_by_act3": 1, "bank_free_by_act4": 1, "bank_free_by_act5": 1,
        "bank_free_by_act0": 1, "bank_free_by_act1": 1, "bank_free_by_act2": 1},
    "edges/dve": {"tile_for_dve": 2},
    "performer/dve": {"dve_own": 8, "tile_for_dve": 14, "bank_free_by_dve0": 4, "bank_free_by_dve1": 4,
        "bank_free_by_dve2": 2, "act_to_dve": 2, "bank_free_by_dve7": 4},
    "mlp0/dve": {"tile_for_dve": 6, "bank_free_by_dve0": 1, "bank_free_by_dve1": 1, "bank_free_by_dve2": 1,
        "bank_free_by_dve3": 1, "bank_free_by_dve4": 1, "bank_free_by_dve5": 1, "act_to_dve": 6},
    "gat0/pe": {"dve_to_pe": 13, "bank_free_by_dve4": 2, "bank_free_by_dve5": 2, "bank_free_by_dve6": 2,
        "bank_free_by_dve0": 3, "bank_free_by_dve1": 3, "bank_free_by_dve2": 2, "bank_free_by_dve3": 2,
        "w_split": 12, "bank_free_by_act3": 2, "bank_free_by_act4": 1, "bank_free_by_act5": 1,
        "bank_free_by_act0": 2, "bank_free_by_act1": 2, "bank_free_by_act2": 2},
    "gat0/act": {"dve_to_act": 17, "tile_for_act": 10, "bank_free_by_act3": 2, "bank_free_by_act4": 1,
        "bank_free_by_act5": 1, "bank_free_by_act0": 2, "bank_free_by_act1": 2, "bank_free_by_act2": 2,
        "rows_free": 1},
    "gat0/dve": {"dve_own": 16, "tile_for_dve": 16, "bank_free_by_dve0": 3, "bank_free_by_dve1": 3,
        "bank_free_by_dve2": 2, "bank_free_by_dve3": 2, "bank_free_by_dve4": 2, "bank_free_by_dve5": 2,
        "act_to_dve": 27, "bank_free_by_dve6": 2, "rows_in": 16},
    "experts0/pe": {"dve_to_pe": 7, "bank_free_by_dve4": 2, "bank_free_by_dve5": 2, "bank_free_by_dve6": 6,
        "bank_free_by_dve0": 2, "bank_free_by_dve1": 2, "bank_free_by_dve2": 2, "bank_free_by_dve3": 2,
        "w_split": 18, "bank_free_by_act3": 1, "bank_free_by_act4": 1, "bank_free_by_act5": 1,
        "bank_free_by_act0": 1, "bank_free_by_act1": 1, "bank_free_by_act2": 1},
    "experts0/act": {"dve_to_act": 6, "tile_for_act": 6, "bank_free_by_act0": 1, "bank_free_by_act1": 1,
        "bank_free_by_act2": 1, "bank_free_by_act3": 1, "bank_free_by_act4": 1, "bank_free_by_act5": 1},
    "experts0/dve": {"tile_for_dve": 18, "bank_free_by_dve0": 2, "bank_free_by_dve1": 2, "bank_free_by_dve2": 2,
        "bank_free_by_dve3": 2, "bank_free_by_dve4": 2, "bank_free_by_dve5": 2, "act_to_dve": 6,
        "bank_free_by_dve6": 6},
    "attention1/pe": {"dve_to_pe": 4, "bank_free_by_dve4": 2, "bank_free_by_dve5": 1, "bank_free_by_dve6": 1,
        "bank_free_by_dve7": 1, "bank_free_by_dve0": 1, "bank_free_by_dve1": 2, "bank_free_by_dve2": 1,
        "bank_free_by_dve3": 1, "w_split": 6, "bank_free_by_act3": 1, "bank_free_by_act0": 1},
    "gat1/pe": {"dve_to_pe": 14, "bank_free_by_dve6": 1, "bank_free_by_dve7": 1, "bank_free_by_dve0": 1,
        "bank_free_by_dve1": 1, "bank_free_by_act2": 1, "bank_free_by_act3": 1, "bank_free_by_act4": 1,
        "bank_free_by_act5": 1},
    "attention1/act": {"dve_to_act": 6, "tile_for_act": 2, "bank_free_by_act3": 1, "bank_free_by_act0": 1},
    "gat1/act": {"tile_for_act": 4, "bank_free_by_act2": 1, "bank_free_by_act3": 1, "bank_free_by_act4": 1,
        "bank_free_by_act5": 1},
    "attention1/dve": {"dve_own": 2, "tile_for_dve": 10, "bank_free_by_dve0": 1, "bank_free_by_dve1": 2,
        "bank_free_by_dve2": 1, "bank_free_by_dve3": 1, "bank_free_by_dve4": 2, "bank_free_by_dve5": 1,
        "act_to_dve": 8, "bank_free_by_dve6": 1, "bank_free_by_dve7": 1},
    "gat1/dve": {"dve_own": 22, "tile_for_dve": 4, "bank_free_by_dve0": 1, "bank_free_by_dve1": 1, "act_to_dve": 8,
        "bank_free_by_dve6": 1, "bank_free_by_dve7": 1},
    "attention2/pe": {"dve_to_pe": 4, "bank_free_by_dve4": 2, "bank_free_by_dve5": 1, "bank_free_by_dve6": 1,
        "bank_free_by_dve7": 1, "bank_free_by_dve0": 1, "bank_free_by_dve1": 2, "bank_free_by_dve2": 1,
        "bank_free_by_dve3": 1, "w_split": 6, "bank_free_by_act3": 1, "bank_free_by_act0": 1},
    "experts2/pe": {"dve_to_pe": 7, "bank_free_by_dve4": 2, "bank_free_by_dve5": 2, "bank_free_by_dve6": 1,
        "bank_free_by_dve0": 2, "bank_free_by_dve1": 2, "bank_free_by_dve2": 2, "bank_free_by_dve3": 2,
        "w_split": 18, "bank_free_by_act3": 1, "bank_free_by_act4": 1, "bank_free_by_act5": 1,
        "bank_free_by_act0": 1, "bank_free_by_act1": 1, "bank_free_by_act2": 1},
    "attention3/pe": {"dve_to_pe": 4, "bank_free_by_dve4": 2, "bank_free_by_dve5": 1, "bank_free_by_dve6": 1,
        "bank_free_by_dve7": 1, "bank_free_by_dve0": 1, "bank_free_by_dve1": 2, "bank_free_by_dve2": 1,
        "bank_free_by_dve3": 1, "w_split": 6, "bank_free_by_act3": 1, "bank_free_by_act0": 1},
    "mlp3/pe": {"dve_to_pe": 6, "bank_free_by_dve4": 1, "bank_free_by_dve5": 1, "bank_free_by_dve0": 1,
        "bank_free_by_dve1": 1, "bank_free_by_dve2": 1, "bank_free_by_dve3": 1, "w_split": 12,
        "bank_free_by_act3": 1, "bank_free_by_act4": 1, "bank_free_by_act5": 1, "bank_free_by_act0": 1,
        "bank_free_by_act1": 1, "bank_free_by_act2": 1},
    "attention2/act": {"dve_to_act": 6, "tile_for_act": 2, "bank_free_by_act3": 1, "bank_free_by_act0": 1},
    "experts2/act": {"dve_to_act": 6, "tile_for_act": 6, "bank_free_by_act3": 1, "bank_free_by_act4": 1,
        "bank_free_by_act5": 1, "bank_free_by_act0": 1, "bank_free_by_act1": 1, "bank_free_by_act2": 1},
    "attention3/act": {"dve_to_act": 6, "tile_for_act": 2, "bank_free_by_act3": 1, "bank_free_by_act0": 1},
    "mlp3/act": {"tile_for_act": 6, "bank_free_by_act3": 1, "bank_free_by_act4": 1, "bank_free_by_act5": 1,
        "bank_free_by_act0": 1, "bank_free_by_act1": 1, "bank_free_by_act2": 1},
    "attention2/dve": {"dve_own": 2, "tile_for_dve": 10, "bank_free_by_dve0": 1, "bank_free_by_dve1": 2,
        "bank_free_by_dve2": 1, "bank_free_by_dve3": 1, "bank_free_by_dve4": 2, "bank_free_by_dve5": 1,
        "act_to_dve": 8, "bank_free_by_dve6": 1, "bank_free_by_dve7": 1},
    "experts2/dve": {"tile_for_dve": 13, "bank_free_by_dve0": 2, "bank_free_by_dve1": 2, "bank_free_by_dve2": 2,
        "bank_free_by_dve3": 2, "bank_free_by_dve4": 2, "bank_free_by_dve5": 2, "act_to_dve": 6,
        "bank_free_by_dve6": 1},
    "attention3/dve": {"dve_own": 2, "tile_for_dve": 10, "bank_free_by_dve0": 1, "bank_free_by_dve1": 2,
        "bank_free_by_dve2": 1, "bank_free_by_dve3": 1, "bank_free_by_dve4": 2, "bank_free_by_dve5": 1,
        "act_to_dve": 8, "bank_free_by_dve6": 1, "bank_free_by_dve7": 1},
    "mlp3/dve": {"tile_for_dve": 6, "bank_free_by_dve0": 1, "bank_free_by_dve1": 1, "bank_free_by_dve2": 1,
        "bank_free_by_dve3": 1, "bank_free_by_dve4": 1, "bank_free_by_dve5": 1, "act_to_dve": 6},
}


def build(nc, t, out, only=None, LOOP_EVENTS={}):
    parts = [p for p in TURNS if only is None or p in only]
    stretches = []
    for p in parts:
        whole, n = p in WHOLE, sum(s[1] for s in stretches)
        if stretches and stretches[-1][2] == whole:
            stretches[-1][1] += TURNS[p]
        else:
            stretches.append([n, TURNS[p], whole, sum(s[1] for s in stretches if s[2] == whole)])
    ctx = ExitStack()
    with ctx:
        def sb(name, shape, dt=F32, where=ctx):
            return where.enter_context(nc.sbuf_tensor(name, shape, dt))

        def sem(name):
            return ctx.enter_context(nc.semaphore(name))

        raw = sb("raw", [P, 2, 3, KC, P])
        w_hi = sb("w_hi", [P, 2, 3, KC, P], F32R)
        w_lo = sb("w_lo", [P, 2, 3, KC, P], F32R)
        x = sb("x", [P, KC, N])
        acc = sb("acc", [P, KC, N])
        scr = sb("scr", [P, KC, N])
        aux = sb("aux", [P, 4, N])
        with ExitStack() as s:
            A, B, H = ((sb(f"{n}_hi", [P, KC, N], F32R, s), sb(f"{n}_lo", [P, KC, N], F32R, s)) for n in "ABH")
        exp_02, head_f, exp_1 = ((sb(f"{n}_0", [P, KC, N]), sb(f"{n}_1", [P, KC, N])) for n in ("exp_02", "head_f", "exp_1"))
        row = sb("row", [P, N])
        rows = sb("rows", [P, 2, D])
        cols = sb("cols", [P, NCOL])
        small = sb("small", [P, KC, NSMALL])
        small_hi = sb("small_hi", [P, KC, NSMALL], F32R)
        small_lo = sb("small_lo", [P, KC, NSMALL], F32R)
        vecs = sb("vecs", [P, NVEC])
        counts = sb("counts", [P, NT, N], I16)
        no_edge = sb("no_edge", [P, NT, N], BF16)
        junk = sb("junk", [1, 16])
        ident = sb("ident", [P, P])
        ones = sb("ones", [P, P])
        ones_r = sb("ones_r", [P, P], F32R)
        ones_b = sb("ones_b", [P, 2], BF16)
        nv = sb("nv", [P, 16, NT])
        al = sb("al", [P, 2, NT, GAT])
        with ExitStack() as s:
            e_hi = sb("e_hi", [P, NT, N], F32R, s)
            e_lo = sb("e_lo", [P, NT, N], F32R, s)
        with ExitStack() as s:
            edge_w = [sb(f"edge_w{u}", [P, NT, N], F32, s) for u in range(2)]
        with ExitStack() as s:
            iota = sb("iota", [P, N], I16, s)
            src_i = sb("src_i", [P, EC], I32, s)
            dst_i = sb("dst_i", [P, EC], I32, s)
            src_f = sb("src_f", [P, EC], F32, s)
            dst_f = sb("dst_f", [P, EC], F32, s)
            hot = sb("hot", [P, 2, 2, N], BF16, s)
        with ExitStack() as s:
            q2 = sb("q2", [P, N], F32, s)
            k2 = sb("k2", [P, N], F32, s)
            orf = sb("orf", [P, 4, ORF], F32, s)
            k_feat = sb("k_feat", [P, NT, ORF], F32, s)
        with ExitStack() as s:
            k_n = sb("k_n", [P, 2, NT, P], F32, s)
            v_n = sb("v_n", [P, 2, NT, P + 2], F32, s)
            q_t = sb("q_t", [P, 2, N], F32, s)
            kv = sb("kv", [P, 2, P], F32, s)
            k_sum = sb("k_sum", [P, 2, P], F32, s)
            same = sb("same", [P, P], F32, s)
        with ExitStack() as s:
            gate_s = sb("gate_s", [P, 12, NT, 8], F32, s)
            comb_n = sb("comb_n", [P, NT, 16], F32, s)
            with ExitStack() as s2:
                comb_t = sb("comb_t", [16, N], F32, s2)
                sel = sb("sel", [16, 3 * D], F32, s2)
                sel_now = sb("sel_now", [16, D], F32, s2)
            with ExitStack() as s2:
                tri = sb("tri", [P, P + 64], F32, s2)
                atom_b = sb("atom_b", [ATOMS, D], F32, s2)
                route = sb("route", [ATOMS, 12], F32, s2)
                cls_w = sb("cls_w", [ATOMS, 8], F32, s2)
                rt = sb("rt", [P, 6, 32], F32, s2)
        ps = ctx.enter_context(nc.psum_tensor("ps", [P, 8, N], F32))
        scr_n = scr[:, :, :].rearrange("p k n -> p (k n)").rearrange("p (m d) -> p m d", m=NT)
        hidden = exp_1[0]
        head_n = [v[:, :, :].rearrange("p k n -> p (k n)")[:, 0:2 * GAT * C2].rearrange(
            "p (m h c) -> p m h c", m=2, h=GAT) for v in head_f]

        loaded, edges_in, rows_in, orf_in, sel_in = (sem(n) for n in ("loaded", "edges_in", "rows_in", "orf_in", "sel_in"))
        setup_done = sem("setup_done")
        pool_done = sem("pool_done")
        raw_in = [sem(f"raw_in{b}") for b in range(6)]
        w_high, w_split, w_used = sem("w_high"), sem("w_split"), sem("w_used")
        raw_used = sem("raw_used")
        tile_for = {"act": sem("tile_for_act"), "dve": sem("tile_for_dve")}
        bank_free = {r: [sem(f"bank_free_by_{r}{b}") for b in range(8)] for r in ("act", "dve")}
        act_to_dve, act_to_pe = sem("act_to_dve"), sem("act_to_pe")
        dve_to_act, dve_to_pe = sem("dve_to_act"), sem("dve_to_pe")
        rows_free, orf_free = sem("rows_free"), sem("orf_free")
        act_own, dve_own = sem("act_own"), sem("dve_own")
        stored = sem("stored")

        block = ctx.enter_context(nc.Block())
        n_setup = 7

        @block.sync
        def _(sp):
            def load(n, b):
                sp.dma_start(raw[:, b // 3, b % 3], t["stream"][bass.ds(n * 6 + b, 1)].rearrange(
                    "o p (k c) -> (o p) k c", k=KC)).then_inc(raw_in[b], 16)

            for b in range(6):
                load(0, b)
            freed = raw_used if stretches[0][2] else w_split
            for n, (first, count, whole, before) in enumerate(stretches):
                if n > 0:
                    for b in range(6):
                        sp.wait_ge(freed, freed_turns * 6 + (b - 5))
                        load(first, b)
                freed, freed_turns = raw_used if whole else w_split, before + count
                with sp.Fori(1, count) as i:
                    for b in range(6):
                        sp.wait_ge(freed, i * 6 + (before * 6 + b - 5))
                        load(i + first, b)

        @block.gpsimd
        def _(pool):
            pool.memset(ident[:, :], 0.0).then_inc(pool_done, 1)
            pool.wait_ge(pool_done, 1)
            pool.affine_select(out=ident[:, :], in_=ident[:, :], compare_op=ALU.not_equal, fill=1.0, base=0,
                               pattern=[[-1, P]], channel_multiplier=1).then_inc(setup_done, 1)
            pool.iota(iota[:, :], pattern=[[1, N]], base=0, channel_multiplier=0).then_inc(setup_done, 1)
            pool.memset(ones[:, :], 1.0).then_inc(setup_done, 1)
            pool.memset(ones_r[:, :].bitcast(F32), 1.0).then_inc(setup_done, 1)
            pool.memset(ones_b[:, :], 1.0).then_inc(setup_done, 1)
            pool.memset(nv[:, :, :], 0.0).then_inc(setup_done, 1)
            pool.memset(hot[:, :, :, :], 0.0).then_inc(setup_done, 1)

            def split(turn, n, b):
                pool.wait_ge(raw_in[b], turn * 16 + 16)
                pool.tensor_tensor(w_hi[:, b // 3, b % 3], raw[:, b // 3, b % 3],
                                   ones[:, :].unsqueeze(1).to_broadcast([P, KC, P]), ALU.mult).then_inc(w_high, 1)
                pool.wait_ge(w_high, n * 6 + (b + 1))
                pool.tensor_tensor(w_lo[:, b // 3, b % 3], raw[:, b // 3, b % 3], w_hi[:, b // 3, b % 3], ALU.subtract)\
                    .then_inc(w_split, 1)

            pool.wait_ge(setup_done, n_setup)
            for first, count, whole, before in stretches:
                if not whole:
                    for b in range(6):
                        if before > 0:
                            pool.wait_ge(w_used, before * 6 + (b - 5))
                        split(first, before, b)
                    with pool.Fori(1, count) as i:
                        for b in range(6):
                            pool.wait_ge(w_used, i * 6 + (before * 6 + b - 5))
                            split(i + first, i + before, b)

        @block.tensor
        def _(pe):
            S = Side(pe, "pe", None, LOOP_EVENTS)
            S.pending = {}

            def use(b):
                if S.pending.get(b):
                    reader = S.pending.pop(b)
                    pe.wait_ge(bank_free[reader][b], S.due(bank_free[reader][b]))

            def done(mm, b, reader):
                mm.then_inc(tile_for[reader], 1)
                S.pending[b] = reader

            def blocks(n=1):
                pe.wait_ge(w_split, S.due(w_split, n))

            owed = [0]

            def blocks_used(n=1, last=True):
                if not last:
                    owed[0] += n
                    return
                pe.matmul(ps[0:2, 7, 0:2], ones_b[:, :], ones_b[:, :], start=True, stop=True,
                          skip_group_check=True).then_inc(w_used, n)

            def whole_block(turn, b):
                pe.wait_ge(raw_in[b], turn * 16 + 16)

            def whole_block_used():
                pe.matmul(ps[0:2, 7, 0:2], ones_b[:, :], ones_b[:, :], start=True, stop=True,
                          skip_group_check=True).then_inc(raw_used, 1)

            def first_turn(p):
                return sum(TURNS[q] for q in parts[:parts.index(p)])

            def mm3(o, wh, wl, xh, xl, first, last):
                mm = pe.matmul(o, wh, xh, start=first, stop=False, skip_group_check=True)
                if owed[0]:
                    mm.then_inc(w_used, owed[0])
                    owed[0] = 0
                pe.matmul(o, wh, xl, start=False, stop=False, skip_group_check=True)
                return pe.matmul(o, wl, xh, start=False, stop=last, skip_group_check=True)

            def tile_t(b, g, j, X, reader, chunks=range(KC), c0=0, c1=N, since=None):
                use(b)
                for n, k in enumerate(chunks):
                    if since:
                        pe.wait_ge(dve_to_pe, since[k])
                    mm = mm3(ps[:, b, c0:c1], w_hi[:, g, j, k], w_lo[:, g, j, k], X[0][:, k, c0:c1], X[1][:, k, c0:c1],
                             n == 0, n == len(chunks) - 1)
                done(mm, b, reader)

            def chunks_due():
                return [S.due(dve_to_pe) for k in range(KC)]

            def turn_t(X, reader, since=None, last=True):
                if since:
                    blocks(3)
                    for j in range(3):
                        use(j)
                    for k in range(KC):
                        pe.wait_ge(dve_to_pe, since[k])
                        for j in range(3):
                            mm = mm3(ps[:, j], w_hi[:, 0, j, k], w_lo[:, 0, j, k], X[0][:, k], X[1][:, k], k == 0, k == KC - 1)
                            if k == KC - 1:
                                done(mm, j, reader)
                    blocks_used(3, False)
                for g in range(1 if since else 0, 2):
                    for j in range(3):
                        blocks()
                        tile_t(3 * g + j, g, j, X, reader)
                        blocks_used(1, last and g == 1 and j == 2)

            def turn_n(X, reader, mid=None, since=None, last=True):
                if since:
                    blocks(3)
                    for m in range(NT):
                        use(m)
                    for k in range(KC):
                        pe.wait_ge(dve_to_pe, since[k])
                        for m in range(NT):
                            c = slice(m * P, m * P + P)
                            mm = mm3(ps[:, m, 0:384].rearrange("p (j c) -> p j c", j=3), X[0][:, k, c], X[1][:, k, c],
                                     w_hi[:, 0, :, k], w_lo[:, 0, :, k], k == 0, k == KC - 1)
                            if k == KC - 1:
                                done(mm, m, reader)
                    if mid:
                        mid(0, NT - 1)
                    blocks_used(3, False)
                for g in range(1 if since else 0, 2):
                    blocks(3)
                    for m in range(NT):
                        b = (4 * g + m) % 6
                        use(b)
                        o = ps[:, b, 0:384].rearrange("p (j c) -> p j c", j=3)
                        c = slice(m * P, m * P + P)
                        for k in range(KC):
                            mm3_ = mm3(o, X[0][:, k, c], X[1][:, k, c], w_hi[:, g, :, k], w_lo[:, g, :, k],
                                       k == 0, k == KC - 1)
                        done(mm3_, b, reader)
                        if mid:
                            mid(g, m)
                    blocks_used(3, last and g == 1)

            def graph_t(reader):
                hn = [B[h][:, :, :].rearrange("p k n -> p (k n)").rearrange("p (m d) -> p m d", m=NT) for h in range(2)]
                for j in range(KC):
                    use(j)
                    for m in range(NT):
                        mm = mm3(ps[:, j], hn[0][:, m, j * P:j * P + P], hn[1][:, m, j * P:j * P + P],
                                 e_hi[:, m], e_lo[:, m], m == 0, m == NT - 1)
                    done(mm, j, reader)

            def norm(since=None):
                use(6)
                for j in range(KC):
                    if since:
                        pe.wait_ge(dve_to_pe, since[j])
                    elif j in S.pending:
                        pe.wait_ge(bank_free["dve"][j], S.seen.get(bank_free["dve"][j].name, 0) + 1)
                    mm = pe.matmul(ps[:, 6], ones[:, :], norm_src[0][:, j], start=j == 0, stop=j == KC - 1,
                                   skip_group_check=True)
                done(mm, 6, "dve")
                use(7)
                for j in range(KC):
                    pe.wait_ge(act_to_pe, S.due(act_to_pe))
                    mm = pe.matmul(ps[:, 7], ones[:, :], aux[:, j % 4], start=j == 0, stop=j == KC - 1,
                                   skip_group_check=True)
                    if j < 2:
                        mm.then_inc(tile_for["act"], 1)
                done(mm, 7, "dve")
                normed[:] = chunks_due()

            norm_src, normed = [x], [0] * KC

            def bcast(b, reader, block=0):
                pe.wait_ge(dve_to_pe, S.due(dve_to_pe))
                use(b)
                done(pe.matmul(ps[:, b], ones[:, :], aux[:, :, block * P:block * P + P], start=True, stop=True), b, reader)

            def gat_rows(g):
                if g == 0:
                    bcast(6, "dve")
                else:
                    bcast(2, "act")
                    bcast(3, "act", 1)

            def gat_den():
                use(6)
                for m in range(NT):
                    pe.wait_ge(dve_to_pe, S.due(dve_to_pe))
                    pe.matmul(ps[:, 6], ones_r[:, :], e_hi[:, m], start=m == 0, stop=False, skip_group_check=True)
                    mm = pe.matmul(ps[:, 6], ones_r[:, :], e_lo[:, m], start=False, stop=m == NT - 1,
                                   skip_group_check=True)
                done(mm, 6, "dve")

            def linear_attention(X, what):
                with S.loop(what, 3) as i:
                    for g in range(2):
                        blocks(2)
                        for m in range(NT):
                            b = 3 * g + 1 + m // 2
                            if m % 2 == 0:
                                use(b)
                            c = slice(m * P, m * P + P)
                            o = ps[:, b, (m % 2) * 256:(m % 2) * 256 + 256].rearrange("p (j c) -> p j c", j=2)
                            for k in range(KC):
                                if g == m == 0:
                                    pe.wait_ge(dve_to_pe, normed[k])
                                mm = mm3(o, X[0][:, k, c], X[1][:, k, c], w_hi[:, g, 0:2, k], w_lo[:, g, 0:2, k],
                                         k == 0, k == KC - 1)
                            if m % 2 == 1:
                                done(mm, b, "dve")
                        blocks_used(2, False)
                        blocks()
                        tile_t(3 * g, g, 2, X, "act")
                        blocks_used()
                    for g in range(2):
                        pe.wait_ge(dve_to_pe, S.due(dve_to_pe))
                        use(6 + g)
                        for m in range(NT):
                            mm = pe.matmul(ps[:, 6 + g, 0:P + 2], k_n[:, g, m], v_n[:, g, m], start=m == 0, stop=m == NT - 1,
                                           skip_group_check=True)
                        done(mm, 6 + g, "dve")
                    for g in range(2):
                        pe.wait_ge(bank_free["dve"][6 + g], S.coming(bank_free["dve"][6 + g]))
                        use(3 * g)
                        done(pe.matmul(ps[:, 3 * g], kv[:, g], q_t[:, g], start=True, stop=True), 3 * g, "dve")
                        use(3 * g + 1)
                        done(pe.matmul(ps[:, 3 * g + 1], k_sum[:, g], q_t[:, g], start=True, stop=True), 3 * g + 1, "dve")
                    S.due(dve_to_pe, 2)
                n = S.seen[dve_to_pe.name]
                return [n - 4] * 4 + [n - 1, n]

            def performer(X, what):
                for b in range(3, 8):
                    use(b)
                with S.loop(what, 3) as i:
                    for g in range(2):
                        blocks()
                        tile_t(0, g, 0, X, "dve", since=normed if g == 0 else None)
                        blocks_used(1, False)
                        blocks()
                        tile_t(1, g, 1, X, "dve")
                        blocks_used(1, False)
                        blocks()
                        use(2)
                        for m in range(NT):
                            c = slice(m * P, m * P + P)
                            for k in range(KC):
                                mm = mm3(ps[:, 2, c], X[0][:, k, c], X[1][:, k, c], w_hi[:, g, 2, k], w_lo[:, g, 2, k],
                                         k == 0, k == KC - 1)
                        done(mm, 2, "dve")
                        blocks_used()
                        for h in range(2):
                            w = orf[:, 2 * g + h]
                            pe.wait_ge(act_to_pe, S.due(act_to_pe))
                            for m in range(NT):
                                use(3 + m % 2)
                                done(pe.matmul(ps[:, 3 + m % 2, 0:ORF], k2[:, m * P:m * P + P], w, start=True, stop=True),
                                     3 + m % 2, "act")
                            for r in range(3):
                                use(5 + r % 2)
                                done(pe.matmul(ps[:, 5 + r % 2], w[:, r * P:r * P + P], q2[:, :], start=True, stop=True),
                                     5 + r % 2, "act")
                            for b in (3, 4, 5, 6, 7):
                                use(b)
                            if h == 0:
                                pe.wait_ge(dve_to_pe, S.due(dve_to_pe))
                            vh = aux[:, 0:2].rearrange("p a n -> p (a n)")[:, 0:NT * 2 * 66].rearrange(
                                "p (m h c) -> p m h c", m=NT, h=2)
                            for r in range(3):
                                for m in range(NT):
                                    mm = pe.matmul(ps[:, 7, r * 68:r * 68 + 66], k_feat[:, m, r * P:r * P + P],
                                                   vh[:, m, h], start=m == 0, stop=m == NT - 1, skip_group_check=True)
                            done(mm, 7, "dve")
                            use(7)
                            ktv = aux[:, 2, 0:ORF].rearrange("p (r c) -> p r c", r=3)
                            use(h)
                            for r in range(3):
                                mm = pe.matmul(ps[:, h], ktv[:, r], scr[:, 3 + r], start=r == 0, stop=r == 2,
                                               skip_group_check=True)
                            done(mm, h, "dve")
                        S.due(dve_to_pe)
                n = S.seen[dve_to_pe.name]
                return [n - 4] * 4 + [n - 2, n]

            def gelu_mlp(X, what):
                with S.loop(what, 4) as i:
                    turn_t(X, "act", normed, last=False)
                    turn_t(H, "dve", chunks_due())

            def router_n(X, c0, n):
                use(6)
                for m in range(NT):
                    for k in range(KC):
                        if m == 0:
                            pe.wait_ge(dve_to_pe, normed[k])
                        c = slice(m * P, m * P + P)
                        mm = mm3(ps[:, 6, m * 8:m * 8 + n], X[0][:, k, c], X[1][:, k, c], small_hi[:, k, c0:c0 + n],
                                 small_lo[:, k, c0:c0 + n], k == 0, k == KC - 1)
                done(mm, 6, "dve")

            def combine_rows():
                pe.wait_ge(dve_to_pe, S.due(dve_to_pe))
                use(6)
                for m in range(NT):
                    mm = pe.transpose(ps[0:16, 6, m * P:m * P + P], comb_n[:, m], ident[:, :])
                done(mm, 6, "dve")

            def experts(X, what, n, per_chunk):
                with S.loop(what, n) as i:
                    turn_t(X, "act", normed, last=False)
                    pe.wait_ge(dve_to_pe, S.due(dve_to_pe))
                    if not per_chunk:
                        use(6)
                        done(pe.matmul(ps[:, 6], sel_now[:, 0:P], comb_t[:, :], start=True, stop=True), 6, "dve")
                    for g in range(2):
                        for j in range(3):
                            blocks()
                            f = 3 * g + j
                            tile_t(f, g, j, X, "dve")
                            if per_chunk:
                                use(6)
                                done(pe.matmul(ps[:, 6], sel_now[:, f * P:f * P + P], comb_t[:, :], start=True, stop=True),
                                     6, "dve")
                            blocks_used(1, False)
                    turn_t(H, "dve", chunks_due())

            def transposes(src, reader, dst_tile_free=True):
                for j in range(KC):
                    use(j)
                    for m in range(NT):
                        mm = pe.transpose(ps[:, j, m * P:m * P + P], src(m, j), ident[:, :])
                    done(mm, j, reader)

            def degrees():
                pe.wait_ge(dve_to_pe, S.due(dve_to_pe))
                use(6)
                for m in range(NT):
                    mm = pe.matmul(ps[:, 6], ones[:, :], aux[:, m], start=m == 0, stop=m == NT - 1, skip_group_check=True)
                done(mm, 6, "dve")

            def to_nodes(src):
                for g in range(2):
                    for m in range(NT):
                        b = (4 * g + m) % 6
                        use(b)
                        for c in range(3):
                            mm = pe.transpose(ps[:, b, c * P:c * P + P], src[:, 3 * g + c, m * P:m * P + P], ident[:, :])
                        done(mm, b, "act")
                        S.pending[b] = "dve"

            pe.wait_ge(setup_done, n_setup)
            for m in range(NT):
                mm = pe.matmul(ps[:, m], hot[:, 1, 0, 0:P], hot[:, 1, 0, :], start=True, stop=False, skip_group_check=True)
                if m >= 2:
                    mm.then_inc(tile_for["dve"], 1)
            with S.loop("edges", EC // 2) as i:
                for c in range(2):
                    pe.wait_ge(dve_to_pe, S.due(dve_to_pe))
                    for m in range(NT):
                        mm = pe.matmul(ps[:, m], hot[:, c, 0, m * P:m * P + P], hot[:, c, 1, :], start=False, stop=False,
                                       skip_group_check=True)
                    mm.then_inc(tile_for["dve"], 1)
            for m in range(NT):
                S.pending[m] = "dve"
            pe.wait_ge(dve_to_pe, S.due(dve_to_pe, NT))
            for m in range(NT):
                use(4 + m % 2)
                for k in range(NT):
                    mm = pe.transpose(ps[:, 4 + m % 2, k * P:k * P + P], aux[:, k, m * P:m * P + P], ident[:, :])
                done(mm, 4 + m % 2, "dve")

            def unpend():
                for b in list(S.pending):
                    use(b)

            def part(p):
                return p in parts

            def norm_of(src, since=None):
                norm_src[0] = src
                norm(since)

            ran = lambda p: p in parts
            pe.wait_ge(loaded, 64)
            norm_of(x)
            if part("mix0"):
                norm_of(acc, list(normed))
                turn_t(H, "dve", performer(B, "performer"))
                norm_of(acc)
                gelu_mlp(B, "mlp0")
            if part("gnn0"):
                turn_n(A, "act", since=normed)
                gat_rows(0)
                gat_rows(1)
                gat_den()
                graph_t("dve")
                unpend()
                with S.loop("gat0", GAT - 1) as i:
                    head = chunks_due()
                    turn_n(A, "act", last=False)
                    pe.wait_ge(dve_to_pe, head[-1])
                    turn_n(H, "dve", lambda g, m: gat_rows(g) if (g, m) in ((0, 1), (1, 0)) else None)
                    gat_den()
                    graph_t("dve")
                    unpend()
                turn_n(H, "dve", since=chunks_due())
                gat_rows(0)
                gat_rows(1)
                gat_den()
                graph_t("dve")
            if part("ffn0"):
                norm_of(x)
                router_n(A, R0, 8)
                combine_rows()
                experts(A, "experts0", 2, True)
                for j in range(2):
                    blocks()
                    tile_t(j, 0, j, A, "act")
                    blocks_used(1, False)
                pe.wait_ge(dve_to_pe, S.due(dve_to_pe))
                for j in range(2):
                    blocks()
                    tile_t(j, (2 + j) // 3, (2 + j) % 3, A, "dve")
                    use(6)
                    done(pe.matmul(ps[:, 6], sel_now[:, j * P:j * P + P], comb_t[:, :], start=True, stop=True), 6, "dve")
                    blocks_used(1, False)
                blocks(2)
                for f in range(KC):
                    use(f)
                    for c in range(2):
                        if f == 0:
                            pe.wait_ge(dve_to_pe, S.due(dve_to_pe))
                        w = [v[:, 1, 1 + f // 3, f % 3 * 2 + c] for v in (w_hi, w_lo)]
                        mm = mm3(ps[:, f], w[0], w[1], H[0][:, c], H[1][:, c], c == 0, c == 1)
                    done(mm, f, "dve")
                blocks_used(2)
            if ran("mix1") or ran("gnn1"):
                norm_of(x)
            if part("mix1"):
                norm_of(acc, list(normed))
                turn_t(H, "dve", linear_attention(B, "attention1"))
            if part("gnn1"):
                turn_n(A, "act", since=normed)
                pe.wait_ge(dve_to_pe, S.due(dve_to_pe))
                unpend()
                with S.loop("gat1", GAT // 2) as i:
                    for u in range(2):
                        bcast(6 + u, "dve", 2 * u)
                    for u in range(2):
                        for r in range(2):
                            bcast(2 + 2 * u + r, "act", 2 * u + r)
                    for u in range(2):
                        use(u)
                        for k in range(NT):
                            pe.wait_ge(dve_to_pe, S.due(dve_to_pe))
                        for m in range(NT):
                            for k in range(NT):
                                mm = pe.matmul(ps[:, u, m * P:m * P + C2], edge_w[u][:, k, m * P:m * P + P],
                                               head_n[k // 2][:, k % 2, bass.ds(i * 2 + u, 1)].rearrange("p o c -> p (o c)"),
                                               start=k == 0, stop=k == NT - 1, skip_group_check=True)
                        done(mm, u, "dve")
                    unpend()
                pe.wait_ge(dve_to_pe, S.due(dve_to_pe))
                acc_n = acc[:, :, :].rearrange("p k n -> p (k n)").rearrange("p (m d) -> p m d", m=NT)
                transposes(lambda m, j: acc_n[:, m, j * P:j * P + P], "act")
                turn_n(H, "act", since=chunks_due())
                gat_rows(0)
                gat_rows(1)
                gat_den()
                graph_t("dve")
            if part("ffn1"):
                norm_of(x)
                unpend()
                pe.wait_ge(dve_to_pe, S.due(dve_to_pe))
                for k in range(KC):
                    mm = pe.matmul(ps[:, 6, 0:30], ones[:, :], aux[:, k % 4, (k // 4) * 32:(k // 4) * 32 + 30],
                                   start=k == 0, stop=k == KC - 1, skip_group_check=True)
                done(mm, 6, "dve")
                turn = first_turn("ffn1")
                for n in range(2):
                    for f in range(KC):
                        q = 6 * n + f
                        c = slice(0, N if q < 2 else 8)
                        whole_block(turn + n, f)
                        use(f)
                        for k in range(KC):
                            if q == 0:
                                pe.wait_ge(dve_to_pe, normed[k])
                            mm = pe.matmul(ps[:, f, c], raw[:, f // 3, f % 3, k], acc[:, k, c], start=k == 0,
                                           stop=k == KC - 1, skip_group_check=True)
                        done(mm, f, "act")
                        whole_block_used()
                pe.wait_ge(dve_to_pe, S.due(dve_to_pe))
                for n in range(2):
                    for f in range(KC):
                        whole_block(turn + 2 + n, f)
                        if n == 0:
                            use(f)
                            for k in range(2):
                                if f == 0:
                                    pe.wait_ge(act_to_pe, S.due(act_to_pe))
                                mm = pe.matmul(ps[:, f], raw[:, f // 3, f % 3, k], scr[:, k], start=k == 0, stop=k == 1,
                                               skip_group_check=True)
                            done(mm, f, "dve")
                            if f == 0:
                                use(6)
                        o = ps[:, 6, (6 * n + f) * 8:(6 * n + f) * 8 + 8]
                        for k in range(2, KC) if n == 0 else range(KC):
                            mm = pe.matmul(o, raw[:, f // 3, f % 3, k], scr[:, 3, (6 * n + k) * 8 - 16:(6 * n + k) * 8 - 8],
                                           start=k == (2 if n == 0 else 0), stop=k == KC - 1, skip_group_check=True)
                        whole_block_used()
                for f in range(KC):
                    mm = pe.matmul(ps[:, 6, 96 + f * 8:104 + f * 8], atom_b[:, f * P:f * P + P], cls_w[:, :], start=True,
                                   stop=True, skip_group_check=True)
                done(mm, 6, "dve")
            if ran("gnn2") or ran("mix2"):
                norm_of(x)
            if part("gnn2"):
                turn_n(A, "act", lambda g, m: degrees() if (g, m) == (0, NT - 1) else None, normed)
                pe.wait_ge(dve_to_pe, S.due(dve_to_pe))
                graph_t("dve")
            if part("mix2"):
                turn_t(H, "dve", linear_attention(A, "attention2"))
            if part("ffn2"):
                norm_of(x)
                router_n(A, R2, 4)
                combine_rows()
                experts(A, "experts2", 8, False)
            if ran("gnn3") or ran("mix3"):
                norm_of(x)
            if part("gnn3"):
                turn_n(A, "act", lambda g, m: degrees() if (g, m) == (0, NT - 1) else None, normed)
                pe.wait_ge(dve_to_pe, S.due(dve_to_pe))
                graph_t("dve")
            if part("mix3"):
                norm_of(acc, list(normed))
                turn_t(H, "dve", linear_attention(B, "attention3"))
                norm_of(acc)
                gelu_mlp(B, "mlp3")
            if part("ffn3"):
                norm_of(x)
                router_n(A, R3, 8)
                to_nodes(acc)
                pe.wait_ge(dve_to_pe, S.due(dve_to_pe))
                use(6)
                for m in range(NT):
                    for k in range(m + 1):
                        mm = pe.matmul(ps[:, 6, m * 8:m * 8 + 8], tri[:, 0:P] if k == m else ones[:, :], gate_s[:, 7, k],
                                       start=k == 0, stop=k == m, skip_group_check=True)
                done(mm, 6, "dve")
                pe.wait_ge(dve_to_pe, S.due(dve_to_pe))
                for j in range(KC):
                    use(j)
                    for h in range(2):
                        bn = B[h][:, :, :].rearrange("p k n -> p (k n)").rearrange("p (m d) -> p m d", m=NT)
                        for m in range(NT):
                            mm = pe.matmul(ps[:, j], bn[:, m, j * P:j * P + P], e_hi[:, m], start=h == 0 and m == 0,
                                           stop=h == 1 and m == NT - 1, skip_group_check=True)
                    done(mm, j, "act")
                turn = first_turn("ffn3")
                for n in range(3):
                    for f in range(KC):
                        q = 6 * n + f
                        whole_block(turn + n, f)
                        if q < 16:
                            use(f)
                            c = slice(64 * (q // 2), 64 * (q // 2) + 64)
                            for k in range(KC):
                                if q == 0:
                                    pe.wait_ge(act_to_pe, S.due(act_to_pe))
                                mm = pe.matmul(ps[:, f, c], raw[:, f // 3, f % 3, k], acc[:, k, c], start=k == 0,
                                               stop=k == KC - 1, skip_group_check=True)
                            done(mm, f, "act")
                        whole_block_used()
                for n in range(3):
                    if n == 0:
                        pe.wait_ge(act_to_pe, S.due(act_to_pe))
                    for f in range(KC):
                        whole_block(turn + 3 + n, f)
                        use(f)
                        for e in range(3 * n, min(3 * n + 3, 8)):
                            for h in range(2):
                                k, q = 2 * (e - 3 * n) + h, 2 * e + h
                                mm = pe.matmul(ps[:, f, e * 64:e * 64 + 64], raw[:, f // 3, f % 3, k],
                                               hidden[:, q // 8, q % 8 * 64:q % 8 * 64 + 64], start=h == 0, stop=h == 1,
                                               skip_group_check=True)
                        done(mm, f, "act")
                        whole_block_used()
                for m in range(NT):
                    use(m)
                    for k in range(NT):
                        mm = pe.transpose(ps[:, m, k * P:k * P + P], aux[:, k, m * P:m * P + P], ident[:, :])
                    done(mm, m, "act")
                    S.pending[m] = "dve"
                pe.wait_ge(act_to_pe, S.due(act_to_pe))
                to_nodes(scr)
                pe.wait_ge(dve_to_pe, S.due(dve_to_pe))
                graph_t("dve")

        @block.scalar
        def _(act):
            S = Side(act, "act", act_own, LOOP_EVENTS)
            first_rows = [True]
            marks = [0]

            def freed(ins, b):
                ins.then_inc(bank_free["act"][b], 1)
                act.wait_ge(bank_free["act"][b], S.due(bank_free["act"][b]))

            def mark(sem):
                marks[0] = (marks[0] + 1) % 7
                act.activation(junk[:, marks[0]:marks[0] + 1], ones[0:1, 0:1], ACT.Copy).then_inc(sem, 1)

            def load_rows(n):
                if not first_rows[0]:
                    act.wait_ge(rows_free, S.due(rows_free))
                first_rows[0] = False
                n = bass.ds(n, 1)
                act.dma_start(rows[:, :, :], t["rows"][n].rearrange("o a d -> (o a) d").partition_broadcast(P))\
                   .then_inc(rows_in, 16)

            def col(name, n=0):
                c = COL[name] + n
                return cols[:, c:c + 1] if isinstance(c, int) else cols[:, bass.ds(c, 1)]

            def high(dst, src):
                act.wait_ge(dve_to_act, S.due(dve_to_act))
                act.copy(dst, src).then_inc(act_to_dve, 1)

            def norm(src, dst, X, beta=None):
                for j in range(KC):
                    act.wait_ge(dve_to_act, S.due(dve_to_act))
                    if j >= 4:
                        act.wait_ge(tile_for["act"], S.due(tile_for["act"]))
                    act.activation(aux[:, j % 4], scr[:, j], ACT.Square).then_inc(act_to_pe, 1)
                act.wait_ge(dve_to_act, S.due(dve_to_act))
                act.activation(row[:, :], row[:, :], ACT.Sqrt).then_inc(act_to_dve, 1)
                if X:
                    for j in range(KC):
                        act.wait_ge(dve_to_act, S.due(dve_to_act))
                        bias = {"bias": col(beta, j)} if beta else {}
                        act.activation(X[0][:, j], dst[:, j], ACT.Identity, **bias).then_inc(act_to_dve, 1)

            def features_n():
                sn = scr[:, :, :].rearrange("p k n -> p (k n)").rearrange("p (m d) -> p m d", m=NT)
                bn = B[0][:, :, :].rearrange("p k n -> p (k n)").rearrange("p (m d) -> p m d", m=NT)
                for g in range(2):
                    for m in range(NT):
                        c = slice(384 * g, 384 * g + 384)
                        b = (4 * g + m) % 6
                        act.wait_ge(tile_for["act"], S.due(tile_for["act"]))
                        freed(act.copy(sn[:, m, c], ps[:, b, 0:384]), b)
                        act.copy(bn[:, m, c], sn[:, m, c]).then_inc(act_to_dve, 1)

            def edge_weights():
                act.wait_ge(tile_for["act"], S.due(tile_for["act"], 2))
                for m in range(NT):
                    q = 2 * (m % 2)
                    e1 = act.activation(aux[:, q], ps[:, 2], ACT.Exp, bias=nv[:, 0, m:m + 1])
                    if m == NT - 1:
                        freed(e1, 2)
                    e2 = act.activation(aux[:, q + 1], ps[:, 3], ACT.Exp, bias=nv[:, 3, m:m + 1])
                    if m < NT - 1:
                        e2.then_inc(act_to_dve, 1)
                    else:
                        freed(e2, 3)
                    if m >= 1:
                        high(e_hi[:, m - 1], scr[:, m - 1])
                high(e_hi[:, NT - 1], scr[:, NT - 1])

            def head_output(bias, from_psum=False):
                for s in range(KC + 1):
                    if s < KC:
                        q = 2 * (s % 2)
                        if from_psum:
                            act.wait_ge(tile_for["act"], S.due(tile_for["act"]))
                            src = ps[:, s]
                        else:
                            act.wait_ge(dve_to_act, S.due(dve_to_act))
                            src = scr[:, s]
                        act.activation(aux[:, q], src, ACT.Exp, bias=bias(s))
                        r = act.activation(aux[:, q + 1], src, ACT.Relu, bias=bias(s))
                        if from_psum:
                            freed(r, s)
                            mark(act_to_dve)
                        else:
                            r.then_inc(act_to_dve, 1)
                    if s >= 1:
                        act.wait_ge(dve_to_act, S.due(dve_to_act))
                        act.activation(H[0][:, s - 1], scr[:, s - 1], ACT.Identity, bias=-1.0).then_inc(act_to_dve, 1)

            def performer(what):
                with S.loop(what, 3) as i:
                    act.dma_start(orf[0:HD, :, :], t["orf"][bass.ds(i, 1)].rearrange("o c (h r) -> (o c) h r", h=4))\
                       .then_inc(orf_in, 16)
                    act.wait_ge(orf_in, S.due(orf_in, 16))
                    for g in range(2):
                        act.wait_ge(dve_to_act, S.due(dve_to_act))
                        for h in range(2):
                            r = slice(h * HD, h * HD + HD)
                            act.copy(q2[0:HD, :], scr[r, 0])
                            act.activation(q2[HD:P, :], scr[r, 0], ACT.Square)
                            act.copy(k2[0:HD, :], scr[r, 1])
                            act.activation(k2[HD:P, :], scr[r, 1], ACT.Square).then_inc(act_to_pe, 1)
                            for m in range(NT):
                                act.wait_ge(tile_for["act"], S.due(tile_for["act"]))
                                freed(act.activation(k_feat[:, m], ps[:, 3 + m % 2, 0:ORF], ACT.Exp), 3 + m % 2)
                            for m in range(3):
                                act.wait_ge(tile_for["act"], S.due(tile_for["act"]))
                                freed(act.activation(scr[:, 3 + m], ps[:, 5 + m % 2], ACT.Exp), 5 + m % 2)
                        high(H[0][:, bass.ds(2 * i + g, 1)].rearrange("p o n -> p (o n)"), aux[:, 3])

            def linear_attention(what, bq):
                with S.loop(what, 3) as i:
                    for g in range(2):
                        for half in range(2):
                            act.wait_ge(dve_to_act, S.due(dve_to_act))
                            act.activation(scr[:, 2 + half, 0:256], aux[:, half, 0:256], ACT.Exp)
                            act.activation(scr[:, 2 + half, 256:512], aux[:, half, 0:256], ACT.Relu)\
                               .then_inc(act_to_dve, 1)
                        b = col(bq, i * 2 + g)
                        act.wait_ge(tile_for["act"], S.due(tile_for["act"]))
                        act.activation(scr[:, 0], ps[:, 3 * g], ACT.Exp, bias=b)
                        freed(act.activation(scr[:, 1], ps[:, 3 * g], ACT.Relu, bias=b), 3 * g)
                        mark(act_to_dve)
                    for g in range(2):
                        high(H[0][:, bass.ds(2 * i + g, 1)].rearrange("p o n -> p (o n)"), aux[:, 2 + g])

            def gelu_mlp(what, bias, func):
                with S.loop(what, 4) as i:
                    for j in range(KC):
                        act.wait_ge(tile_for["act"], S.due(tile_for["act"]))
                        freed(act.activation(scr[:, j], ps[:, j], func, bias=col(bias, i * KC + j)), j)
                        act.copy(H[0][:, j], scr[:, j]).then_inc(act_to_dve, 1)

            def experts(what, n):
                with S.loop(what, n) as i:
                    gated_high(KC)

            def gated_high(chunks):
                for j in range(chunks):
                    act.wait_ge(tile_for["act"], S.due(tile_for["act"]))
                    freed(act.activation(scr[:, j], ps[:, j], ACT.Silu), j)
                for j in range(chunks):
                    high(H[0][:, j], scr[:, j])

            def router_exp():
                act.wait_ge(dve_to_act, S.due(dve_to_act))
                act.activation(gate_s[:, 1], gate_s[:, 0], ACT.Exp).then_inc(act_to_dve, 1)

            act.dma_start(src_i[:, :], t["src"]).then_inc(edges_in, 16)
            act.dma_start(dst_i[:, :], t["dst"]).then_inc(edges_in, 16)
            act.dma_start(x[:, :, :], t["x"]).then_inc(loaded, 16)
            act.dma_start(cols[:, :], t["cols"]).then_inc(loaded, 16)
            act.dma_start(small[:, :, :], t["small"]).then_inc(loaded, 16)
            act.dma_start(vecs[:, :], t["vecs"].partition_broadcast(P)).then_inc(loaded, 16)
            act.wait_ge(loaded, 64)
            act.wait_ge(setup_done, n_setup)
            S.step(act.copy(small_hi[:, :, :], small[:, :, :]))
            mark(act_to_dve)
            norm(x, acc, A)
            if "mix0" in parts:
                load_rows(ROW_KV0)
                norm(acc, scr, B, "L0_mix_ln1_b")
                performer("performer")
                norm(acc, scr, B, "L0_mix_ln2_b")
                gelu_mlp("mlp0", "L0_mix_fc1_b", ACT.Gelu_apprx_tanh)
            if "gnn0" in parts:
                load_rows(0)
                features_n()
                edge_weights()
                head_output(lambda j: col("L0_gnn_b1", j))
                with S.loop("gat0", GAT - 1) as i:
                    load_rows(i + 1)
                    act.wait_ge(dve_to_act, S.due(dve_to_act))
                    features_n()
                    edge_weights()
                    head_output(lambda j: col("L0_gnn_b1", i * KC + KC + j))
                load_rows(ROW_L0B)
                act.wait_ge(dve_to_act, S.due(dve_to_act))
                an = acc[:, :, :].rearrange("p k n -> p (k n)").rearrange("p (m d) -> p m d", m=NT)
                bn = B[0][:, :, :].rearrange("p k n -> p (k n)").rearrange("p (m d) -> p m d", m=NT)
                for m in range(NT):
                    act.copy(bn[:, m], an[:, m]).then_inc(act_to_dve, 1)
                edge_weights()
            if "ffn0" in parts:
                norm(x, acc, A)
                act.wait_ge(dve_to_act, S.due(dve_to_act))
                act.activation(gate_s[:, 2], gate_s[:, 1], ACT.Exp, scale=-1.0).then_inc(act_to_dve, 1)
                act.wait_ge(dve_to_act, S.due(dve_to_act))
                S.step(act.activation(gate_s[:, 4], gate_s[:, 3], ACT.Ln))
                mark(act_to_dve)
                act.wait_ge(dve_to_act, S.due(dve_to_act))
                act.activation(gate_s[:, 6], gate_s[:, 5], ACT.Sqrt).then_inc(act_to_dve, 1)
                act.dma_start(sel[0:16, :], t["sel0"]).then_inc(sel_in, 16)
                experts("experts0", 2)
                gated_high(2)

            if "mix1" in parts or "gnn1" in parts:
                norm(x, acc, A)
            if "mix1" in parts:
                load_rows(ROW_KV1)
                norm(acc, scr, B, "L1_mix_ln_beta")
                linear_attention("attention1", "zero")
            if "gnn1" in parts:
                load_rows(ROW_L1)
                act.wait_ge(dve_to_act, S.due(dve_to_act))
                for g in range(2):
                    for m in range(NT):
                        b = (4 * g + m) % 6
                        act.wait_ge(tile_for["act"], S.due(tile_for["act"]))
                        freed(act.copy(head_n[m // 2][:, m % 2, 4 * g:4 * g + 4, 0:C1],
                                       ps[:, b, 0:384].rearrange("p (h c) -> p h c", h=4)), b)
                        mark(act_to_dve)
                with S.loop("gat1", GAT // 2) as i:
                    for u in range(2):
                        act.wait_ge(tile_for["act"], S.due(tile_for["act"], 2))
                        for m in range(NT):
                            e1 = act.activation(exp_1[u][:, m], ps[:, 2 + 2 * u], ACT.Exp, bias=nv[:, 8 * u, m:m + 1])
                            e2 = act.activation(exp_02[u][:, m], ps[:, 3 + 2 * u], ACT.Exp, bias=nv[:, 8 * u + 3, m:m + 1])
                            if m < NT - 1:
                                e2.then_inc(act_to_dve, 1)
                        e1.then_inc(bank_free["act"][2 + 2 * u], 1)
                        freed(e2, 3 + 2 * u)
                        act.wait_ge(bank_free["act"][2 + 2 * u], S.due(bank_free["act"][2 + 2 * u]))
                        mark(act_to_dve)
                head_output(lambda j: col("L1_gnn_b1", j), True)
                load_rows(ROW_L1B)
                act.wait_ge(dve_to_act, S.due(dve_to_act))
                features_n()
                edge_weights()
            if "ffn1" in parts:
                norm(x, acc, None)
                act.dma_start(atom_b[:, :], t["atom_b"]).then_inc(sel_in, 16)
                act.dma_start(route[:, :], t["route"]).then_inc(sel_in, 16)
                act.wait_ge(dve_to_act, S.due(dve_to_act))
                act.activation(rt[:, 1, 12:30], rt[:, 0, 12:30], ACT.Sqrt).then_inc(act_to_dve, 1)
                act.wait_ge(dve_to_act, S.due(dve_to_act))
                act.activation(rt[:, 3, 0:6], rt[:, 2, 0:6], ACT.Exp).then_inc(act_to_dve, 1)
                for q in range(12):
                    act.wait_ge(tile_for["act"], S.due(tile_for["act"]))
                    b = col("L1_ffn_in_b", q)
                    if q < 2:
                        freed(act.activation(scr[:, q], ps[:, q], ACT.Gelu, bias=b), q)
                        mark(act_to_pe)
                    else:
                        freed(act.activation(scr[:, 2, q * 8 - 16:q * 8 - 8], ps[:, q % 6, 0:8], ACT.Gelu, bias=b), q % 6)
                mark(act_to_dve)

            def gcn():
                act.wait_ge(dve_to_act, S.due(dve_to_act))
                act.activation(row[:, :], row[:, :], ACT.Sqrt).then_inc(act_to_dve, 1)
                for m in range(NT):
                    high(e_hi[:, m], scr[:, m])
                act.wait_ge(dve_to_act, S.due(dve_to_act))
                features_n()

            if "gnn2" in parts or "mix2" in parts:
                norm(x, acc, A)
            if "gnn2" in parts:
                gcn()
            if "mix2" in parts:
                load_rows(ROW_KV2)
                linear_attention("attention2", "L2_mix_bq")
            if "ffn2" in parts:
                norm(x, acc, A)
                act.wait_ge(dve_to_act, S.due(dve_to_act))
                act.activation(gate_s[:, 2, :, 0:3], gate_s[:, 1, :, 0:3], ACT.Exp, scale=-1.0).then_inc(act_to_dve, 1)
                act.dma_start(sel[0:16, :], t["sel2"]).then_inc(sel_in, 16)
                experts("experts2", 8)
            if "gnn3" in parts or "mix3" in parts:
                norm(x, acc, A)
            if "gnn3" in parts:
                gcn()
            if "mix3" in parts:
                load_rows(ROW_KV3)
                norm(acc, scr, B, "L3_mix_ln1_b")
                linear_attention("attention3", "L3_mix_qkv_b")
                norm(acc, scr, B, "L3_mix_ln2_b")
                gelu_mlp("mlp3", "L3_mix_fc1_b", ACT.Gelu)
            if "ffn3" in parts:
                def nodes_high():
                    bn = B[0][:, :, :].rearrange("p k n -> p (k n)").rearrange("p (m d) -> p m d", m=NT)
                    for g in range(2):
                        for m in range(NT):
                            act.wait_ge(tile_for["act"], S.due(tile_for["act"]))
                            act.copy(bn[:, m, 384 * g:384 * g + 384], ps[:, (4 * g + m) % 6, 0:384])\
                               .then_inc(act_to_dve, 1)

                norm(x, acc, A)
                act.dma_start(tri[:, :], t["tri"]).then_inc(sel_in, 16)
                act.wait_ge(dve_to_act, S.due(dve_to_act))
                act.activation(gate_s[:, 2], gate_s[:, 1], ACT.Exp).then_inc(act_to_dve, 1)
                nodes_high()
                for j in range(KC):
                    act.wait_ge(tile_for["act"], S.due(tile_for["act"]))
                    freed(act.copy(acc[:, j], ps[:, j]), j)
                    mark(act_to_pe)
                for q in range(16):
                    act.wait_ge(tile_for["act"], S.due(tile_for["act"]))
                    c, c0 = slice(q % 8 * 64, q % 8 * 64 + 64), 64 * (q // 2)
                    freed(act.activation(hidden[:, q // 8, c], ps[:, q % 6, c0:c0 + 64], ACT.Gelu_apprx_tanh,
                                         bias=col("L3_ffn_b1", q)), q % 6)
                mark(act_to_pe)
                for n in range(3):
                    for f in range(KC):
                        act.wait_ge(tile_for["act"], S.due(tile_for["act"]))
                        for e in range(3 * n, min(3 * n + 3, 8)):
                            c = slice(e * 64, e * 64 + 64)
                            ins = act.activation(scr[:, f, c], ps[:, f, c], ACT.Gelu_apprx_tanh, bias=col("L3_ffn_b2", e * KC + f))
                        freed(ins, f)
                mark(act_to_pe)
                for m in range(NT):
                    act.wait_ge(tile_for["act"], S.due(tile_for["act"]))
                    act.copy(e_hi[:, m], ps[:, m]).then_inc(act_to_dve, 1)
                nodes_high()
            act.wait_ge(dve_to_act, S.due(dve_to_act))
            act.dma_start(out, x[:, :, :]).then_inc(stored, 16)
            act.wait_ge(stored, 16)

        @block.vector
        def _(dve):
            S = Side(dve, "dve", dve_own, LOOP_EVENTS)
            A_hi, A_lo = A
            eps_inv = 1.0 / D
            marks = [0]

            def freed(ins, b):
                ins.then_inc(bank_free["dve"][b], 1)
                dve.wait_ge(bank_free["dve"][b], S.due(bank_free["dve"][b]))

            def mark(sem):
                marks[0] = (marks[0] + 1) % 7
                dve.memset(junk[:, 8 + marks[0]:9 + marks[0]], 0.0).then_inc(sem, 1)

            def col(name, n=0):
                c = COL[name] + n
                return cols[:, c:c + 1] if isinstance(c, int) else cols[:, bass.ds(c, 1)]

            def low(X, j, v, beta=None):
                dve.wait_ge(act_to_dve, S.due(act_to_dve))
                if beta:
                    dve.scalar_tensor_tensor(out=X[1][:, j], in0=v, scalar=col(beta, j), in1=X[0][:, j], op0=ALU.add,
                                             op1=ALU.subtract).then_inc(dve_to_pe, 1)
                    return
                dve.tensor_tensor(X[1][:, j], v, X[0][:, j], ALU.subtract).then_inc(dve_to_pe, 1)

            def norm(src, dst, X, eps, gamma=None, beta=None):
                dve.wait_ge(tile_for["dve"], S.due(tile_for["dve"]))
                for j in range(KC):
                    dve.scalar_tensor_tensor(out=scr[:, j], in0=ps[:, 6], scalar=-eps_inv, in1=src[:, j], op0=ALU.mult,
                                             op1=ALU.add).then_inc(dve_to_act, 1)
                mark(bank_free["dve"][6])
                dve.wait_ge(bank_free["dve"][6], S.due(bank_free["dve"][6]))
                dve.wait_ge(tile_for["dve"], S.due(tile_for["dve"]))
                freed(dve.tensor_scalar(row[:, :], ps[:, 7], eps_inv, eps, ALU.mult, ALU.add), 7)
                mark(dve_to_act)
                dve.wait_ge(act_to_dve, S.due(act_to_dve))
                S.step(dve.reciprocal(row[:, :], row[:, :]))
                for j in range(KC):
                    if gamma:
                        y = dve.scalar_tensor_tensor(out=dst[:, j], in0=scr[:, j], scalar=col(gamma, j), in1=row[:, :],
                                                     op0=ALU.mult, op1=ALU.mult)
                    else:
                        y = dve.tensor_tensor(dst[:, j], scr[:, j], row[:, :], ALU.mult)
                    y.then_inc(dve_to_act if X else dve_to_pe, 1)
                    if X and j >= 1:
                        low(X, j - 1, dst[:, j - 1], beta)
                if X:
                    low(X, KC - 1, dst[:, KC - 1], beta)
                else:
                    S.step(dve.memset(junk[:, 14:15], 0.0))

            sn = scr[:, :, :].rearrange("p k n -> p (k n)").rearrange("p (m d) -> p m d", m=NT)
            accn = acc[:, :, :].rearrange("p k n -> p (k n)").rearrange("p (m d) -> p m d", m=NT)
            bn = [B[h][:, :, :].rearrange("p k n -> p (k n)").rearrange("p (m d) -> p m d", m=NT) for h in range(2)]
            flat = aux[:, :, :].rearrange("p a n -> p (a n)")

            def features_n():
                for g in range(2):
                    for m in range(NT):
                        c = slice(384 * g, 384 * g + 384)
                        dve.wait_ge(act_to_dve, S.due(act_to_dve))
                        ins = dve.tensor_tensor(bn[1][:, m, c], sn[:, m, c], bn[0][:, m, c], ALU.subtract)
                return ins

            def terms(src):
                dve.wait_ge(rows_in, S.due(rows_in, 16))
                spare = edge_w[0][:, :, :].rearrange("p m n -> p (m n)")[:, 0:D]
                for r in range(2):
                    for m in range(NT):
                        S.step(dve.tensor_tensor_reduce(spare, src[:, m], rows[:, r], 1.0, 0.0, ALU.mult, ALU.add,
                                                        nv[:, r, m:m + 1]))
                    if r == 0:
                        source_row()
                mark(rows_free)

            def diagonals(v, block):
                dve.tensor_tensor(aux[:, :, block * P:block * P + P], ident[:, :].unsqueeze(1).to_broadcast([P, NT, P]),
                                  v.unsqueeze(2).to_broadcast([P, NT, P]), ALU.mult).then_inc(dve_to_pe, 1)

            def source_row(u=0):
                diagonals(nv[:, 8 * u], 2 * u)

            def target_rows(u=0, spare=aux):
                src, tgt, most, src_02, total, top, row_1, row_02 = (nv[:, 8 * u + n] for n in range(8))
                dve.wait_ge(tile_for["dve"], S.due(tile_for["dve"]))
                dve.memset(junk[:, 15:16], 0.0)
                for m in range(NT):
                    ins = dve.tensor_tensor_reduce(spare[:, m], ps[:, 6 + u], no_edge[:, m], 1.0, -3e38, ALU.add, ALU.max,
                                                   most[:, m:m + 1])
                freed(ins, 6 + u)
                S.step(dve.tensor_tensor(total, tgt, most, ALU.add))
                S.step(dve.scalar_tensor_tensor(out=top, in0=total, scalar=0.2, in1=total, op0=ALU.mult, op1=ALU.max))
                dve.tensor_scalar(src_02, src, 0.2, None, ALU.mult)
                dve.tensor_tensor(row_1, tgt, top, ALU.subtract)
                S.step(dve.scalar_tensor_tensor(out=row_02, in0=tgt, scalar=0.2, in1=top, op0=ALU.mult, op1=ALU.subtract))
                for r, v in enumerate((row_1, row_02)):
                    diagonals(v, 2 * u + r)

            def edge_weights():
                def low_e(m):
                    dve.tensor_tensor(e_lo[:, m], scr[:, m], e_hi[:, m], ALU.subtract).then_inc(dve_to_pe, 1)

                for m in range(NT):
                    q = 2 * (m % 2)
                    dve.wait_ge(act_to_dve, S.due(act_to_dve))
                    S.step(dve.tensor_tensor(aux[:, q], aux[:, q], aux[:, q + 1], ALU.max))
                    dve.scalar_tensor_tensor(out=scr[:, m], in0=aux[:, q], scalar=1.0, in1=counts[:, m], op0=ALU.min,
                                             op1=ALU.mult).then_inc(dve_to_act, 1)
                    if 1 <= m < NT - 1:
                        dve.wait_ge(act_to_dve, S.due(act_to_dve))
                    if m >= 1:
                        low_e(m - 1)
                dve.wait_ge(act_to_dve, S.due(act_to_dve))
                low_e(NT - 1)

            def inverse_sums():
                dve.wait_ge(tile_for["dve"], S.due(tile_for["dve"]))
                freed(dve.tensor_scalar(row[:, :], ps[:, 6], 1e-16, None, ALU.add), 6)
                S.step(dve.reciprocal(row[:, :], row[:, :]))

            def head_output(from_psum=False):
                for s in range(KC + 2):
                    if s < KC and not from_psum:
                        dve.wait_ge(tile_for["dve"], S.due(tile_for["dve"]))
                        freed(dve.tensor_tensor(scr[:, s], ps[:, s], row[:, :], ALU.mult), s)
                        mark(dve_to_act)
                    if 1 <= s <= KC:
                        j = s - 1
                        q = 2 * (j % 2)
                        dve.wait_ge(act_to_dve, S.due(act_to_dve))
                        dve.scalar_tensor_tensor(out=scr[:, j], in0=aux[:, q], scalar=1.0, in1=aux[:, q + 1], op0=ALU.min,
                                                 op1=ALU.add).then_inc(dve_to_act, 1)
                    if s >= 2:
                        j = s - 2
                        dve.wait_ge(act_to_dve, S.due(act_to_dve))
                        dve.scalar_tensor_tensor(out=H[1][:, j], in0=scr[:, j], scalar=-1.0, in1=H[0][:, j], op0=ALU.add,
                                                 op1=ALU.subtract).then_inc(dve_to_pe, 1)

            def add_n(g, tiles=range(NT)):
                for m in tiles:
                    b = (4 * g + m) % 6
                    c = slice(384 * g, 384 * g + 384)
                    dve.wait_ge(tile_for["dve"], S.due(tile_for["dve"]))
                    freed(dve.tensor_tensor(accn[:, m, c], ps[:, b, 0:384], accn[:, m, c], ALU.add), b)

            def add_t(dst, bias=None):
                for j in range(KC):
                    dve.wait_ge(tile_for["dve"], S.due(tile_for["dve"]))
                    if bias:
                        ins = dve.scalar_tensor_tensor(out=dst[:, j], in0=ps[:, j], scalar=col(bias, j), in1=dst[:, j],
                                                       op0=ALU.add, op1=ALU.add)
                    else:
                        ins = dve.tensor_tensor(dst[:, j], ps[:, j], dst[:, j], ALU.add)
                    freed(ins, j)

            def gat_sum(bias):
                for j in range(KC):
                    dve.wait_ge(tile_for["dve"], S.due(tile_for["dve"]))
                    S.step(dve.tensor_tensor(scr[:, j], ps[:, j], row[:, :], ALU.mult))
                    freed(dve.scalar_tensor_tensor(out=x[:, j], in0=scr[:, j], scalar=col(bias, j), in1=x[:, j],
                                                   op0=ALU.add, op1=ALU.add), j)

            def performer(what):
                scale = HD ** -0.25
                vh = flat[:, 0:NT * 132].rearrange("p (m h c) -> p m h c", m=NT, h=2)
                S.step(dve.memset(orf[HD:P, :, :], -0.5))
                dve.wait_ge(rows_in, S.due(rows_in, 16))
                with S.loop(what, 3) as i:
                    for g in range(2):
                        for b, c in ((0, 0), (1, KC)):
                            dve.wait_ge(tile_for["dve"], S.due(tile_for["dve"]))
                            freed(dve.tensor_scalar(scr[:, b], ps[:, b], col("L0_mix_qkv_b", i * 2 + (g + c)), scale,
                                                    ALU.add, ALU.mult), b)
                        mark(dve_to_act)
                        dve.wait_ge(tile_for["dve"], S.due(tile_for["dve"]))
                        for m in range(NT):
                            ins = dve.tensor_tensor(vh[:, m, :, 0:HD],
                                                    ps[:, 2, m * P:m * P + P].rearrange("p (h c) -> p h c", h=2),
                                                    rows[:, 1, bass.ds(i * 256 + g * P, P)].rearrange("p (h c) -> p h c", h=2),
                                                    ALU.add)
                        freed(ins, 2)
                        dve.memset(vh[:, :, :, HD:HD + 2], 1.0).then_inc(dve_to_pe, 1)
                        for h in range(2):
                            dve.wait_ge(tile_for["dve"], S.due(tile_for["dve"]))
                            for r in range(3):
                                dve.tensor_copy(aux[:, 2, r * P:r * P + HD], ps[:, 7, r * 68:r * 68 + HD])
                                ins = dve.tensor_scalar(aux[:, 2, r * P + HD:r * P + P], ones[:, 0:HD],
                                                        ps[:, 7, r * 68 + HD:r * 68 + HD + 1], None, ALU.mult)
                            freed(ins, 7)
                            dve.wait_ge(tile_for["dve"], S.due(tile_for["dve"]))
                            S.step(dve.tensor_scalar(row[0:HD, :], ps[HD:P, h], 1e-8 * ORF, None, ALU.add))
                            S.step(dve.reciprocal(row[0:HD, :], row[0:HD, :]))
                            freed(dve.tensor_tensor(aux[h * HD:h * HD + HD, 3], ps[0:HD, h], row[0:HD, :], ALU.mult), h)
                        mark(dve_to_act)
                        dve.wait_ge(act_to_dve, S.due(act_to_dve))
                        f = bass.ds(2 * i + g, 1)
                        dve.tensor_tensor(H[1][:, f].rearrange("p o n -> p (o n)"), aux[:, 3],
                                          H[0][:, f].rearrange("p o n -> p (o n)"), ALU.subtract).then_inc(dve_to_pe, 1)
                mark(rows_free)

            def linear_attention(what, eps):
                S.step(dve.memset(kv[:, :, :], 0.0))
                S.step(dve.memset(same[:, :], 0.0))
                dve.memset(same[0:HD, 0:HD], 1.0)
                S.step(dve.memset(same[HD:P, HD:P], 1.0))
                S.step(dve.memset(v_n[:, :, :, P:P + 2], 1.0))
                dve.wait_ge(rows_in, S.due(rows_in, 16))
                with S.loop(what, 3) as i:
                    for g in range(2):
                        c = bass.ds(i * 256 + g * P, P)
                        for half in range(2):
                            b = 3 * g + 1 + half
                            dve.wait_ge(tile_for["dve"], S.due(tile_for["dve"]))
                            for m in range(2):
                                o = m * 256
                                dve.tensor_tensor(aux[:, half, m * P:m * P + P], ps[:, b, o:o + P], rows[:, 0, c], ALU.add)
                                ins = dve.tensor_tensor(v_n[:, g, 2 * half + m, 0:P], ps[:, b, o + P:o + 2 * P],
                                                        rows[:, 1, c], ALU.add)
                            freed(ins, b)
                            mark(dve_to_act)
                        for half in range(2):
                            dve.wait_ge(act_to_dve, S.due(act_to_dve))
                            dve.scalar_tensor_tensor(
                                out=k_n[:, g, 2 * half:2 * half + 2].rearrange("p m c -> p (m c)"),
                                in0=scr[:, 2 + half, 0:256], scalar=1.0, in1=scr[:, 2 + half, 256:512], op0=ALU.min,
                                op1=ALU.add)
                        dve.wait_ge(act_to_dve, S.due(act_to_dve))
                        dve.scalar_tensor_tensor(out=q_t[:, g], in0=scr[:, 0], scalar=1.0, in1=scr[:, 1], op0=ALU.min,
                                                 op1=ALU.add).then_inc(dve_to_pe, 1)
                    for g in range(2):
                        dve.wait_ge(tile_for["dve"], S.due(tile_for["dve"]))
                        dve.tensor_copy(kv[0:HD, g, 0:HD], ps[0:HD, 6 + g, 0:HD])
                        dve.tensor_copy(kv[HD:P, g, HD:P], ps[HD:P, 6 + g, HD:P])
                        freed(dve.tensor_scalar(k_sum[:, g], same[:, :], ps[:, 6 + g, P:P + 1], None, ALU.mult), 6 + g)
                    for g in range(2):
                        dve.wait_ge(tile_for["dve"], S.due(tile_for["dve"], 2))
                        freed(dve.tensor_scalar(row[:, :], ps[:, 3 * g + 1], eps, None, ALU.add), 3 * g + 1)
                        S.step(dve.reciprocal(row[:, :], row[:, :]))
                        freed(dve.tensor_tensor(aux[:, 2 + g], ps[:, 3 * g], row[:, :], ALU.mult), 3 * g)
                        mark(dve_to_act)
                    for g in range(2):
                        dve.wait_ge(act_to_dve, S.due(act_to_dve))
                        f = bass.ds(2 * i + g, 1)
                        dve.tensor_tensor(H[1][:, f].rearrange("p o n -> p (o n)"), aux[:, 2 + g],
                                          H[0][:, f].rearrange("p o n -> p (o n)"), ALU.subtract).then_inc(dve_to_pe, 1)
                mark(rows_free)

            def gelu_mlp(what, bias):
                for j in range(KC):
                    ins = dve.scalar_tensor_tensor(out=x[:, j], in0=acc[:, j], scalar=col(bias, j), in1=x[:, j],
                                                   op0=ALU.add, op1=ALU.add)
                S.step(ins)
                with S.loop(what, 4) as i:
                    for j in range(KC):
                        low(H, j, scr[:, j])
                    add_t(x)

            def experts(what, n, limit, per_chunk, periods):
                with S.loop(what, n) as i:
                    dve.tensor_copy(sel_now[:, :], sel[:, bass.ds(i * D, D)]).then_inc(dve_to_pe, 1) if per_chunk else \
                        dve.tensor_copy(sel_now[:, 0:P], sel[:, bass.ds(i * P, P)]).then_inc(dve_to_pe, 1)
                    if not per_chunk:
                        dve.wait_ge(tile_for["dve"], S.due(tile_for["dve"]))
                        freed(dve.tensor_copy(row[:, :], ps[:, 6]), 6)
                    for j in range(KC):
                        if per_chunk:
                            clamped(j, j, limit)
                        else:
                            dve.wait_ge(tile_for["dve"], S.due(tile_for["dve"]))
                            freed(dve.tensor_tensor(scr[:, j], scr[:, j], ps[:, j], ALU.mult), j)
                            dve.tensor_tensor(scr[:, j], scr[:, j], row[:, :], ALU.mult).then_inc(dve_to_act, 1)
                        if j >= 1:
                            low(H, j - 1, scr[:, j - 1])
                    low(H, KC - 1, scr[:, KC - 1])
                    add_t(x)

            def clamped(j, b, limit):
                dve.wait_ge(tile_for["dve"], S.due(tile_for["dve"], 2))
                freed(dve.scalar_tensor_tensor(out=scr[:, j], in0=scr[:, j], scalar=silu_limit, in1=ps[:, 6],
                                               op0=ALU.min, op1=ALU.mult), 6)
                freed(dve.tensor_scalar(aux[:, j % 4], ps[:, b], limit, -limit, ALU.min, ALU.max), b)
                dve.tensor_tensor(scr[:, j], scr[:, j], aux[:, j % 4], ALU.mult).then_inc(dve_to_act, 1)

            silu_limit = 10.0 / (1.0 + float(np.exp(-10.0)))

            def best(src, eq, mask):
                S.step(dve.tensor_reduce(nv[:, 8], src, AX_X, ALU.max))
                S.step(dve.tensor_tensor(eq, src, nv[:, 8, :].unsqueeze(2).to_broadcast(list(src.shape)), ALU.is_equal))
                S.step(dve.scalar_tensor_tensor(out=eq, in0=eq, scalar=-100.0, in1=gate_s[:, 11, :, 0:src.shape[2]],
                                                op0=ALU.mult, op1=ALU.add))
                S.step(dve.tensor_reduce(nv[:, 8], eq, AX_X, ALU.min))
                S.step(dve.tensor_tensor(mask, eq,
                                         nv[:, 8, :].unsqueeze(2).to_broadcast(list(src.shape)), ALU.is_equal))

            def numbers():
                for e in range(8):
                    dve.memset(gate_s[:, 11, :, e:e + 1], float(e))
                dve.memset(comb_n[:, :, 0:8], 0.0)
                dve.memset(comb_n[:, :, 9:16], 0.0)
                ins = dve.memset(comb_n[:, :, 8:9], 1.0)
                S.step(ins)

            def router_logits(n):
                dve.wait_ge(tile_for["dve"], S.due(tile_for["dve"]))
                freed(dve.tensor_copy(gate_s[:, 0, :, 0:n], ps[:, 6, 0:32].rearrange("p (m e) -> p m e", m=NT)[:, :, 0:n]), 6)

            def combine(n, score, rank):
                mask, two, tmp = gate_s[:, 7, :, 0:n], gate_s[:, 8, :, 0:n], gate_s[:, 9, :, 0:n]
                best(rank, tmp, two)
                S.step(dve.scalar_tensor_tensor(out=rank, in0=two, scalar=-3e38, in1=rank, op0=ALU.mult, op1=ALU.add))
                best(rank, tmp, mask)
                S.step(dve.tensor_tensor(two, two, mask, ALU.add))
                S.step(dve.tensor_tensor(two, two, score, ALU.mult))
                S.step(dve.tensor_reduce(nv[:, 9], two, AX_X, ALU.add))
                S.step(dve.tensor_scalar(nv[:, 9], nv[:, 9], 1e-6 if n == 8 else 0.0, None, ALU.max))
                S.step(dve.reciprocal(nv[:, 9], nv[:, 9]))
                dve.tensor_tensor(comb_n[:, :, 0:n], two, nv[:, 9, :].unsqueeze(2).to_broadcast([P, NT, n]), ALU.mult)\
                   .then_inc(dve_to_pe, 1)
                dve.wait_ge(tile_for["dve"], S.due(tile_for["dve"]))
                freed(dve.tensor_copy(comb_t[:, :], ps[0:16, 6]), 6)
                dve.wait_ge(sel_in, S.due(sel_in, 16))

            dve.wait_ge(edges_in, 32)
            dve.wait_ge(setup_done, n_setup)
            dve.tensor_copy(src_f[:, :], src_i[:, :])
            S.step(dve.tensor_copy(dst_f[:, :], dst_i[:, :]))
            with S.loop("edges", EC // 2) as i:
                for c in range(2):
                    dve.wait_ge(tile_for["dve"], S.due(tile_for["dve"]))
                    for r, f in enumerate((src_f, dst_f)):
                        ins = dve.tensor_scalar(hot[:, c, r], iota[:, :], f[:, bass.ds(i * 2 + c, 1)], None, ALU.is_equal)
                    ins.then_inc(dve_to_pe, 1)
            dve.wait_ge(tile_for["dve"], S.due(tile_for["dve"], 2))
            for m in range(NT):
                dve.tensor_copy(aux[:, m], ps[:, m]).then_inc(bank_free["dve"][m], 1)
                dve.wait_ge(bank_free["dve"][m], S.due(bank_free["dve"][m]))
                dve.tensor_copy(counts[:, m], aux[:, m]).then_inc(dve_to_pe, 1)
            for m in range(NT):
                dve.wait_ge(tile_for["dve"], S.due(tile_for["dve"]))
                freed(dve.tensor_scalar(no_edge[:, m], ps[:, 4 + m % 2], 0.0, NO_EDGE, ALU.is_equal, ALU.mult), 4 + m % 2)
            dve.wait_ge(loaded, 64)
            dve.wait_ge(act_to_dve, S.due(act_to_dve))
            S.step(dve.tensor_tensor(small_lo[:, :, :], small[:, :, :], small_hi[:, :, :], ALU.subtract))

            norm(x, acc, A, 1e-5)
            if "mix0" in parts:
                norm(acc, scr, B, 1e-5, "L0_mix_ln1_g", "L0_mix_ln1_b")
                performer("performer")
                add_t(acc, "L0_mix_proj_b")
                norm(acc, scr, B, 1e-5, "L0_mix_ln2_g", "L0_mix_ln2_b")
                gelu_mlp("mlp0", "L0_mix_fc2_b")
            if "gnn0" in parts:
                S.step(dve.memset(acc[:, :, :], 0.0))
                features_n()
                terms(sn)
                target_rows()
                edge_weights()
                inverse_sums()
                head_output()
                with S.loop("gat0", GAT - 1) as i:
                    mark(dve_to_act)
                    features_n()
                    terms(sn)
                    add_n(0, (0, 1))
                    target_rows()
                    add_n(0, (2, 3))
                    edge_weights()
                    add_n(1)
                    inverse_sums()
                    head_output()
                add_n(0)
                add_n(1)
                mark(dve_to_act)
                terms(accn)
                for m in range(NT):
                    dve.wait_ge(act_to_dve, S.due(act_to_dve))
                    dve.tensor_tensor(bn[1][:, m], accn[:, m], bn[0][:, m], ALU.subtract)
                target_rows()
                edge_weights()
                inverse_sums()
                gat_sum("L0_gnn_b2")
            if "ffn0" in parts:
                norm(x, acc, A, 1e-5)
                numbers()
                router_logits(8)
                S.step(dve.tensor_scalar(gate_s[:, 1], gate_s[:, 0], -1.0, None, ALU.mult))
                dve.tensor_tensor(gate_s[:, 1], gate_s[:, 1], gate_s[:, 0], ALU.max).then_inc(dve_to_act, 1)
                dve.wait_ge(act_to_dve, S.due(act_to_dve))
                dve.tensor_scalar(gate_s[:, 3], gate_s[:, 2], 1.0, None, ALU.add).then_inc(dve_to_act, 1)
                dve.wait_ge(act_to_dve, S.due(act_to_dve))
                dve.scalar_tensor_tensor(out=gate_s[:, 5], in0=gate_s[:, 0], scalar=0.0, in1=gate_s[:, 4], op0=ALU.max,
                                         op1=ALU.add).then_inc(dve_to_act, 1)
                dve.wait_ge(act_to_dve, S.due(act_to_dve))
                for m in range(NT):
                    ins = dve.tensor_tensor(gate_s[:, 10, m], gate_s[:, 6, m], vecs[:, V_GATE:V_GATE + 8], ALU.add)
                S.step(ins)
                combine(8, gate_s[:, 6], gate_s[:, 10])
                experts("experts0", 2, 10.0, True, 2)
                dve.tensor_copy(sel_now[:, 0:2 * P], sel[:, 2 * D:2 * D + 2 * P]).then_inc(dve_to_pe, 1)
                for j in range(2):
                    clamped(j, j, 10.0)
                for j in range(2):
                    low(H, j, scr[:, j])
                add_t(x)

            if "mix1" in parts or "gnn1" in parts:
                norm(x, acc, A, 1e-5)
            if "mix1" in parts:
                norm(acc, scr, B, 1e-5, "L1_mix_ln_gamma", "L1_mix_ln_beta")
                linear_attention("attention1", 1e-6)
                add_t(x, "L1_mix_b_proj")
            if "gnn1" in parts:
                mark(dve_to_act)
                for v in head_n:
                    dve.memset(v[:, :, :, C1:C2], 1.0)
                dve.wait_ge(rows_in, S.due(rows_in, 16))
                for g in range(2):
                    for m in range(NT):
                        dve.wait_ge(act_to_dve, S.due(act_to_dve))
                        c = slice(384 * g, 384 * g + 384)
                        for r in range(2):
                            S.step(dve.tensor_tensor(flat[:, 0:384].rearrange("p (h c) -> p h c", h=4),
                                                     head_n[m // 2][:, m % 2, 4 * g:4 * g + 4, 0:C1],
                                                     rows[:, r, c].rearrange("p (h c) -> p h c", h=4), ALU.mult))
                            S.step(dve.tensor_reduce(al[:, r, m, 4 * g:4 * g + 4],
                                                     flat[:, 0:384].rearrange("p (h c) -> p h c", h=4), AX_X, ALU.add))
                mark(rows_free)
                mark(dve_to_pe)
                with S.loop("gat1", GAT // 2) as i:
                    for u in range(2):
                        for r in range(2):
                            S.step(dve.tensor_copy(nv[:, 8 * u + r],
                                                   al[:, r, :, bass.ds(i * 2 + u, 1)].rearrange("p m o -> p (m o)")))
                        source_row(u)
                    for u in range(2):
                        target_rows(u, edge_w[u])
                    for u in range(2):
                        for m in range(NT + 1):
                            if m < NT:
                                dve.wait_ge(act_to_dve, S.due(act_to_dve))
                                dve.tensor_tensor(exp_1[u][:, m], exp_1[u][:, m], exp_02[u][:, m], ALU.max)\
                                   .then_inc(dve_own, 1)
                            if m >= 1:
                                dve.wait_ge(dve_own, S.due(dve_own))
                                dve.scalar_tensor_tensor(out=edge_w[u][:, m - 1], in0=exp_1[u][:, m - 1], scalar=1.0,
                                                         in1=counts[:, m - 1], op0=ALU.min, op1=ALU.mult)\
                                   .then_inc(dve_to_pe, 1)
                    for u in range(2):
                        inv = row[:, 4 * u:4 * u + 4]
                        o = ps[:, u, :].rearrange("p (m c) -> p m c", m=NT)
                        dve.wait_ge(tile_for["dve"], S.due(tile_for["dve"]))
                        S.step(dve.tensor_scalar(inv, o[:, :, C1], 1e-16, None, ALU.add))
                        S.step(dve.reciprocal(inv, inv))
                        for m in range(NT):
                            ins = dve.tensor_scalar(accn[:, m, bass.ds((i * 2 + u) * C1, C1)], o[:, m, 0:C1],
                                                    inv[:, m:m + 1], None, ALU.mult)
                        freed(ins, u)
                mark(dve_to_pe)
                head_output(True)
                mark(dve_to_act)
                features_n()
                terms(sn)
                target_rows()
                edge_weights()
                inverse_sums()
                gat_sum("L1_gnn_b2")
            if "ffn1" in parts:
                norm(x, acc, None, 1e-5)
                g3 = small[:, :, GP:GP + 12]
                for k in range(KC):
                    o = aux[:, k % 4, (k // 4) * 32:(k // 4) * 32 + 30]
                    xk = acc[:, k, 0:NCLS]
                    dve.tensor_tensor(o[:, 0:12].rearrange("p (n r) -> p n r", r=2), g3[:, k].rearrange("p (n r) -> p n r", r=2),
                                      xk.unsqueeze(2).to_broadcast([P, NCLS, 2]), ALU.mult)
                    dve.tensor_tensor(o[:, 12:24], g3[:, k], g3[:, k], ALU.mult)
                    ins = dve.tensor_tensor(o[:, 24:30], xk, xk, ALU.mult)
                ins.then_inc(dve_to_pe, 1)
                dve.wait_ge(tile_for["dve"], S.due(tile_for["dve"]))
                freed(dve.tensor_copy(rt[:, 0, 0:30], ps[:, 6, 0:30]), 6)
                mark(dve_to_act)
                dve.wait_ge(act_to_dve, S.due(act_to_dve))
                S.step(dve.tensor_scalar(rt[:, 1, 12:30], rt[:, 1, 12:30], 1e-12, None, ALU.max))
                S.step(dve.reciprocal(rt[:, 1, 12:30], rt[:, 1, 12:30]))
                S.step(dve.tensor_tensor(rt[:, 0, 0:12], rt[:, 0, 0:12], rt[:, 1, 12:24], ALU.mult))
                lg = rt[:, 0, 0:12].rearrange("p (n r) -> p n r", r=2)
                S.step(dve.tensor_tensor(lg, lg, rt[:, 1, 24:30].unsqueeze(2).to_broadcast([P, NCLS, 2]), ALU.mult))
                S.step(dve.tensor_tensor(rt[:, 0, 0:12], rt[:, 0, 0:12], vecs[:, V_BAL:V_BAL + 12], ALU.add))
                S.step(dve.tensor_tensor(rt[:, 4, 0:6], lg[:, :, 1], lg[:, :, 0], ALU.subtract))
                S.step(dve.tensor_scalar(rt[:, 2, 0:6], rt[:, 4, 0:6], -1.0, None, ALU.mult))
                dve.tensor_tensor(rt[:, 2, 0:6], rt[:, 2, 0:6], rt[:, 4, 0:6], ALU.min).then_inc(dve_to_act, 1)
                dve.wait_ge(act_to_dve, S.due(act_to_dve))
                S.step(dve.tensor_scalar(rt[:, 3, 0:6], rt[:, 3, 0:6], 1.0, None, ALU.add))
                S.step(dve.reciprocal(rt[:, 3, 0:6], rt[:, 3, 0:6]))
                w = rt[:, 5, 0:12].rearrange("p (n r) -> p n r", r=2)
                S.step(dve.tensor_scalar(rt[:, 4, 0:6], rt[:, 4, 0:6], 0.0, None, ALU.is_gt))
                S.step(dve.tensor_tensor(w[:, :, 1], rt[:, 4, 0:6], rt[:, 3, 0:6], ALU.mult))
                S.step(dve.tensor_tensor(w[:, :, 0], rt[:, 3, 0:6], w[:, :, 1], ALU.subtract))
                S.step(dve.memset(cls_w[:, :], 0.0))
                dve.wait_ge(sel_in, S.due(sel_in, 32))
                S.step(dve.tensor_tensor(route[:, :], route[:, :], rt[0:ATOMS, 5, 0:12], ALU.mult))
                S.step(dve.tensor_reduce(cls_w[:, 0:6], route[:, :].rearrange("p (n r) -> p n r", r=2), AX_X, ALU.add))
                S.step(dve.memset(scr[:, 3, 0:80], 0.0))
                dve.wait_ge(act_to_dve, S.due(act_to_dve))
                hid = scr[:, 2, 0:80].rearrange("p (a h n) -> p a h n", a=ATOMS, h=2)
                wei = scr[:, 3, 0:80].rearrange("p (a h n) -> p a h n", a=ATOMS, h=2)
                for n in range(NCLS):
                    for r in range(2):
                        of, to = PAIRS[n][r], PAIRS[n][1 - r]
                        ins = dve.tensor_scalar(wei[:, to, :, n:n + 1], hid[:, of, :, n:n + 1], w[:, n, r:r + 1], None, ALU.mult)
                ins.then_inc(dve_to_pe, 1)
                for j in range(KC):
                    dve.wait_ge(tile_for["dve"], S.due(tile_for["dve"]))
                    freed(dve.scalar_tensor_tensor(out=x[:, j, NCLS:N], in0=ps[:, j, NCLS:N], scalar=col("L1_ffn_fc2_b", j),
                                                   in1=x[:, j, NCLS:N], op0=ALU.add, op1=ALU.add), j)
                dve.wait_ge(tile_for["dve"], S.due(tile_for["dve"]))
                for r, o in enumerate((0, 48, 96)):
                    ins = dve.tensor_tensor(x[:, :, 0:NCLS], x[:, :, 0:NCLS],
                                            ps[:, 6, o:o + 48].rearrange("p (f n) -> p f n", n=8)[:, :, 0:NCLS], ALU.add)
                    if r < 2:
                        S.step(ins)
                freed(ins, 6)

            def gcn(bias):
                for m in range(NT):
                    S.step(dve.tensor_copy(aux[:, m], counts[:, m]))
                    c = slice(m * P, m * P + P)
                    S.step(dve.tensor_tensor(aux[:, m, c], aux[:, m, c], ident[:, :], ALU.add))
                mark(dve_to_pe)
                dve.wait_ge(tile_for["dve"], S.due(tile_for["dve"]))
                freed(dve.tensor_copy(row[:, :], ps[:, 6]), 6)
                mark(dve_to_act)
                dve.wait_ge(act_to_dve, S.due(act_to_dve))
                S.step(dve.reciprocal(row[:, :], row[:, :]))
                for m in range(NT):
                    S.step(dve.tensor_tensor_reduce(flat_junk, ident[:, :], row[:, m * P:m * P + P], 1.0, 0.0, ALU.mult,
                                                    ALU.add, nv[:, 14, m:m + 1]))
                for m in range(NT):
                    dve.scalar_tensor_tensor(out=scr[:, m], in0=aux[:, m], scalar=nv[:, 14, m:m + 1], in1=row[:, :],
                                             op0=ALU.mult, op1=ALU.mult).then_inc(dve_to_act, 1)
                for m in range(NT):
                    dve.wait_ge(act_to_dve, S.due(act_to_dve))
                    dve.tensor_tensor(e_lo[:, m], scr[:, m], e_hi[:, m], ALU.subtract)
                mark(dve_to_act)
                features_n()
                mark(dve_to_pe)
                add_t(x, bias)

            flat_junk = scr[:, 5, 0:P]
            if "gnn2" in parts or "mix2" in parts:
                norm(x, acc, A, 1e-5)
            if "gnn2" in parts:
                gcn("L2_gnn_b")
            if "mix2" in parts:
                linear_attention("attention2", 0.0)
                add_t(x, "L2_mix_bo")
            if "ffn2" in parts:
                norm(x, acc, A, 1e-5)
                numbers()
                router_logits(3)
                for m in range(NT):
                    ins = dve.tensor_tensor(gate_s[:, 1, m, 0:3], gate_s[:, 0, m, 0:3], vecs[:, V_ROUTE:V_ROUTE + 3], ALU.add)
                ins.then_inc(dve_to_act, 1)
                dve.wait_ge(act_to_dve, S.due(act_to_dve))
                S.step(dve.tensor_scalar(gate_s[:, 6, :, 0:3], gate_s[:, 2, :, 0:3], 1.0, None, ALU.add))
                S.step(dve.reciprocal(gate_s[:, 6, :, 0:3], gate_s[:, 6, :, 0:3]))
                S.step(dve.tensor_copy(gate_s[:, 10, :, 0:3], gate_s[:, 6, :, 0:3]))
                combine(3, gate_s[:, 6, :, 0:3], gate_s[:, 10, :, 0:3])
                experts("experts2", 8, 0.0, False, 8)
            if "gnn3" in parts or "mix3" in parts:
                norm(x, acc, A, 1e-5)
            if "gnn3" in parts:
                gcn("L3_gnn_b")
            if "mix3" in parts:
                norm(acc, scr, B, 1e-8, "L3_mix_ln1_w", "L3_mix_ln1_b")
                linear_attention("attention3", 0.0)
                add_t(acc, "L3_mix_proj_b")
                norm(acc, scr, B, 1e-8, "L3_mix_ln2_w", "L3_mix_ln2_b")
                gelu_mlp("mlp3", "L3_mix_fc2_b")
            if "ffn3" in parts:
                def nodes_low():
                    for g in range(2):
                        for m in range(NT):
                            c = slice(384 * g, 384 * g + 384)
                            b = (4 * g + m) % 6
                            dve.wait_ge(act_to_dve, S.due(act_to_dve))
                            freed(dve.tensor_tensor(bn[1][:, m, c], ps[:, b, 0:384], bn[0][:, m, c], ALU.subtract), b)

                norm(x, acc, A, 1e-5)
                numbers()
                router_logits(8)
                wide = [P, NT, 8]
                S.step(dve.tensor_reduce(nv[:, 11], gate_s[:, 0], AX_X, ALU.max))
                dve.tensor_tensor(gate_s[:, 1], gate_s[:, 0], nv[:, 11, :].unsqueeze(2).to_broadcast(wide), ALU.subtract)\
                   .then_inc(dve_to_act, 1)
                dve.wait_ge(act_to_dve, S.due(act_to_dve))
                S.step(dve.tensor_reduce(nv[:, 12], gate_s[:, 2], AX_X, ALU.add))
                S.step(dve.reciprocal(nv[:, 12], nv[:, 12]))
                best(gate_s[:, 0], gate_s[:, 9], gate_s[:, 7])
                dve.wait_ge(sel_in, S.due(sel_in, 16))
                mark(dve_to_pe)
                nodes_low()
                dve.wait_ge(tile_for["dve"], S.due(tile_for["dve"]))
                S.step(dve.tensor_scalar(gate_s[:, 8], ps[:, 6, 0:32].rearrange("p (m e) -> p m e", m=NT), 64.0, None, ALU.is_lt))
                S.step(dve.tensor_tensor(gate_s[:, 8], gate_s[:, 8], gate_s[:, 7], ALU.mult))
                freed(dve.scalar_tensor_tensor(out=gate_s[:, 9], in0=ps[:, 6, 0:32].rearrange("p (m e) -> p m e", m=NT),
                                               scalar=1.0, in1=gate_s[:, 8], op0=ALU.add, op1=ALU.mult), 6)
                S.step(dve.tensor_scalar(al[:, 0], gate_s[:, 9], -1.0, None, ALU.add))
                slots = [P, 8, 64]
                for m in range(NT):
                    S.step(dve.tensor_tensor(aux[:, m].rearrange("p (e c) -> p e c", e=8),
                                             tri[:, P:P + 64].unsqueeze(1).to_broadcast(slots),
                                             al[:, 0, m].unsqueeze(2).to_broadcast(slots), ALU.is_equal))
                for m in range(NT):
                    S.step(dve.tensor_copy(e_hi[:, m], aux[:, m]))
                    S.step(dve.tensor_scalar(aux[:, m], aux[:, m], nv[:, 12, m:m + 1], None, ALU.mult))
                mark(dve_to_pe)
                for m in range(NT):
                    dve.wait_ge(act_to_dve, S.due(act_to_dve))
                    freed(dve.tensor_tensor(e_lo[:, m], ps[:, m], e_hi[:, m], ALU.subtract), m)
                nodes_low()
                mark(dve_to_pe)
                add_t(x)
            mark(dve_to_act)


def stacked(inputs, *names):
    return [np.asarray(inputs[n]) for n in names]


def padded(a, n, axis):
    shape = list(a.shape)
    shape[axis] = n - a.shape[axis]
    return np.concatenate([a, np.zeros(shape, a.dtype)], axis)


def weight_stream(v, parts):
    out = []

    def cols_of(w):
        out.extend(w[:, 384 * g:384 * g + 384] for g in range(w.shape[1] // 384))

    def thirds(q, k, u):
        for f in range(KC):
            c = slice(f * P, f * P + P)
            out.append(np.concatenate([q[:, c], k[:, c], u[:, c]], 1))

    def kvq(w):
        thirds(w[:, D:2 * D], w[:, 2 * D:], w[:, 0:D])

    def mlp(w1, w2):
        for i in range(w1.shape[1] // D):
            cols_of(w1[:, i * D:i * D + D])
            cols_of(w2[i * D:i * D + D])

    def gated(g, u, d):
        for i in range(g.shape[1] // D):
            cols_of(g[:, i * D:i * D + D])
            cols_of(u[:, i * D:i * D + D])
            cols_of(d[i * D:i * D + D])

    if "mix0" in parts:
        w = v["L0_mix_qkv_w"]
        thirds(w[:, 0:D], w[:, D:2 * D], w[:, 2 * D:])
        cols_of(v["L0_mix_proj_w"])
        mlp(v["L0_mix_fc1_w"], v["L0_mix_fc2_w"])
    if "gnn0" in parts:
        w1, w2 = v["L0_gnn_W1"], v["L0_gnn_W2"]
        cols_of(w1[:, 0:D])
        for h in range(1, GAT):
            cols_of(w1[:, h * D:h * D + D])
            cols_of(w2[h * D - D:h * D])
        cols_of(w2[7 * D:])
    if "ffn0" in parts:
        def wide(w, s):
            return padded(np.concatenate(list(w) + [s], 1), n, 1)

        def packed(j):
            return np.concatenate([down[2 * D + c * P:2 * D + c * P + P, f * P:f * P + P] for f in range(3 * j, 3 * j + 3)
                                   for c in range(2)], 0)

        n = 2 * D + 2 * P
        gate, up = wide(v["L0_ffn_w1"], v["L0_ffn_w1s"]), wide(v["L0_ffn_w3"], v["L0_ffn_w3s"])
        down = padded(np.concatenate(list(v["L0_ffn_w2"]) + [v["L0_ffn_w2s"]], 0), n, 0)
        gated(gate[:, 0:2 * D], up[:, 0:2 * D], down[0:2 * D])
        out.append(np.concatenate([gate[:, 2 * D:n], up[:, 2 * D:2 * D + P]], 1))
        out.append(np.concatenate([up[:, 2 * D + P:n], packed(0), packed(1)], 1))
    if "mix1" in parts:
        kvq(v["L1_mix_w_qkv"].T)
        cols_of(v["L1_mix_w_proj"].T)
    if "gnn1" in parts:
        cols_of(v["L1_gnn_W1"])
        cols_of(v["L1_gnn_W2"])
    if "ffn1" in parts:
        ups = [v["L1_ffn_fc1_w"].T] + [w.T for w in v["L1_ffn_atom_in_w"]]
        cols_of(np.concatenate([padded(w, 256, 1) for w in ups], 1))
        downs = [v["L1_ffn_fc2_w"].T] + [w.T for w in v["L1_ffn_atom_out_w"]]
        down = np.concatenate([padded(w, 256, 0) for w in downs], 0)
        cols_of(down[0:D])
        cols_of(down[D:])
    if "gnn2" in parts:
        cols_of(v["L2_gnn_W"])
    if "mix2" in parts:
        thirds(v["L2_mix_Wk"], v["L2_mix_Wv"], v["L2_mix_Wq"])
        cols_of(v["L2_mix_Wo"])
    if "ffn2" in parts:
        gated(v["L2_ffn_shared_gate"], v["L2_ffn_shared_up"], v["L2_ffn_shared_down"])
        for e in range(3):
            gated(v["L2_ffn_routed_gate"][e], v["L2_ffn_routed_up"][e], v["L2_ffn_routed_down"][e])
    if "gnn3" in parts:
        cols_of(v["L3_gnn_W"])
    if "mix3" in parts:
        kvq(v["L3_mix_qkv_w"])
        cols_of(v["L3_mix_proj_w"])
        mlp(v["L3_mix_fc1_w"], v["L3_mix_fc2_w"])
    if "ffn3" in parts:
        up = np.concatenate([padded(w, 256, 1) for w in v["L3_ffn_w1"]], 1)
        cols_of(padded(up, 3 * D, 1))
        down = padded(np.concatenate([padded(w, 256, 0) for w in v["L3_ffn_w2"]], 0), 3 * D, 0)
        for i in range(3):
            cols_of(down[i * D:i * D + D])
    return np.concatenate([w.reshape(KC, P, 3, P).transpose(2, 1, 0, 3).reshape(3, P, D) for w in out])


def column_table(v):
    def in_columns(a):
        return a.reshape(-1, P).T

    special = {
        "L1_ffn_in_b": lambda: padded(np.concatenate([v["L1_ffn_fc1_b"][None], v["L1_ffn_atom_in_b"]], 0), 256, 1),
        "L3_ffn_b1": lambda: padded(v["L3_ffn_b1"], 256, 1),
        "zero": lambda: np.zeros(D, np.float32),
    }
    return np.concatenate([in_columns(np.ascontiguousarray(special[n]() if n in special else v[n])) for n, _ in COLUMNS], 1)


def selectors(width, expert_of):
    s = np.zeros((16, 3 * D), np.float32)
    for c in range(width):
        s[expert_of(c), c] = 1.0
    return s


def lay_out(v, parts):
    def t_layout(a):
        return a.reshape(KC, P, -1).transpose(1, 0, 2)

    small = np.zeros((D, NSMALL), np.float32)
    small[:, R0:R0 + 8] = v["L0_ffn_gate_w"]
    small[:, R2:R2 + 3] = v["L2_ffn_router_w"]
    small[:, R3:R3 + 8] = v["L3_ffn_router_w"]
    small[:, GP:GP + 12] = v["L1_ffn_gate_pair"].reshape(12, D).T
    rows = np.zeros((NROWS, 2, D), np.float32)
    rows[0:8, 0], rows[0:8, 1] = v["L0_gnn_a_src1"], v["L0_gnn_a_dst1"]
    rows[ROW_L0B, 0], rows[ROW_L0B, 1] = v["L0_gnn_a_src2"][0], v["L0_gnn_a_dst2"][0]
    rows[ROW_L1, 0], rows[ROW_L1, 1] = v["L1_gnn_a_src1"].reshape(D), v["L1_gnn_a_dst1"].reshape(D)
    rows[ROW_L1B, 0], rows[ROW_L1B, 1] = v["L1_gnn_a_src2"][0], v["L1_gnn_a_dst2"][0]
    rows[ROW_KV0] = v["L0_mix_qkv_b"].reshape(3, D)[1:]
    rows[ROW_KV2, 0], rows[ROW_KV2, 1] = v["L2_mix_bk"], v["L2_mix_bv"]
    rows[ROW_KV3] = v["L3_mix_qkv_b"].reshape(3, D)[1:]
    vecs = np.zeros(NVEC, np.float32)
    vecs[V_GATE:V_GATE + 8] = v["L0_ffn_gate_bias"]
    vecs[V_ROUTE:V_ROUTE + 3] = v["L2_ffn_routing_bias"]
    vecs[V_BAL:V_BAL + 12] = v["L1_ffn_balance_bias"].reshape(12)
    made = {
        "x": t_layout(v["x"].T),
        "src": v["src"].reshape(P, EC),
        "dst": v["dst"].reshape(P, EC),
        "stream": weight_stream(v, parts),
        "cols": column_table(v),
        "small": t_layout(small),
        "rows": rows,
        "vecs": vecs,
        "orf": v["L0_mix_w_orf"].reshape(3, 4, HD, ORF).transpose(0, 2, 1, 3).reshape(3, HD, 4 * ORF),
        "sel0": selectors(9 * FF, lambda c: c // FF),
        "sel2": selectors(8 * P, lambda c: 8 if c < 2 * P else c // (2 * P) - 1),
        "atom_b": v["L1_ffn_atom_out_b"],
        "tri": np.concatenate([np.triu(np.ones((P, P))), np.tile(np.arange(64), (P, 1))], 1).astype(np.float32),
        "route": np.array([[float(PAIRS[n][1 - r] == a) for n in range(NCLS) for r in range(2)] for a in range(ATOMS)],
                          np.float32),
    }
    return {k: np.ascontiguousarray(a) for k, a in made.items()}


def kernel(**inputs):
    import concourse.bacc as bacc
    from concourse.bass_utils import run_bass_kernel_spmd

    arrays = lay_out({k: np.asarray(a) for k, a in inputs.items()}, list(TURNS))
    nc = bacc.Bacc("TRN2", target_bir_lowering=False, num_devices=1)
    t = {k: nc.dram_tensor(k + "_dram", a.shape, mybir.dt.from_np(a.dtype), kind="ExternalInput").ap()
         for k, a in arrays.items()}
    out = nc.dram_tensor("out_dram", (P, KC, N), F32, kind="ExternalOutput").ap()
    build(nc, t, out, list(TURNS), LOOP_EVENTS)
    r = run_bass_kernel_spmd(nc, [{k + "_dram": a for k, a in arrays.items()}], core_ids=[0])
    return r.results[0]["out_dram"].transpose(1, 0, 2).reshape(D, N).T
```
